# Optimizing a Trainium2 kernel written in Bass

```python
import numpy as np
import jax
import jax.numpy as jnp

def _softmax(x, axis=-1):
    return jax.nn.softmax(x, axis=axis)

def _gelu(x):
    return jax.nn.gelu(x, approximate=True)

def _silu(x):
    return jax.nn.silu(x)

def _sigmoid(x):
    return jax.nn.sigmoid(x)

def _layernorm(x, axis=-1, eps=1e-05):
    m = jnp.mean(x, axis=axis, keepdims=True)
    v = jnp.var(x, axis=axis, keepdims=True)
    return (x - m) / jnp.sqrt(v + eps)

def _scatter_add(tgt, idx, src, axis=0):
    return tgt.at[idx].add(src)

def _segment_sum(src, seg, n):
    return jax.ops.segment_sum(src, seg, n)
kernel_name = 'mk_prb_d2_jaxref_r8_2dc23b'

def setup_inputs(seed: int=0):
    np.random.seed(seed)
    _w = jnp.asarray

    def _L0_attn_setup():
        import jax, jax.numpy as jnp
        import numpy as np
        EMBED_DIM = 128
        NUM_HEADS = 16
        HEAD_DIM = EMBED_DIM // NUM_HEADS
        B, T = (2, 256)
        key = jax.random.key(seed)
        ks = jax.random.split(key, 7)
        s = 0.02
        return {'x': jax.random.normal(ks[0], (B, T, EMBED_DIM), dtype=jnp.float32), 'Wq': jax.random.normal(ks[1], (EMBED_DIM, EMBED_DIM), dtype=jnp.float32) * s, 'bq': jax.random.normal(ks[2], (EMBED_DIM,), dtype=jnp.float32) * s, 'Wkv': jax.random.normal(ks[3], (2 * HEAD_DIM, EMBED_DIM), dtype=jnp.float32) * s, 'bkv': jax.random.normal(ks[4], (2 * HEAD_DIM,), dtype=jnp.float32) * s, 'Wo': jax.random.normal(ks[5], (EMBED_DIM, EMBED_DIM), dtype=jnp.float32) * s, 'bo': jax.random.normal(ks[6], (EMBED_DIM,), dtype=jnp.float32) * s}
    _L0_attn_in = _L0_attn_setup()

    def _L0_ffn_setup():
        import jax, jax.numpy as jnp
        import numpy as np
        B, S, D = (2, 256, 128)
        H, E, P, K = (8, 8, 128, 2)
        SCALE = 1.0 / np.sqrt(P)

        def _get_sel_gate(x, w, route_scale):
            logits = jnp.einsum('bsd,ed->bse', x, w).astype(jnp.float32)
            raw = logits.reshape(x.shape[0], x.shape[1], H, E)
            probs = jax.nn.sigmoid(raw)
            vals, idx = jax.lax.top_k(probs, K)
            vals = vals / jnp.clip(vals.sum(-1, keepdims=True), 1e-09)
            vals = vals * route_scale
            gate = (jax.nn.one_hot(idx, E, dtype=vals.dtype) * vals[..., None]).sum(-2)
            return gate
        key = jax.random.key(seed)
        ks = jax.random.split(key, 8)
        std = 1.0 / np.sqrt(D)
        return {'x': jax.random.normal(ks[0], (B, S, D), jnp.float32), 'q_w': jax.random.normal(ks[1], (H * P, D), jnp.float32) * std, 'k_w': jax.random.normal(ks[2], (H * P, D), jnp.float32) * std, 'v_w': jax.random.normal(ks[3], (H * E, D, P), jnp.float32) * std, 'o_w': jax.random.normal(ks[4], (H * E, P, D), jnp.float32) * (1.0 / np.sqrt(H * P)), 'sel_v_w': jax.random.normal(ks[5], (H * E, D), jnp.float32) * std, 'sel_o_w': jax.random.normal(ks[6], (H * E, D), jnp.float32) * std, 'route_scale': jnp.ones((1,), jnp.float32)}
    _L0_ffn_in = _L0_ffn_setup()

    def _L1_attn_setup():
        import jax, jax.numpy as jnp
        import numpy as np
        EPS_FEAT = 0.0001
        EPS_DEN = 0.01

        def _favorp(data, proj, is_query):
            d = data.shape[-1]
            data_normalizer = d ** (-0.25)
            ratio = proj.shape[-2] ** (-0.5)
            data_dash = jnp.einsum('bhnd,hjd->bhnj', data_normalizer * data, proj)
            diag = jnp.sum(data * data, axis=-1, keepdims=True) * (0.5 * data_normalizer * data_normalizer)
            if is_query:
                stab = jax.lax.stop_gradient(jnp.max(data_dash, axis=-1, keepdims=True))
            else:
                stab = jax.lax.stop_gradient(jnp.max(data_dash, axis=(-1, -2), keepdims=True))
            return ratio * jnp.exp(data_dash - diag - stab) + EPS_FEAT
        key = jax.random.key(seed)
        ks = jax.random.split(key, 6)
        B, N, D, H, J = (4, 512, 128, 16, 64)
        dh = D // H
        s = 0.02
        return {'query': jax.random.normal(ks[0], (B, N, D), dtype=jnp.float32), 'Wq': jax.random.normal(ks[1], (D, D), dtype=jnp.float32) * s, 'bq': jnp.zeros((D,), dtype=jnp.float32), 'Wk': jax.random.normal(ks[2], (D, D), dtype=jnp.float32) * s, 'bk': jnp.zeros((D,), dtype=jnp.float32), 'Wv': jax.random.normal(ks[3], (D, D), dtype=jnp.float32) * s, 'bv': jnp.zeros((D,), dtype=jnp.float32), 'Wo': jax.random.normal(ks[4], (D, D), dtype=jnp.float32) * s, 'bo': jnp.zeros((D,), dtype=jnp.float32), 'proj': jax.random.normal(ks[5], (H, J, dh), dtype=jnp.float32)}
    _L1_attn_in = _L1_attn_setup()

    def _L1_ffn_setup():
        import jax, jax.numpy as jnp
        import numpy as np
        B, S, DIM = (4, 256, 128)
        E, K, HID = (8, 2, 512)
        key = jax.random.key(seed)
        ks = jax.random.split(key, 8)
        init = lambda k, sh: jax.random.normal(k, sh, jnp.float32) * 0.02
        return {'x': jax.random.normal(ks[0], (B, S, DIM), jnp.float32), 'gate_w': init(ks[1], (DIM, E)), 'gate_b': jnp.zeros((E,), jnp.float32), 'w1': init(ks[2], (E, DIM, HID)), 'b1': jnp.zeros((E, HID), jnp.float32), 'w2': init(ks[3], (E, HID, DIM)), 'b2': jnp.zeros((E, DIM), jnp.float32), 'ws1': init(ks[4], (DIM, HID)), 'bs1': jnp.zeros((HID,), jnp.float32), 'ws2': init(ks[5], (HID, DIM)), 'bs2': jnp.zeros((DIM,), jnp.float32)}
    _L1_ffn_in = _L1_ffn_setup()
    _d = {'L0_attn_x': _L0_attn_in['x'], 'L0_attn_Wq': _L0_attn_in['Wq'], 'L0_attn_bq': _L0_attn_in['bq'], 'L0_attn_Wkv': _L0_attn_in['Wkv'], 'L0_attn_bkv': _L0_attn_in['bkv'], 'L0_attn_Wo': _L0_attn_in['Wo'], 'L0_attn_bo': _L0_attn_in['bo'], 'L0_ffn_q_w': _L0_ffn_in['q_w'], 'L0_ffn_k_w': _L0_ffn_in['k_w'], 'L0_ffn_v_w': _L0_ffn_in['v_w'], 'L0_ffn_o_w': _L0_ffn_in['o_w'], 'L0_ffn_sel_v_w': _L0_ffn_in['sel_v_w'], 'L0_ffn_sel_o_w': _L0_ffn_in['sel_o_w'], 'L0_ffn_route_scale': _L0_ffn_in['route_scale'], 'L1_attn_Wq': _L1_attn_in['Wq'], 'L1_attn_bq': _L1_attn_in['bq'], 'L1_attn_Wk': _L1_attn_in['Wk'], 'L1_attn_bk': _L1_attn_in['bk'], 'L1_attn_Wv': _L1_attn_in['Wv'], 'L1_attn_bv': _L1_attn_in['bv'], 'L1_attn_Wo': _L1_attn_in['Wo'], 'L1_attn_bo': _L1_attn_in['bo'], 'L1_attn_proj': _L1_attn_in['proj'], 'L1_ffn_gate_w': _L1_ffn_in['gate_w'], 'L1_ffn_gate_b': _L1_ffn_in['gate_b'], 'L1_ffn_w1': _L1_ffn_in['w1'], 'L1_ffn_b1': _L1_ffn_in['b1'], 'L1_ffn_w2': _L1_ffn_in['w2'], 'L1_ffn_b2': _L1_ffn_in['b2'], 'L1_ffn_ws1': _L1_ffn_in['ws1'], 'L1_ffn_bs1': _L1_ffn_in['bs1'], 'L1_ffn_ws2': _L1_ffn_in['ws2'], 'L1_ffn_bs2': _L1_ffn_in['bs2']}
    _x0 = _d['L0_attn_x']
    _d['L0_attn_x'] = jax.random.normal(jax.random.fold_in(jax.random.key(seed), 1), (4, 1024, 128), dtype=_x0.dtype)
    del _x0
    return _d

def reference(L0_attn_x, L0_attn_Wq, L0_attn_bq, L0_attn_Wkv, L0_attn_bkv, L0_attn_Wo, L0_attn_bo, L0_ffn_q_w, L0_ffn_k_w, L0_ffn_v_w, L0_ffn_o_w, L0_ffn_sel_v_w, L0_ffn_sel_o_w, L0_ffn_route_scale, L1_attn_Wq, L1_attn_bq, L1_attn_Wk, L1_attn_bk, L1_attn_Wv, L1_attn_bv, L1_attn_Wo, L1_attn_bo, L1_attn_proj, L1_ffn_gate_w, L1_ffn_gate_b, L1_ffn_w1, L1_ffn_b1, L1_ffn_w2, L1_ffn_b2, L1_ffn_ws1, L1_ffn_bs1, L1_ffn_ws2, L1_ffn_bs2):

    def _L0_attn_ref(x, Wq, bq, Wkv, bkv, Wo, bo):
        import jax, jax.numpy as jnp
        import numpy as np
        EMBED_DIM = 128
        NUM_HEADS = 16
        HEAD_DIM = EMBED_DIM // NUM_HEADS
        B, T = (2, 256)
        bsz, tgt_len, _ = x.shape
        scaling = HEAD_DIM ** (-0.5)
        q = (jnp.einsum('bte,oe->bto', x, Wq) + bq) * scaling
        kv = jnp.einsum('bte,oe->bto', x, Wkv) + bkv
        k, v = (kv[..., :HEAD_DIM], kv[..., HEAD_DIM:])
        qr = q.reshape(bsz, NUM_HEADS * tgt_len, HEAD_DIM)
        attn_weights = jnp.einsum('brd,bsd->brs', qr, k)
        attn_probs = jax.nn.softmax(attn_weights, axis=-1)
        attn_output = jnp.einsum('brs,bsd->brd', attn_probs, v)
        attn_output = attn_output.reshape(bsz, NUM_HEADS, tgt_len, HEAD_DIM)
        attn_output = attn_output.transpose(0, 2, 1, 3).reshape(bsz, tgt_len, EMBED_DIM)
        out = jnp.einsum('bte,oe->bto', attn_output, Wo) + bo
        return out

    def _L0_ffn_ref(x, q_w, k_w, v_w, o_w, sel_v_w, sel_o_w, route_scale):
        import jax, jax.numpy as jnp
        import numpy as np
        B, S, D = (2, 256, 128)
        H, E, P, K = (8, 8, 128, 2)
        SCALE = 1.0 / np.sqrt(P)

        def _get_sel_gate(x, w, route_scale):
            logits = jnp.einsum('bsd,ed->bse', x, w).astype(jnp.float32)
            raw = logits.reshape(x.shape[0], x.shape[1], H, E)
            probs = jax.nn.sigmoid(raw)
            vals, idx = jax.lax.top_k(probs, K)
            vals = vals / jnp.clip(vals.sum(-1, keepdims=True), 1e-09)
            vals = vals * route_scale
            gate = (jax.nn.one_hot(idx, E, dtype=vals.dtype) * vals[..., None]).sum(-2)
            return gate
        rs = route_scale[0]
        gate_v = _get_sel_gate(x, sel_v_w, rs)
        gate_o = _get_sel_gate(x, sel_o_w, rs)
        q = jnp.einsum('bsd,hpd->bhsp', x, q_w.reshape(H, P, D))
        k = jnp.einsum('bsd,hpd->bhsp', x, k_w.reshape(H, P, D))
        xv = jnp.einsum('bsd,hedp->bshep', x, v_w.reshape(H, E, D, P))
        v = jnp.einsum('bshep,bshe->bhsp', xv, gate_v)
        att = jax.nn.softmax(jnp.einsum('bhqp,bhkp->bhqk', q, k) * SCALE, axis=-1)
        ctx = jnp.einsum('bhqk,bhkp->bqhp', att, v)
        weighted = ctx[:, :, :, None, :] * gate_o[..., None]
        out = jnp.einsum('bshep,hepd->bsd', weighted, o_w.reshape(H, E, P, D))
        return out

    def _L1_attn_ref(query, Wq, bq, Wk, bk, Wv, bv, Wo, bo, proj):
        import jax, jax.numpy as jnp
        import numpy as np
        EPS_FEAT = 0.0001
        EPS_DEN = 0.01

        def _favorp(data, proj, is_query):
            d = data.shape[-1]
            data_normalizer = d ** (-0.25)
            ratio = proj.shape[-2] ** (-0.5)
            data_dash = jnp.einsum('bhnd,hjd->bhnj', data_normalizer * data, proj)
            diag = jnp.sum(data * data, axis=-1, keepdims=True) * (0.5 * data_normalizer * data_normalizer)
            if is_query:
                stab = jax.lax.stop_gradient(jnp.max(data_dash, axis=-1, keepdims=True))
            else:
                stab = jax.lax.stop_gradient(jnp.max(data_dash, axis=(-1, -2), keepdims=True))
            return ratio * jnp.exp(data_dash - diag - stab) + EPS_FEAT
        B, N, D = query.shape
        H = proj.shape[0]
        dh = D // H

        def split_heads(x):
            return x.reshape(B, N, H, dh).transpose(0, 2, 1, 3)
        q = split_heads(query @ Wq.T + bq)
        k = split_heads(query @ Wk.T + bk)
        v = split_heads(query @ Wv.T + bv)
        q_prime = _favorp(q, proj, is_query=True)
        k_prime = _favorp(k, proj, is_query=False)
        kv = jnp.einsum('bhnj,bhnd->bhjd', k_prime, v)
        qkv = jnp.einsum('bhnj,bhjd->bhnd', q_prime, kv)
        normalizer = jnp.einsum('bhnj,bhj->bhn', q_prime, k_prime.sum(axis=2))
        out = qkv / jnp.clip(normalizer, EPS_DEN, None)[..., None]
        out = out.transpose(0, 2, 1, 3).reshape(B, N, D)
        return out @ Wo.T + bo

    def _L1_ffn_ref(x, gate_w, gate_b, w1, b1, w2, b2, ws1, bs1, ws2, bs2):
        import jax, jax.numpy as jnp
        import numpy as np
        B, S, DIM = (4, 256, 128)
        E, K, HID = (8, 2, 512)
        orig_shape = x.shape
        xf = x.reshape(-1, DIM)
        logits = xf @ gate_w + gate_b
        top_w, top_i = jax.lax.top_k(logits, K)
        gw = jax.nn.softmax(top_w, axis=-1).astype(xf.dtype)
        combine = (gw[:, :, None] * jax.nn.one_hot(top_i, E, dtype=xf.dtype)).sum(axis=1)
        out = jnp.zeros_like(xf)
        for e in range(E):
            h = jax.nn.gelu(xf @ w1[e] + b1[e], approximate=False)
            out = out + combine[:, e:e + 1] * (h @ w2[e] + b2[e])
        shared = jax.nn.gelu(xf @ ws1 + bs1, approximate=False) @ ws2 + bs2
        return (out + shared).reshape(orig_shape)
    x = L0_attn_x
    xn = _layernorm(x, axis=-1)
    x = x + _L0_attn_ref(xn, L0_attn_Wq, L0_attn_bq, L0_attn_Wkv, L0_attn_bkv, L0_attn_Wo, L0_attn_bo) + _L0_ffn_ref(xn, L0_ffn_q_w, L0_ffn_k_w, L0_ffn_v_w, L0_ffn_o_w, L0_ffn_sel_v_w, L0_ffn_sel_o_w, L0_ffn_route_scale)
    xn = _layernorm(x, axis=-1)
    x = x + _L1_attn_ref(xn, L1_attn_Wq, L1_attn_bq, L1_attn_Wk, L1_attn_bk, L1_attn_Wv, L1_attn_bv, L1_attn_Wo, L1_attn_bo, L1_attn_proj) + _L1_ffn_ref(xn, L1_ffn_gate_w, L1_ffn_gate_b, L1_ffn_w1, L1_ffn_b1, L1_ffn_w2, L1_ffn_b2, L1_ffn_ws1, L1_ffn_bs1, L1_ffn_ws2, L1_ffn_bs2)
    return x

_drawn_inputs = setup_inputs


def setup_inputs(seed=0):
    import zlib

    import numpy as np

    out = dict(_drawn_inputs(seed))
    spreads = {'L1_attn_bq': (0.0, 2.0),
     'L1_attn_bk': (0.0, 2.0),
     'L1_attn_bv': (0.0, 2.0),
     'L1_attn_bo': (0.0, 0.1),
     'L1_ffn_gate_b': (0.0, 0.1),
     'L1_ffn_b1': (0.0, 0.468),
     'L1_ffn_b2': (0.0, 0.1),
     'L1_ffn_bs1': (0.0, 0.37),
     'L1_ffn_bs2': (0.0, 0.1)}
    factors = {'L0_attn_Wq': 8.0,
     'L0_attn_bq': 8.0,
     'L0_attn_Wkv': 8.0,
     'L0_attn_bkv': 8.0,
     'L0_attn_Wo': 8.0,
     'L1_attn_Wq': 200.0,
     'L1_attn_Wk': 64.0,
     'L1_attn_Wv': 64.0,
     'L1_attn_proj': 64.0,
     'L0_attn_bo': 3.732,
     'L0_ffn_q_w': 2.885,
     'L0_ffn_k_w': 2.837,
     'L1_attn_Wo': 5.115}
    for name, (base, spread) in spreads.items():
        noise = np.random.default_rng([zlib.crc32(name.encode()), seed]).standard_normal(out[name].shape)
        drawn = base * np.exp(spread * noise) if base else spread * noise
        out[name] = jnp.asarray(drawn.astype(out[name].dtype))
    for name, factor in factors.items():
        out[name] = (out[name] * factor).astype(out[name].dtype)
    return out
```

```python
from contextlib import ExitStack

import numpy as np

import concourse.bass as bass
from concourse import mybir

ALU = mybir.AluOpType
ACT = mybir.ActivationFunctionType
AX = mybir.AxisListType
F32 = mybir.dt.float32
BF16 = mybir.dt.bfloat16

P = 128
B, T, D = 4, 1024, 128
NT = B * T // P
TPB = T // P
H0, HD = 16, 8
SPLIT = 6
HS, ES, PS = 8, 8, 128
SW_SCALE = PS ** -0.5
HF, JF = 16, 64
FT = HF * JF // P
DN = float(HD) ** -0.25
RATIO = float(JF) ** -0.5
EPS_FEAT, EPS_DEN, LN_EPS = 1e-4, 1e-2, 1e-5
EM, HID = 8, 512
HT = HID // P


class Slot:

    def __init__(self, ctx, nc, name, buf=None, step=1):
        self.name, self.buf, self.step = name, buf, step
        self.full = ctx.enter_context(nc.semaphore(f"full_{name}"))
        self.free = ctx.enter_context(nc.semaphore(f"free_{name}"))
        self.start, self.uses = {}, {}


class Use:

    def __init__(self, slot=None, nth=None):
        self.slot, self.nth = slot, nth

    @property
    def buf(self):
        return self.slot.buf

    @property
    def full(self):
        return self.slot.full

    @property
    def free(self):
        return self.slot.free


class Part:

    def __init__(self, name, rounds=1, base=0):
        self.name, self.rounds, self.base, self.steps, self.count = name, rounds, base, [], {}

    def use(self, slot):
        n = self.count.get(slot, 0)
        self.count[slot] = n + 1
        return Use(slot, n)

    def ring(self):
        return Use()

    def chain(self, slot, n):
        return [self.use(slot) for _ in range(n)]

    def step(self, engine, tick, what, rings=()):
        self.steps.append((tick, len(self.steps), engine, what, rings))

    def settle(self, ring_slots):
        self.steps.sort(key=lambda s: (s[0], s[1]))
        n = 0
        for _, _, engine, _, rings in self.steps:
            for u in rings:
                got = self.use(ring_slots[n % len(ring_slots)])
                u.slot, u.nth = got.slot, got.nth
                n += 1


class Run:

    def __init__(self, eng, part, starts, i):
        self.eng, self.part, self.starts, self.i = eng, part, starts, i

    def nth(self, u):
        per = self.part.count[u.slot]
        return self.i * per + (self.starts.get(u.slot, 0) + u.nth)

    def claim(self, u):
        self.eng.wait_ge(u.free, self.nth(u) + 1)

    def ready(self, u):
        self.eng.wait_ge(u.full, (self.nth(u) + 1) * u.slot.step)

    def ready_apart(self, u, tally):
        self.ready(u)
        self.eng.sem_inc(tally.full, 1)

    def all_freed(self, slot):
        self.eng.wait_ge(slot.free, self.starts[slot] + 1)


class Links:

    def __init__(self, run, uses):
        self.run, self.uses, self.at = run, uses, 0

    def __call__(self, ins):
        u = self.uses[self.at]
        self.at += 1
        ins.then_inc(u.full, 1)
        self.run.ready(u)


def run_block(nc, parts, slots, ring_slots=()):
    starts, total = {}, {}
    for part in parts:
        part.settle(ring_slots)
        starts[part] = dict(total)
        for s, n in part.count.items():
            total[s] = total.get(s, 0) + n * part.rounds
    with nc.Block() as block:
        def program(name):
            def emit(eng):
                if name == "sync":
                    for s in slots:
                        eng.sem_inc(s.free, 1)
                for part in parts:
                    mine = [s for s in part.steps if s[2] == name]
                    if not mine:
                        continue
                    if part.rounds == 1:
                        r = Run(eng, part, starts[part], 0)
                        for s in mine:
                            s[3](r)
                    else:
                        with eng.Fori(0, part.rounds) as i:
                            r = Run(eng, part, starts[part], i)
                            for s in mine:
                                s[3](r)
            return emit

        block.sync(program("sync"))
        block.gpsimd(program("gpsimd"))
        block.scalar(program("scalar"))
        block.tensor(program("tensor"))
        block.vector(program("vector"))
    with nc.Block() as block:
        @block.gpsimd
        def _(eng):
            for s in slots:
                eng.sem_clear(s.full)
                eng.sem_clear(s.free)


def spread(ap, n):
    return ap.unsqueeze(len(ap.shape)).to_broadcast([*ap.shape, n])


class Block:

    def __init__(self, nc, ctx, name):
        self.nc, self.ctx, self.name, self.slots, self.parts, self.rings = nc, ctx, name, [], [], []

    def sbuf(self, name, shape, dt=F32):
        return self.ctx.enter_context(self.nc.sbuf_tensor(f"{self.name}_{name}", shape, dt))

    def psum(self, name, shape):
        return self.ctx.enter_context(self.nc.psum_tensor(f"{self.name}_{name}", shape, F32))

    def slot(self, name, shape=None, dt=F32, step=1):
        buf = self.sbuf(name, shape, dt) if shape else None
        return self.keep(Slot(self.ctx, self.nc, f"{self.name}_{name}", buf, step))

    def bank(self, name, shape):
        return self.keep(Slot(self.ctx, self.nc, f"{self.name}_{name}", self.psum(name, shape)))

    def keep(self, slot):
        self.slots.append(slot)
        return slot

    def ring(self, n, shape):
        self.rings = [self.bank(f"ring{k}", shape) for k in range(n)]

    def part(self, name, rounds=1, base=0):
        self.parts.append(Part(name, rounds, base))
        return self.parts[-1]

    def run(self):
        run_block(self.nc, self.parts, self.slots, self.rings)



def layer_norm_stats(blk, part, tick, x, st, loaded):
    chain = blk.slot("ln_chain")
    links = part.chain(chain, 7)
    sq, root, done = (part.use(blk.slot(f"ln_{k}")) for k in ("var", "root", "done"))
    bn, mean, rs, va, t1, y = (st[k] for k in ("bn", "mean", "rstd", "va", "t1", "y"))

    def moments(r):
        v, link = r.eng, Links(r, links)
        if loaded is not None:
            r.ready(loaded)
        for t in range(NT):
            last = v.bn_stats(bn[:, t, :], x[:, t, :])
        link(last)
        v.tensor_tensor(t1[:, :], bn[:, :, 1], bn[:, :, 4], ALU.subtract)
        v.tensor_tensor(va[:, :], bn[:, :, 2], bn[:, :, 5], ALU.add)
        link(v.tensor_tensor(mean[:, :], bn[:, :, 1], bn[:, :, 4], ALU.add))
        v.tensor_scalar(mean[:, :], mean[:, :], 0.5, None, ALU.mult)
        v.tensor_scalar(va[:, :], va[:, :], 1.0 / D, LN_EPS, ALU.mult, ALU.add)
        link(v.scalar_tensor_tensor(out=t1[:, :], in0=t1[:, :], scalar=0.25, in1=t1[:, :],
                                    op0=ALU.mult, op1=ALU.mult))
        v.tensor_tensor(va[:, :], va[:, :], t1[:, :], ALU.add).then_inc(sq.full, 1)

    def root_table(r):
        r.ready(sq)
        r.eng.activation(rs[:, :], va[:, :], ACT.Sqrt).then_inc(root.full, 1)

    def newton(r):
        v, link = r.eng, Links(r, links[3:])
        r.ready(root)
        link(v.reciprocal(y[:, :], rs[:, :]))
        link(v.tensor_tensor(t1[:, :], y[:, :], y[:, :], ALU.mult))
        link(v.scalar_tensor_tensor(out=t1[:, :], in0=t1[:, :], scalar=-0.5, in1=va[:, :],
                                    op0=ALU.mult, op1=ALU.mult))
        v.scalar_tensor_tensor(out=rs[:, :], in0=t1[:, :], scalar=1.5, in1=y[:, :],
                               op0=ALU.add, op1=ALU.mult).then_inc(done.full, 1)
        r.ready(done)
    part.step("vector", tick, moments)
    part.step("scalar", tick + 0.1, root_table)
    part.step("vector", tick + 0.2, newton)
    return done


TOP2_LINKS = 11


def top2(v, link, p, tmp, order):
    sel, c, q, m, first = (tmp[k] for k in ("sel", "c", "q", "m", "first"))
    g = m.shape[1]
    ob = order.unsqueeze(1).to_broadcast([P, g, 8])

    def choose(src, peak):
        link(v.tensor_reduce(peak, src, AX.X, ALU.max))
        link(v.tensor_tensor(c, src, spread(peak, 8), ALU.is_equal))
        link(v.tensor_tensor(c, c, ob, ALU.mult))
        link(v.tensor_reduce(m, c, AX.X, ALU.max))

    choose(p, first)
    link(v.tensor_tensor(sel, c, spread(m, 8), ALU.is_equal))
    link(v.scalar_tensor_tensor(out=q, in0=sel, scalar=-3.0e38, in1=p, op0=ALU.mult, op1=ALU.add))
    choose(q, tmp["second"])
    link(v.tensor_tensor(q, c, spread(m, 8), ALU.is_equal))
    return sel, q


def split_keys_or_queries(v, ready_hi, link, f, hi, minus_m1, minus_m2, out):
    ready_hi()
    link(v.scalar_tensor_tensor(out=f, in0=hi, scalar=minus_m1, in1=f, op0=ALU.mult, op1=ALU.add))
    link(v.tensor_copy(hi, f))
    return v.scalar_tensor_tensor(out=out, in0=hi, scalar=minus_m2, in1=f, op0=ALU.mult, op1=ALU.add)


def prepare0(nc, a, x, xnT, ident, st, order, w):
    with ExitStack() as ctx:
        blk = Block(nc, ctx, "p0")
        qw, kw = blk.sbuf("qw", [P, HS, D]), blk.sbuf("kw", [P, HS, D])
        selv, wk = blk.sbuf("selv", [D, 160]), blk.sbuf("wk", [D, 2, P])
        bv, bk = blk.sbuf("bv", [P, 32]), blk.sbuf("bk", [P, 2])
        route = blk.sbuf("route", [P, 1])
        loads_x, loads_w = blk.slot("loads_x", step=16), blk.slot("loads_w", step=16 * 9)
        eye = blk.slot("eye")
        xn = blk.slot("xn", [P, 4, D])
        xs = blk.slot("xs", [P, 4 * P])
        kf, kh = blk.slot("kf", [P, 2, 512]), blk.slot("kh", [P, 2, 512], BF16)
        v32, split, kept = blk.slot("v32"), blk.slot("split"), blk.slot("kept")
        turned = blk.bank("turned", [P, 512])
        logits = blk.bank("logits", [P, 4, 256])
        keys = blk.bank("keys", [P, 2, 512])
        qk_ps = blk.bank("qk", [P, HS, P])

        first = blk.part("first")
        ux, uw, ue, uq = first.use(loads_x), first.use(loads_w), first.use(eye), first.use(qk_ps)

        def load(r):
            e = r.eng
            e.dma_start(x[:, :, :], a["x"].rearrange("(t p) d -> p t d", p=P)).then_inc(ux.full, 16)
            for dst, src in (
                (qw[:, :, :], a["q_w"].rearrange("(h p) d -> p h d", p=PS)),
                (kw[:, :, :], a["k_w"].rearrange("(h p) d -> p h d", p=PS)),
                (selv[:, :], a["selv"]), (wk[:, :, :], a["wk"]),
                (bv[:, :], a["bv"].partition_broadcast(P)), (bk[:, :], a["bk"]),
                (route[:, :], a["route"].partition_broadcast(P)),
                (order[:, :], a["order"].partition_broadcast(P)), (w["split"][:, :], a["split"]),
            ):
                e.dma_start(dst, src).then_inc(uw.full, 16)
        first.step("sync", 0, load)

        def eye_zero(r):
            r.eng.memset(ident[:, :], 0.0).then_inc(ue.full, 1)
            r.ready(ue)
            r.eng.affine_select(out=ident[:, :], in_=ident[:, :], compare_op=ALU.not_equal, fill=1.0,
                                base=0, pattern=[[-1, P]], channel_multiplier=1).then_inc(ue2.full, 1)
        ue2 = first.use(eye)
        first.step("gpsimd", 0, eye_zero)
        stats = layer_norm_stats(blk, first, 0, x, st, ux)

        def heads(r):
            r.ready(uw)
            r.ready(ue2)
            for h in range(HS):
                last = r.eng.matmul(qk_ps.buf[:, h, :], qw[:, h, :], kw[:, h, :], start=True, stop=True)
            last.then_inc(uq.full, 1)

        def keep_heads(r):
            r.ready(uq)
            r.eng.activation(w["qk"][:, :, :], qk_ps.buf[:, :, :], ACT.Copy).then_inc(uq.free, 1)
        first.step("tensor", 0, heads)
        first.step("scalar", 0.5, keep_heads)
        first.step("scalar", 0.6, lambda r: r.ready(uw))
        first.step("vector", 0.6, lambda r: r.ready(uw))

        tiles = blk.part("tiles", rounds=NT // 4)
        u = {n: tiles.use(s) for n, s in (
            ("xn", xn), ("xs", xs), ("kf", kf), ("kh", kh), ("v32", v32),
            ("turned", turned), ("logits", logits), ("keys", keys), ("kept", kept))}
        slinks = tiles.chain(split, 2)

        def normalise(r):
            v = r.eng
            r.claim(u["xn"])
            for j in range(4):
                last = v.tensor_scalar(xn.buf[:, j, :], x[:, r.i * 4 + j, :], st["mean"][:, bass.ds(r.i * 4 + j, 1)],
                                       st["rstd"][:, bass.ds(r.i * 4 + j, 1)], ALU.subtract, ALU.mult)
            last.then_inc(u["xn"].full, 1)
        tiles.step("vector", 0, normalise)

        def turn(r):
            r.ready(u["xn"])
            r.claim(u["turned"])
            for j in range(4):
                last = r.eng.transpose(turned.buf[:, j * P:(j + 1) * P], xn.buf[:, j, :], ident[:, :])
            last.then_inc(u["turned"].full, 1)
        tiles.step("tensor", 1, turn)

        def keep_turned(r):
            r.ready(u["turned"])
            r.claim(u["xs"])
            r.eng.activation(xs.buf[:, :], turned.buf[:, :], ACT.Copy).then_inc(u["xs"].full, 1)
        tiles.step("scalar", 2, keep_turned)

        def keep_xnT(r):
            r.ready(u["xs"])
            r.eng.tensor_copy(xnT[:, bass.ds(r.i * 512, 512)], xs.buf[:, :]).then_inc(u["kept"].full, 1)
        tiles.step("gpsimd", 3, keep_xnT)

        def project(r):
            r.ready(u["xs"])
            r.claim(u["logits"])
            for j in range(4):
                last = r.eng.matmul(logits.buf[:, j, 0:160], xs.buf[:, j * P:(j + 1) * P], selv[:, :],
                                    start=True, stop=True)
            last.then_inc(u["logits"].full, 1)
            r.claim(u["keys"])
            for hh in range(2):
                last = r.eng.matmul(keys.buf[:, hh, :], wk[:, hh, :], xs.buf[:, :], start=True, stop=True)
            last.then_inc(u["keys"].full, 1)
        tiles.step("tensor", 4, project)

        def keep_values(r):
            r.ready(u["logits"])
            r.eng.tensor_tensor(w["v32"][:, bass.ds(r.i * 4, 4), :], logits.buf[:, :, 128:160],
                                bv[:, :].unsqueeze(1).to_broadcast([P, 4, 32]), ALU.add)\
                .then_inc(u["v32"].full, 1)
            r.eng.sem_inc(u["xn"].free, 1)
        tiles.step("vector", 5, keep_values)

        def sigmoid_exps(r):
            r.ready(u["v32"])
            r.eng.sem_inc(u["turned"].free, 1)
            r.eng.activation(w["gate"][:, bass.ds(r.i * 4, 4), :], logits.buf[:, :, 0:128], ACT.Exp,
                             scale=-1.0).then_inc(u["logits"].free, 1)
            r.ready(u["keys"])
            r.claim(u["kf"])
            for hh in range(2):
                r.eng.activation(kf.buf[:, hh, :], keys.buf[:, hh, :], ACT.Identity, bias=bk[:, hh:hh + 1])
                last = r.eng.activation(kh.buf[:, hh, :], keys.buf[:, hh, :], ACT.Identity, bias=bk[:, hh:hh + 1])
            last.then_inc(u["kf"].full, 1)
        tiles.step("scalar", 6, sigmoid_exps)

        def split_keys(r):
            v, link = r.eng, Links(r, slinks)
            split_keys_or_queries(
                v, lambda: r.ready(u["kf"]), link, kf.buf[:, :, :], kh.buf[:, :, :], w["split"][:, 2:3],
                w["split"][:, 3:4], w["ks"][:, :, bass.ds(r.i * 512, 512)]).then_inc(u["kf"].free, 1)
            v.sem_inc(u["keys"].free, 1)
            r.ready(u["kept"])
            v.sem_inc(u["xs"].free, 1)
        tiles.step("vector", 7, split_keys)

        gates = blk.part("gates", rounds=4)
        tmp = {n: blk.sbuf(f"t2_{n}", [P, 128, 8]) for n in ("sel", "c", "q")} | {
            n: blk.sbuf(f"t2_{n}", [P, 128]) for n in ("m", "first", "second")}
        tmp = {k: (b[:, :, :] if len(b.shape) == 3 else b[:, :]) for k, b in tmp.items()}
        prob = blk.sbuf("t2_prob", [P, 128, 8])[:, :, :]
        glinks = gates.chain(blk.slot("gates"), 2 + TOP2_LINKS + 7)

        def route_gates(r):
            v, link = r.eng, Links(r, glinks)
            r.all_freed(logits)
            flat = w["gate"][:, bass.ds(r.i * 8, 8), :].rearrange("p t (g e) -> p (t g) e", e=8)
            link(v.tensor_scalar(prob, flat, 1.0, None, ALU.add))
            link(v.reciprocal(prob, prob))
            one, other = top2(v, link, prob, tmp, order[:, :])
            link(v.tensor_tensor(one, one, other, ALU.add))
            link(v.tensor_tensor(one, one, prob, ALU.mult))
            link(v.tensor_reduce(tmp["m"], one, AX.X, ALU.add))
            link(v.tensor_scalar(tmp["m"], tmp["m"], 1e-9, None, ALU.max))
            link(v.reciprocal(tmp["m"], tmp["m"]))
            link(v.tensor_scalar(tmp["m"], tmp["m"], route[:, 0:1], None, ALU.mult))
            link(v.tensor_tensor(flat, one, spread(tmp["m"], 8), ALU.mult))
        gates.step("vector", 0, route_gates)
        blk.run()


def main0(nc, a, x, xnT, ident, w):
    with ExitStack() as ctx:
        blk = Block(nc, ctx, "m0")
        sb, slot = blk.sbuf, blk.slot
        bq = sb("bq", [P, H0 // 2])
        identb = sb("identb", [P, P], BF16)
        consts = slot("consts", step=16)
        eyeb = slot("eyeb")
        tally = slot("tally")
        wq = slot("wq", [D, P], step=16)
        wv = slot("wv", [D, ES * PS], step=16)
        wo = slot("wo", [PS, ES * D], step=16)
        xcur = slot("xcur", [D, T])
        qf, qh = slot("qf", [P, T]), sb("qh", [P, T], BF16)
        qsplit = slot("qsplit")
        qnext, qcur = slot("qnext", [P, T], BF16), slot("qcur", [P, T], BF16)
        peaks = sb("peaks", [P, TPB, 2])
        mparts, mrest = slot("mparts", [P, TPB, 2, 3], BF16), sb("mrest", [P, TPB, 2])
        mchain, mrows = slot("mchain"), slot("mrows", [6, T], BF16)
        vnext, vcur = slot("vnext", [P, TPB, PS]), slot("vcur", [P, TPB, PS])
        qk, v32 = slot("qk", [D, D]), slot("v32", [P, TPB, 32])
        yT = slot("yT", [D, T])
        neg = [slot(f"neg{k}", [P, 1]) for k in range(2)]
        prob = [slot(f"prob{k}", [P, T]) for k in range(2)]
        den = sb("den", [P, TPB])
        probT = [slot(f"probT{k}", [P, TPB, 2 * P]) for k in range(2)]
        ctxT = [slot(f"ctxT{k}", [PS, 2 * P]) for k in range(2)]
        rden, go = slot("rden", [P, 2]), sb("go", [P, TPB, ES])
        expA = [slot(f"expA{k}", [P, T]) for k in range(2)]
        sumsT = slot("sumsT", [P, 512])
        vprod, oprod = slot("vprod", [P, ES, P]), [sb(f"oprod{k}", [P, ES, P]) for k in range(2)]
        part_sum = [slot(f"part_sum{k}", [P, D]) for k in range(2)]
        sums = blk.bank("sums", [P, 512])
        ctx_ps = blk.bank("ctx", [P, 512])
        blk.ring(3, [P, T])

        def of(r, n_is):
            n = r.i + (r.part.base + n_is)
            return n // HS, n % HS

        def begin(part, ahead):
            u = {k: part.use(s) for k, s in (
                ("wq", wq), ("wv", wv), ("xcur", xcur), ("qf", qf), ("qnext", qnext),
                ("mparts", mparts), ("vnext", vnext))}
            split_links, m_links = part.chain(qsplit, 2), part.chain(mchain, 4)
            qps = part.ring()

            def load(r):
                b, h = of(r, ahead)
                r.claim(u["wq"])
                r.eng.dma_start(wq.buf[:, :], a["wq"][bass.ds(h, 1), :, :].rearrange("h d m -> (h d) m"))\
                    .then_inc(u["wq"].full, 16)
                r.claim(u["wv"])
                r.eng.dma_start(wv.buf[:, :].rearrange("d (e p) -> d e p", e=ES),
                                a["v_w"][bass.ds(h * ES, ES), :, :].rearrange("e d p -> d e p"))\
                    .then_inc(u["wv"].full, 16)
            part.step("sync", 0, load)

            def copy_x(r):
                b, h = of(r, ahead)
                r.claim(u["xcur"])
                r.eng.tensor_copy(xcur.buf[:, :], xnT[:, bass.ds(b * T, T)]).then_inc(u["xcur"].full, 1)
            part.step("gpsimd", 0, copy_x)

            def queries(r):
                r.ready(u["wq"])
                r.ready(u["xcur"])
                r.claim(qps)
                for c in range(2):
                    last = r.eng.matmul(qps.buf[:, c * 512:(c + 1) * 512], wq.buf[:, :],
                                        xcur.buf[:, c * 512:(c + 1) * 512], start=True, stop=True)
                last.then_inc(qps.full, 1)
            part.step("tensor", 0.1, queries, [qps])

            def keep_queries(r):
                b, h = of(r, ahead)
                r.ready(qps)
                r.eng.sem_inc(u["wq"].free, 1)
                r.claim(u["qf"])
                for out in (qf.buf, qh):
                    last = r.eng.activation(out[:, :], qps.buf[:, :], ACT.Identity, bias=bq[:, bass.ds(h, 1)],
                                            scale=HD ** -0.5)
                last.then_inc(qps.free, 1)
            part.step("scalar", 0.2, keep_queries)

            def split_queries(r):
                v, link = r.eng, Links(r, split_links)

                def both():
                    v.wait_ge(qps.free, r.nth(qps) + 2)
                    r.claim(u["qnext"])
                split_keys_or_queries(v, both, link, qf.buf[:, :], qh[:, :], w["split"][:, 0:1],
                                      w["split"][:, 1:2], qnext.buf[:, :]).then_inc(u["qnext"].full, 1)
            part.step("vector", 0.3, split_queries)

            def free_qf(r):
                r.ready(u["qnext"])
                r.eng.sem_inc(u["qf"].free, 1)
            part.step("gpsimd", 0.4, free_qf)

            for t in range(TPB):
                for hh in range(2):
                    ps = part.ring()

                    def scores(r, t=t, hh=hh, ps=ps):
                        b, _ = of(r, ahead)
                        if t == 0 and hh == 0:
                            r.ready(u["qnext"])
                        r.claim(ps)
                        for c in range(2):
                            last = r.eng.matmul(ps.buf[:, c * 512:(c + 1) * 512],
                                                qnext.buf[:, t * P:(t + 1) * P],
                                                w["ks"][:, hh, bass.ds(b * T + c * 512, 512)],
                                                start=True, stop=True)
                        last.then_inc(ps.full, 1)
                    part.step("tensor", 1 + t + 0.1 * hh, scores, [ps])

                    def largest(r, t=t, hh=hh, ps=ps):
                        r.ready(ps)
                        r.eng.tensor_reduce(peaks[:, t, hh:hh + 1], ps.buf[:, :], AX.X, ALU.max)\
                            .then_inc(ps.free, 1)
                        if t == TPB - 1 and hh == 1:
                            r.eng.wait_ge(ps.free, r.nth(ps) + 2)
                    part.step("vector", 1 + t + 0.1 * hh, largest)

                vps, pr = part.ring(), part.use(vprod)

                def values(r, t=t, vps=vps):
                    if t == 0:
                        r.ready(u["wv"])
                    r.claim(vps)
                    for c in range(2):
                        last = r.eng.matmul(vps.buf[:, c * 512:(c + 1) * 512],
                                            xcur.buf[:, t * P:(t + 1) * P],
                                            wv.buf[:, c * 512:(c + 1) * 512], start=True, stop=True)
                    last.then_inc(vps.full, 1)
                part.step("tensor", 1.5 + t, values, [vps])

                def gate_values(r, t=t, vps=vps, pr=pr):
                    b, h = of(r, ahead)
                    r.ready(vps)
                    r.claim(pr)
                    gate = w["gate"][:, bass.ds(b * TPB + t, 1), bass.ds(h * ES, ES)]\
                        .rearrange("p o e -> p (o e)")
                    r.eng.tensor_tensor(pr.buf[:, :, :], vps.buf[:, :].rearrange("p (e d) -> p e d", e=ES),
                                        spread(gate, P), ALU.mult).then_inc(vps.free, 1)
                    if t == TPB - 1:
                        r.eng.sem_inc(u["wv"].free, 1)
                        r.eng.sem_inc(u["xcur"].free, 1)
                    r.eng.wait_ge(vps.free, r.nth(vps) + 2)
                    if t == 0:
                        r.claim(u["vnext"])
                    r.eng.tensor_reduce(vnext.buf[:, t, :], pr.buf[:, :, :].rearrange("p e d -> p d e"),
                                        AX.X, ALU.add).then_inc(pr.free, 1)
                    if t == TPB - 1:
                        r.eng.wait_ge(pr.free, r.nth(pr) + 2)
                        r.eng.sem_inc(u["vnext"].full, 1)
                part.step("vector", 1.6 + t, gate_values)

            def cut_peaks(r):
                v, link = r.eng, Links(r, m_links)
                r.claim(u["mparts"])
                mp = mparts.buf
                link(v.tensor_scalar(mrest[:, :, :], peaks[:, :, :], -1.0, None, ALU.mult))
                link(v.tensor_copy(mp[:, :, :, 0], mrest[:, :, :]))
                link(v.tensor_tensor(mrest[:, :, :], mrest[:, :, :], mp[:, :, :, 0], ALU.subtract))
                link(v.tensor_copy(mp[:, :, :, 1], mrest[:, :, :]))
                v.tensor_tensor(mp[:, :, :, 2], mrest[:, :, :], mp[:, :, :, 1], ALU.subtract)\
                    .then_inc(u["mparts"].full, 1)
            part.step("vector", 9, cut_peaks)
            mps = part.ring()

            def turn_peaks(r):
                r.ready(u["mparts"])
                r.claim(mps)
                rows = mps.buf[:, 0:512].bitcast(BF16)
                for t in range(TPB):
                    last = r.eng.transpose(rows[0:6, t * P:(t + 1) * P],
                                           mparts.buf[:, t, :, :].rearrange("p h c -> p (h c)"), identb[:, :])
                last.then_inc(mps.full, 1)
            part.step("tensor", 9.1, turn_peaks, [mps])

            mr = part.use(mrows)

            def keep_peaks(r):
                r.ready(mps)
                r.eng.sem_inc(u["mparts"].free, 1)
                r.claim(mr)
                r.eng.activation(mrows.buf[:, :], mps.buf[0:6, 0:512].bitcast(BF16), ACT.Copy).then_inc(mr.full, 1)
                r.ready(mr)
                r.eng.sem_inc(mps.free, 1)
            part.step("scalar", 9.2, keep_peaks)

            qc, vc = part.use(qcur), part.use(vcur)

            def hand_queries(r):
                r.claim(qc)
                r.eng.tensor_copy(qcur.buf[0:96, :], qnext.buf[0:96, :])
                r.ready(mr)
                r.eng.tensor_copy(qcur.buf[96:102, :], mrows.buf[:, :]).then_inc(qc.full, 1)
                r.ready(qc)
                r.eng.sem_inc(mr.free, 1)
                r.eng.sem_inc(u["qnext"].free, 1)
            part.step("vector", 11, hand_queries)

            def hand_values(r):
                r.claim(vc)
                r.ready(u["vnext"])
                r.eng.activation(vcur.buf[:, :, :], vnext.buf[:, :, :], ACT.Copy).then_inc(vc.full, 1)
                r.ready(vc)
                r.eng.sem_inc(u["vnext"].free, 1)
            part.step("scalar", 11, hand_values)

        def finish(part):
            u = {k: part.use(s) for k, s in (
                ("wo", wo), ("qk", qk), ("v32", v32), ("yT", yT), ("sums", sums), ("sumsT", sumsT))}
            yps = part.ring()

            def load(r):
                _, h = of(r, 0)
                r.claim(u["wo"])
                r.eng.dma_start(wo.buf[:, :].rearrange("p (e d) -> p e d", e=ES),
                                a["o_w"][bass.ds(h * ES, ES), :, :].rearrange("e p d -> p e d"))\
                    .then_inc(u["wo"].full, 16)
            part.step("sync", 0, load)

            def copies(r):
                b, h = of(r, 0)
                r.claim(u["qk"])
                r.eng.tensor_copy(qk.buf[:, :], w["qk"][:, bass.ds(h, 1), :].rearrange("d h e -> d (h e)"))\
                    .then_inc(u["qk"].full, 1)
                r.claim(u["v32"])
                r.eng.tensor_copy(v32.buf[:, :, :], w["v32"][:, bass.ds(b * TPB, TPB), :])\
                    .then_inc(u["v32"].full, 1)
            part.step("gpsimd", 0, copies)

            def make_y(r):
                b, _ = of(r, 0)
                r.ready(u["qk"])
                r.claim(yps)
                for c in range(2):
                    last = r.eng.matmul(yps.buf[:, c * 512:(c + 1) * 512], qk.buf[:, :],
                                        xnT[:, bass.ds(b * T + c * 512, 512)], start=True, stop=True)
                last.then_inc(yps.full, 1)
            part.step("tensor", 0, make_y, [yps])

            def keep_y(r):
                r.ready(yps)
                r.eng.sem_inc(u["qk"].free, 1)
                r.claim(u["yT"])
                r.eng.activation(yT.buf[:, :], yps.buf[:, :], ACT.Copy, scale=SW_SCALE).then_inc(u["yT"].full, 1)
                r.ready(u["yT"])
                r.eng.sem_inc(yps.free, 1)
            part.step("scalar", 0.1, keep_y)

            ctx_uses = []
            for t in range(TPB):
                ps, ng, pb = part.ring(), part.use(neg[t % 2]), part.use(prob[t % 2])

                def scores(r, t=t, ps=ps):
                    b, _ = of(r, 0)
                    if t == 0:
                        r.ready(u["yT"])
                    r.claim(ps)
                    for c in range(2):
                        last = r.eng.matmul(ps.buf[:, c * 512:(c + 1) * 512], yT.buf[:, t * P:(t + 1) * P],
                                            xnT[:, bass.ds(b * T + c * 512, 512)], start=True, stop=True)
                    last.then_inc(ps.full, 1)
                part.step("tensor", 0.3 + t, scores, [ps])

                def largest(r, t=t, ps=ps, ng=ng):
                    r.ready(ps)
                    r.claim(ng)
                    r.eng.tensor_reduce(ng.buf[:, :], ps.buf[:, :], AX.X, ALU.max, negate=True)\
                        .then_inc(ng.full, 1)
                part.step("vector", 0.4 + t, largest)

                def softmax(r, t=t, ps=ps, ng=ng, pb=pb):
                    r.ready(ng)
                    r.claim(pb)
                    r.eng.activation(pb.buf[:, :], ps.buf[:, :], ACT.Exp, bias=ng.buf[:, :],
                                     accum_out=den[:, t:t + 1]).then_inc(pb.full, 1)
                    r.ready(pb)
                    r.eng.sem_inc(ps.free, 1)
                    r.eng.sem_inc(ng.free, 1)
                    if t == TPB - 1:
                        r.eng.sem_inc(u["yT"].free, 1)
                part.step("scalar", 0.5 + t, softmax)

                tps = part.ring()
                if t % 2 == 0:
                    pT = part.use(probT[(t // 2) % 2])

                def turn(r, tps=tps, pb=pb):
                    r.ready(pb)
                    r.claim(tps)
                    for c in range(TPB):
                        last = r.eng.transpose(tps.buf[:, c * P:(c + 1) * P], pb.buf[:, c * P:(c + 1) * P],
                                               ident[:, :])
                    last.then_inc(tps.full, 1)
                part.step("tensor", 1.2 + t, turn, [tps])

                def keep_turned(r, t=t, tps=tps, pT=pT, pb=pb):
                    r.ready(tps)
                    r.eng.sem_inc(pb.free, 1)
                    if t % 2 == 0:
                        r.claim(pT)
                    ins = r.eng.activation(pT.buf[:, :, (t % 2) * P:(t % 2 + 1) * P],
                                           tps.buf[:, :].rearrange("p (c q) -> p c q", c=TPB), ACT.Copy)\
                        .then_inc(tps.free, 1)
                    if t % 2:
                        r.eng.wait_ge(tps.free, r.nth(tps) + 2)
                        r.eng.sem_inc(pT.full, 1)
                part.step("scalar", 1.3 + t, keep_turned)

                if t % 2:
                    g = t // 2
                    cp, ct = part.use(ctx_ps), part.use(ctxT[g % 2])
                    rd = part.use(rden)
                    ctx_uses.append((pT, cp, ct))

                    def weigh(r, g=g, pT=pT, cp=cp):
                        if g == 0:
                            wait_handed(r, vcur)
                        r.ready(pT)
                        r.claim(cp)
                        for k in range(TPB):
                            last = r.eng.matmul(cp.buf[:, 0:2 * P], vcur.buf[:, k, :], pT.buf[:, k, :],
                                                start=(k == 0), stop=(k == TPB - 1))
                        last.then_inc(cp.full, 1)
                    part.step("tensor", 2.25 + t, weigh)

                    def keep_ctx(r, g=g, pT=pT, cp=cp, ct=ct):
                        r.ready(cp)
                        r.eng.sem_inc(pT.free, 1)
                        if g == TPB // 2 - 1:
                            r.eng.sem_inc(vcur.free, 1)
                        r.claim(ct)
                        r.eng.activation(ct.buf[:, :], cp.buf[:, 0:2 * P], ACT.Copy).then_inc(ct.full, 1)
                        r.ready(ct)
                        r.eng.sem_inc(cp.free, 1)
                    part.step("scalar", 2.3 + t, keep_ctx)

                    def output_gates(r, g=g, rd=rd, pb=pb):
                        b, h = of(r, 0)
                        r.ready(pb)
                        r.eng.reciprocal(rden.buf[:, :], den[:, 2 * g:2 * g + 2]).then_inc(rd.full, 1)
                        r.ready(rd)
                        r.eng.tensor_tensor(go[:, 2 * g:2 * g + 2, :],
                                            w["gate"][:, bass.ds(b * TPB + 2 * g, 2), bass.ds((h + HS) * ES, ES)],
                                            spread(rden.buf[:, :], ES), ALU.mult).then_inc(rd.free, 1)
                        r.eng.wait_ge(rd.free, r.nth(rd) + 2)
                    part.step("vector", 2.3 + t, output_gates)

                    for tt in (t - 1, t):
                        ops, pr, ss = part.ring(), oprod[tt % 2], part.use(part_sum[tt % 2])

                        def outputs(r, tt=tt, ct=ct, ops=ops):
                            if tt == 0:
                                r.ready(u["wo"])
                            r.ready(ct)
                            r.claim(ops)
                            for c in range(2):
                                last = r.eng.matmul(ops.buf[:, c * 512:(c + 1) * 512],
                                                    ct.buf[:, (tt % 2) * P:(tt % 2 + 1) * P],
                                                    wo.buf[:, c * 512:(c + 1) * 512], start=True, stop=True)
                            last.then_inc(ops.full, 1)
                        part.step("tensor", 3.25 + t + 0.3 * (tt % 2), outputs, [ops])

                        def gate_outputs(r, tt=tt, ct=ct, ops=ops, pr=pr, ss=ss):
                            r.ready(ops)
                            if tt % 2:
                                r.eng.sem_inc(ct.free, 1)
                            if tt == TPB - 1:
                                r.eng.sem_inc(u["wo"].free, 1)
                            r.claim(ss)
                            r.eng.tensor_tensor(pr[:, :, :],
                                                ops.buf[:, :].rearrange("p (e d) -> p e d", e=ES),
                                                spread(go[:, tt, :], P), ALU.mult).then_inc(ops.free, 1)
                            r.eng.wait_ge(ops.free, r.nth(ops) + 2)
                            r.eng.tensor_reduce(ss.buf[:, :], pr[:, :, :].rearrange("p e d -> p d e"),
                                                AX.X, ALU.add).then_inc(ss.full, 1)
                        part.step("vector", 3.4 + t + 0.3 * (tt % 2), gate_outputs)

                        def add_residual(r, tt=tt, ss=ss):
                            b, _ = of(r, 0)
                            r.ready_apart(ss, tally)
                            xt = x[:, bass.ds(b * TPB + tt, 1), :].rearrange("p o d -> p (o d)")
                            r.eng.tensor_tensor(xt, xt, ss.buf[:, :], ALU.add).then_inc(ss.free, 1)
                        part.step("gpsimd", 3.5 + t + 0.3 * (tt % 2), add_residual)

            for k in range(TPB):
                es = []
                for hh in range(2):
                    ps, e = part.ring(), part.use(expA[hh])
                    es.append(e)

                    def scoresT(r, k=k, hh=hh, ps=ps):
                        b, _ = of(r, 0)
                        if k == 0 and hh == 0:
                            wait_handed(r, qcur)
                        r.claim(ps)
                        for c in range(2):
                            last = r.eng.matmul(ps.buf[:, c * 512:(c + 1) * 512],
                                                w["ks"][:, hh, bass.ds(b * T + k * P, P)],
                                                qcur.buf[:, c * 512:(c + 1) * 512], start=True, stop=True)
                        last.then_inc(ps.full, 1)
                    part.step("tensor", 0.6 + k + 0.2 * hh, scoresT, [ps])

                    def exps(r, k=k, hh=hh, ps=ps, e=e):
                        r.ready(ps)
                        if k == TPB - 1 and hh == 1:
                            r.eng.sem_inc(qcur.free, 1)
                        r.claim(e)
                        r.eng.activation(e.buf[:, :], ps.buf[:, :], ACT.Exp).then_inc(e.full, 1)
                        r.ready(e)
                        r.eng.sem_inc(ps.free, 1)
                    part.step("scalar", 0.7 + k + 0.2 * hh, exps)

                def sum_values(r, k=k, es=es):
                    if k == 0:
                        r.ready(u["v32"])
                        r.claim(u["sums"])
                    for e in es:
                        r.ready(e)
                    for hh in range(2):
                        for c in range(2):
                            j = 2 * hh + c
                            last = r.eng.matmul(sums.buf[32 * j:32 * j + 32, :], v32.buf[:, k, :],
                                                es[hh].buf[:, c * 512:(c + 1) * 512],
                                                start=(k == 0), stop=(k == TPB - 1))
                            if c == 1:
                                last.then_inc(es[hh].free, 1)
                part.step("tensor", 1.95 + k, sum_values)

            def keep_sums(r):
                r.claim(u["sumsT"])
                r.eng.wait_ge(es_last[1].free, r.nth(es_last[1]) + 2)
                r.eng.sem_inc(u["v32"].free, 1)
                r.eng.activation(sumsT.buf[:, :], sums.buf[:, :], ACT.Copy).then_inc(u["sumsT"].full, 1)
                r.ready(u["sumsT"])
                r.eng.sem_inc(u["sums"].free, 1)
            es_last = es
            part.step("scalar", 9.5, keep_sums)
            sps = part.ring()

            def turn_sums(r):
                r.ready(u["sumsT"])
                r.claim(sps)
                for s in range(4):
                    last = r.eng.transpose(sps.buf[:, s * P:(s + 1) * P], sumsT.buf[:, s * P:(s + 1) * P],
                                           ident[:, :])
                last.then_inc(sps.full, 1)
            part.step("tensor", 10, turn_sums, [sps])

            def keep_o(r):
                b, h = of(r, 0)
                r.ready(sps)
                r.eng.sem_inc(u["sumsT"].free, 1)
                v = sps.buf[:, 0:512].rearrange("p (s h c k) -> p h c s k", s=4, h=2, c=2)
                for hh in range(2):
                    for c in range(2):
                        ins = r.eng.activation(
                            w["o_all"][:, bass.ds(b * TPB + c * 4, 4), bass.ds(h * 2 + hh, 1), :]
                            .rearrange("p s o k -> p s (o k)"), v[:, hh, c, :, 0:HD + 1], ACT.Copy)
                ins.then_inc(sps.free, 1)
            part.step("scalar", 10.1, keep_o)

        def wait_handed(r, slot):
            r.eng.wait_ge(slot.full, r.i + (r.part.base + 1))

        first = blk.part("first")
        uc = first.use(consts)
        ub = [first.use(eyeb) for _ in range(2)]
        first.step("sync", -1, lambda r: r.eng.dma_start(bq[:, :], a["bq"]).then_inc(uc.full, 16))

        def eye_b(r):
            r.eng.memset(qcur.buf[96:128, :], 0.0)
            r.eng.tensor_copy(identb[:, :], ident[:, :]).then_inc(ub[0].full, 1)
        first.step("vector", -1, eye_b)

        def scale_bias(r):
            r.ready(uc)
            r.eng.tensor_scalar(bq[:, :], bq[:, :], HD ** -0.5, None, ALU.mult).then_inc(ub[1].full, 1)
        first.step("vector", -0.9, scale_bias)
        first.step("scalar", -1, lambda r: r.ready(ub[1]))
        first.step("tensor", -1, lambda r: r.ready(ub[0]))
        begin(first, 0)
        loop = blk.part("loop", rounds=NT - 1)
        begin(loop, 1)
        finish(loop)
        finish(blk.part("last", base=NT - 1))
        blk.run()


def close0(nc, a, x, ident, w):
    with ExitStack() as ctx:
        blk = Block(nc, ctx, "c0")
        half = T // H0
        wo, bo = blk.sbuf("wo", [P, D]), blk.sbuf("bo", [1, D])
        ones = blk.sbuf("ones", [1, P])
        loads = blk.slot("loads", step=32)
        rden = blk.slot("rden", [P, TPB, H0])
        o = blk.slot("o", [P, H0 // 2, TPB, 2, HD])
        oT = blk.slot("oT", [P, half, H0])
        turned = blk.bank("turned", [P, T])
        out = blk.bank("out", [P, TPB, D])

        first = blk.part("first")
        ul, u1 = first.use(loads), first.use(rden)

        def load(r):
            r.eng.dma_start(wo[:, :], a["wo"]).then_inc(ul.full, 16)
            r.eng.dma_start(bo[:, :], a["bo"].unsqueeze(0)).then_inc(ul.full, 16)
        first.step("sync", 0, load)
        first.step("vector", 0, lambda r: r.eng.memset(ones[:, :], 1.0).then_inc(u1.full, 1))

        def wait_consts(r):
            r.ready(ul)
            r.ready(u1)
        first.step("tensor", 0, wait_consts)

        loop = blk.part("loop", rounds=B)
        u = {k: loop.use(s) for k, s in (("rden", rden), ("o", o), ("oT", oT), ("turned", turned), ("out", out))}

        def divide(r):
            v = r.eng
            tiles = w["o_all"][:, bass.ds(r.i * TPB, TPB), :, :]
            v.reciprocal(rden.buf[:, :, :], tiles[:, :, :, HD]).then_inc(u["rden"].full, 1)
            r.ready(u["rden"])
            r.claim(u["o"])
            for side in range(2):
                rows = slice(side * half, (side + 1) * half)
                for odd in range(2):
                    last = v.tensor_tensor(
                        o.buf[odd * half:(odd + 1) * half, :, :, side, :],
                        w["o_all"][rows, bass.ds(r.i * TPB, TPB), odd::2, 0:HD].rearrange("p t h k -> p h t k"),
                        spread(rden.buf[rows, :, odd::2].rearrange("p t h -> p h t"), HD), ALU.mult)
            last.then_inc(u["o"].full, 1)
        loop.step("vector", 0, divide)

        def turn(r):
            r.ready(u["o"])
            r.claim(u["turned"])
            for h in range(H0 // 2):
                last = r.eng.transpose(turned.buf[:, h * P:(h + 1) * P],
                                       o.buf[:, h, :, :, :].rearrange("u t s k -> u (t s k)"), ident[:, :])
            last.then_inc(u["turned"].full, 1)
        loop.step("tensor", 1, turn)

        def keep(r):
            r.ready(u["turned"])
            r.eng.sem_inc(u["o"].free, 1)
            r.claim(u["oT"])
            r.eng.activation(oT.buf[:, :, :], turned.buf[:, :].rearrange("p (h u) -> p u h", h=H0), ACT.Copy)\
                .then_inc(u["oT"].full, 1)
            r.ready(u["oT"])
            r.eng.sem_inc(u["turned"].free, 1)
        loop.step("scalar", 2, keep)

        def project(r):
            r.ready(u["oT"])
            r.claim(u["out"])
            for t in range(TPB):
                r.eng.matmul(out.buf[:, t, :], ones[:, :], bo[:, :], start=True, stop=False)
                last = r.eng.matmul(out.buf[:, t, :],
                                    oT.buf[:, t * P // H0:(t + 1) * P // H0, :].rearrange("p u h -> p (u h)"),
                                    wo[:, :], start=False, stop=True)
            last.then_inc(u["out"].full, 1)
        loop.step("tensor", 3, project)

        def add(r):
            r.ready(u["out"])
            r.eng.sem_inc(u["oT"].free, 1)
            xt = x[:, bass.ds(r.i * TPB, TPB), :]
            r.eng.tensor_tensor(xt, xt, out.buf[:, :, :], ALU.add).then_inc(u["out"].free, 1)
        loop.step("vector", 4, add)
        blk.run()


def prepare1(nc, a, x, xnT, ident, st, order, w):
    with ExitStack() as ctx:
        blk = Block(nc, ctx, "p1")
        gw, gb = blk.sbuf("gw", [D, EM]), blk.sbuf("gb", [P, EM])
        lg = blk.sbuf("lg", [P, NT, EM])
        loads = blk.slot("loads", step=32)
        xn, xs = blk.slot("xn", [P, 4, D]), blk.slot("xs", [P, 4 * P])
        kept, lgs = blk.slot("kept"), blk.slot("lgs")
        turned, logits = blk.bank("turned", [P, 512]), blk.bank("logits", [P, 4, EM])

        first = blk.part("first")
        ul = first.use(loads)

        def load(r):
            r.eng.dma_start(gw[:, :], a["gate_w"]).then_inc(ul.full, 16)
            r.eng.dma_start(gb[:, :], a["gate_b"].partition_broadcast(P)).then_inc(ul.full, 16)
        first.step("sync", 0, load)
        first.step("tensor", 0, lambda r: r.ready(ul))
        first.step("vector", 0, lambda r: r.ready(ul))
        layer_norm_stats(blk, first, 0, x, st, None)

        tiles = blk.part("tiles", rounds=NT // 4)
        u = {n: tiles.use(s) for n, s in (("xn", xn), ("xs", xs), ("turned", turned), ("logits", logits),
                                          ("kept", kept))}

        def normalise(r):
            r.claim(u["xn"])
            for j in range(4):
                at = r.i * 4 + j
                last = r.eng.tensor_scalar(xn.buf[:, j, :], x[:, at, :], st["mean"][:, bass.ds(at, 1)],
                                           st["rstd"][:, bass.ds(at, 1)], ALU.subtract, ALU.mult)
            last.then_inc(u["xn"].full, 1)
        tiles.step("vector", 0, normalise)

        def turn(r):
            r.ready(u["xn"])
            r.claim(u["turned"])
            for j in range(4):
                last = r.eng.transpose(turned.buf[:, j * P:(j + 1) * P], xn.buf[:, j, :], ident[:, :])
            last.then_inc(u["turned"].full, 1)
        tiles.step("tensor", 1, turn)

        def keep_turned(r):
            r.ready(u["turned"])
            r.eng.sem_inc(u["xn"].free, 1)
            r.claim(u["xs"])
            r.eng.activation(xs.buf[:, :], turned.buf[:, :], ACT.Copy).then_inc(u["xs"].full, 1)
            r.ready(u["xs"])
            r.eng.sem_inc(u["turned"].free, 1)
        tiles.step("scalar", 2, keep_turned)

        def keep_xnT(r):
            r.ready(u["xs"])
            r.eng.tensor_copy(xnT[:, bass.ds(r.i * 512, 512)], xs.buf[:, :]).then_inc(u["kept"].full, 1)
        tiles.step("gpsimd", 3, keep_xnT)

        def route(r):
            r.ready(u["xs"])
            r.claim(u["logits"])
            for j in range(4):
                last = r.eng.matmul(logits.buf[:, j, :], xs.buf[:, j * P:(j + 1) * P], gw[:, :],
                                    start=True, stop=True)
            last.then_inc(u["logits"].full, 1)
        tiles.step("tensor", 4, route)

        def keep_logits(r):
            r.ready(u["logits"])
            r.eng.tensor_tensor(lg[:, bass.ds(r.i * 4, 4), :], logits.buf[:, :, :],
                                gb[:, :].unsqueeze(1).to_broadcast([P, 4, EM]), ALU.add)\
                .then_inc(u["logits"].free, 1)
            r.ready(u["kept"])
            r.eng.sem_inc(u["xs"].free, 1)
        tiles.step("vector", 5, keep_logits)

        mix = blk.part("mix")
        tmp = {n: blk.sbuf(f"t2_{n}", [P, NT, 8])[:, :, :] for n in ("sel", "c", "q")} | {
            n: blk.sbuf(f"t2_{n}", [P, NT])[:, :] for n in ("m", "first", "second")}
        chain = mix.chain(blk.slot("mix"), TOP2_LINKS + 6)
        e, e_of = mix.use(lgs), mix.use(blk.slot("exps"))

        def choose(r):
            v, link = r.eng, Links(r, chain)
            r.all_freed(logits)
            one, other = top2(v, link, lg[:, :, :], tmp, order[:, :])
            link(v.tensor_tensor(one, one, other, ALU.add))
            link(v.tensor_tensor(lg[:, :, :], lg[:, :, :], spread(tmp["first"], 8), ALU.subtract))
            v.sem_inc(e.full, 1)
            r.ready(e_of)
            link(v.tensor_tensor(lg[:, :, :], lg[:, :, :], one, ALU.mult))
            link(v.tensor_reduce(tmp["m"], lg[:, :, :], AX.X, ALU.add))
            link(v.reciprocal(tmp["m"], tmp["m"]))
            link(v.tensor_tensor(w["combine"][:, :, 0:EM], lg[:, :, :], spread(tmp["m"], 8), ALU.mult))
            v.memset(w["combine"][:, :, EM:EM + 1], 1.0)

        def exps(r):
            r.ready(e)
            r.eng.activation(lg[:, :, :], lg[:, :, :], ACT.Exp).then_inc(e_of.full, 1)
        mix.step("vector", 0, choose)
        mix.step("scalar", 0, exps)
        blk.run()


def main1(nc, a, x, xnT, ident, w):
    with ExitStack() as ctx:
        blk = Block(nc, ctx, "m1")
        sb, slot = blk.sbuf, blk.slot
        wqT, wkT, wvT, woT = (sb(n, [D, D]) for n in ("wqT", "wkT", "wvT", "woT"))
        bqk, bv, bo = sb("bqk", [P, 2]), sb("bv", [P, D]), sb("bo", [1, D])
        proj, half = sb("proj", [P, HF * JF]), sb("half", [P, HF])
        vmask = sb("vmask", [P, 18])
        eps, ones, ones_rows = sb("eps", [P, 1]), sb("ones", [1, P]), sb("ones_rows", [HF, P])
        w1, b1 = sb("w1", [D, EM + 1, HID]), sb("b1", [P, EM + 1, HT])
        w2, b2 = sb("w2", [P, EM + 1, HT, D]), sb("b2", [EM + 1, D])
        n_loads = 15
        loads = slot("loads", step=16 * n_loads)
        consts, tally = slot("consts"), slot("tally")
        xcur = slot("xcur", [D, T])
        kT, k2 = slot("kT", [P, T]), slot("k2", [P, T])
        diag, peaks = slot("diag", [P, TPB, HF]), sb("peaks", [P, TPB, HF])
        dd = slot("dd", [P, TPB, HF * JF])
        stab, stab_in, stab_d = slot("stab"), sb("stab_in", [P, HF]), sb("stab_d", [HF, HF + 1])
        shift = slot("shift", [P, TPB, HF])
        vext = slot("vext", [P, TPB, FT, 18])
        kp = [slot(f"kp{k}", [P, HF * JF]) for k in range(2)]
        kpe = slot("kpe")
        kv = slot("kv", [P, FT, 18])
        qd = [slot(f"qd{k}", [P, HF * JF]) for k in range(2)]
        qsub, qmax = slot("qsub", [P, HF]), slot("qmax", [P, HF])
        qe = [slot(f"qe{k}") for k in range(2)]
        qpT = [slot(f"qpT{k}", [P, FT, P]) for k in range(2)]
        oden, o1 = slot("oden", [P, FT, 2]), slot("o1", [P, 4, D])
        o1T = slot("o1T", [P, 4 * P])
        hT = [slot(f"hT{k}", [P, HT, 512]) for k in range(2)]
        mixed = [slot(f"mixed{k}", [P, 4, D]) for k in range(2)]
        cT = slot("cT", [EM + 1, 512])
        cmb, biased = slot("cmb", [P, 4, EM + 1]), slot("biased", [P, 4, D])
        attn = slot("attn", [P, 512])
        kpx = [slot(f"kpx{k}") for k in range(2)]
        ochain = slot("ochain")
        ones16 = ones_rows[:, :]
        kv_ps, small = blk.bank("kv_sums", [P, FT, 18]), blk.bank("small", [P, 512])
        blk.ring(3, [P, T])

        first = blk.part("first")
        ul, uc = first.use(loads), [first.use(consts) for _ in range(2)]

        def load(r):
            for dst, src in (
                (wqT, a["wqT"]), (wkT, a["wkT"]), (wvT, a["wvT"]), (woT, a["woT"]), (bqk, a["bqk"]),
                (bv, a["bv1"].partition_broadcast(P)), (bo, a["bo1"].unsqueeze(0)), (proj, a["proj"]),
                (half, a["half"]), (vmask, a["vmask"]), (b2, a["b2"]),
            ):
                r.eng.dma_start(dst[:, :], src).then_inc(ul.full, 16)
            r.eng.dma_start(b1[:, :, :], a["b1"].rearrange("e (t p) -> p e t", p=P), allow_slow_non_contiguous=True)\
                .then_inc(ul.full, 16)
            r.eng.dma_start(w1[:, 0:EM, :], a["w1"].rearrange("e d h -> d e h")).then_inc(ul.full, 16)
            r.eng.dma_start(w1[:, EM, :], a["ws1"]).then_inc(ul.full, 16)
            r.eng.dma_start(w2[:, :, :, :], a["w2"].rearrange("e (t p) d -> p e t d", p=P)).then_inc(ul.full, 16)
        first.step("sync", 0, load)

        def constants(r):
            v = r.eng
            v.memset(eps[:, :], EPS_FEAT)
            v.memset(ones[:, :], 1.0)
            v.memset(ones_rows[:, :], 1.0)
            v.memset(vext.buf[:, :, :, 16:18], 1.0)
            r.ready(ul)
            v.tensor_scalar(bqk[:, :], bqk[:, :], DN, None, ALU.mult).then_inc(uc[0].full, 1)
            r.ready(uc[0])
        first.step("vector", 0, constants)
        for engine in ("tensor", "scalar", "gpsimd"):
            first.step(engine, 0, lambda r: (r.ready(ul), r.ready(uc[0])))

        loop = blk.part("loop", rounds=B)
        performer(loop, blk, locals())
        experts(loop, blk, locals())
        blk.run()


def performer(part, blk, n):
    (xnT, x, w, ident) = (n[k] for k in ("xnT", "x", "w", "ident"))
    u = {k: part.use(n[k]) for k in ("xcur", "diag", "dd", "shift", "vext", "kv", "kv_ps")}

    def copy_x(r):
        r.claim(u["xcur"])
        r.eng.tensor_copy(n["xcur"].buf[:, :], xnT[:, bass.ds(r.i * T, T)]).then_inc(u["xcur"].full, 1)
    part.step("gpsimd", 0, copy_x)

    vps = part.ring()

    def values(r):
        r.ready(u["xcur"])
        r.claim(vps)
        for t in range(TPB):
            last = r.eng.matmul(vps.buf[:, t * P:(t + 1) * P], n["xcur"].buf[:, t * P:(t + 1) * P],
                                n["wvT"][:, :], start=True, stop=True)
        last.then_inc(vps.full, 1)
    part.step("tensor", 0.1, values, [vps])

    def keep_values(r):
        r.ready(vps)
        r.claim(u["vext"])
        for t in range(TPB):
            last = r.eng.tensor_tensor(
                n["vext"].buf[:, t, :, 0:16], vps.buf[:, t * P:(t + 1) * P].rearrange("p (f k) -> p f k", f=FT),
                n["bv"][:, :].rearrange("p (f k) -> p f k", f=FT), ALU.add)
        last.then_inc(vps.free, 1)
        r.eng.wait_ge(vps.free, r.nth(vps) + 2)
        r.eng.sem_inc(u["vext"].full, 1)
    part.step("vector", 0.2, keep_values)

    def side(tick, weights, col, name):
        ps, t, sq, dps, dg = (part.ring(), part.use(n["kT"]), part.use(n["k2"]), part.use(n["small"]), None)

        def product(r):
            r.ready(u["xcur"])
            r.claim(ps)
            for c in range(2):
                last = r.eng.matmul(ps.buf[:, c * 512:(c + 1) * 512], n[weights][:, :],
                                    n["xcur"].buf[:, c * 512:(c + 1) * 512], start=True, stop=True)
            last.then_inc(ps.full, 1)
        part.step("tensor", tick, product, [ps])

        def keep(r):
            r.ready(ps)
            if col == 0:
                r.eng.sem_inc(u["xcur"].free, 1)
            r.claim(t)
            r.eng.activation(n["kT"].buf[:, :], ps.buf[:, :], ACT.Identity, bias=n["bqk"][:, col:col + 1],
                             scale=DN).then_inc(t.full, 1)
            r.ready(t)
            r.eng.sem_inc(ps.free, 1)
        part.step("scalar", tick + 0.1, keep)

        def square(r):
            r.ready(t)
            r.claim(sq)
            r.eng.tensor_tensor(n["k2"].buf[:, :], n["kT"].buf[:, :], n["kT"].buf[:, :], ALU.mult)\
                .then_inc(sq.full, 1)
        part.step("gpsimd", tick + 0.2, square)

        def half_sums(r):
            r.ready(sq)
            r.claim(dps)
            for k in range(TPB):
                last = r.eng.matmul(n["small"].buf[:, k * HF:(k + 1) * HF], n["k2"].buf[:, k * P:(k + 1) * P],
                                    n["half"][:, :], start=True, stop=True)
            last.then_inc(dps.full, 1)
        part.step("tensor", tick + 0.5, half_sums)
        return t, sq, dps

    kt, k2, kd = side(0.3, "wkT", 1, "k")
    dg = u["diag"]

    def keep_diag(r):
        r.ready(kd)
        r.eng.sem_inc(k2.free, 1)
        r.claim(dg)
        r.eng.activation(n["diag"].buf[:, :, :], n["small"].buf[:, 0:P].rearrange("p (t h) -> p t h", t=TPB),
                         ACT.Copy).then_inc(dg.full, 1)
        r.ready(dg)
        r.eng.sem_inc(kd.free, 1)
    part.step("scalar", 0.9, keep_diag)

    for t in range(TPB):
        ps, at = part.ring(), 1 + 0.6 * t

        def features(r, t=t, ps=ps):
            if t == 0:
                r.ready(kt)
            r.claim(ps)
            for c in range(2):
                last = r.eng.matmul(ps.buf[:, c * 512:(c + 1) * 512], n["kT"].buf[:, t * P:(t + 1) * P],
                                    n["proj"][:, c * 512:(c + 1) * 512], start=True, stop=True)
            last.then_inc(ps.full, 1)
        part.step("tensor", at, features, [ps])

        kept = part.use(n["kpe"])

        def keep_features(r, t=t, ps=ps, kept=kept):
            r.ready(ps)
            if t == 0:
                r.claim(u["dd"])
            if t == TPB - 1:
                r.eng.sem_inc(kt.free, 1)
            r.eng.activation(n["dd"].buf[:, t, :], ps.buf[:, :], ACT.Copy).then_inc(kept.full, 1)
            r.ready(kept)
            r.eng.sem_inc(ps.free, 1)
        part.step("scalar", at + 0.1, keep_features)

        def largest(r, t=t, kept=kept):
            r.ready(kept)
            ins = r.eng.tensor_reduce(n["peaks"][:, t, :], n["dd"].buf[:, t, :].rearrange("p (h j) -> p h j", h=HF),
                                      AX.X, ALU.max)
            if t == TPB - 1:
                ins.then_inc(u["dd"].full, 1)
        part.step("vector", at + 0.2, largest)

    s = [part.use(n["stab"]) for _ in range(3)]
    sp, sp2 = part.ring(), part.ring()
    at = 6

    def over_tiles(r):
        r.ready(u["dd"])
        r.eng.tensor_reduce(n["stab_in"][:, :], n["peaks"][:, :, :].rearrange("p t h -> p h t"), AX.X, ALU.max)\
            .then_inc(s[0].full, 1)
    part.step("vector", at, over_tiles)

    def turn_stab(r):
        r.ready(s[0])
        r.claim(sp)
        r.eng.transpose(sp.buf[0:HF, 0:P], n["stab_in"][:, :], ident[:, :]).then_inc(sp.full, 1)
    part.step("tensor", at + 0.1, turn_stab, [sp])

    def over_tokens(r):
        r.ready(sp)
        r.eng.tensor_reduce(n["stab_d"][:, HF:HF + 1], sp.buf[0:HF, 0:P], AX.X, ALU.max).then_inc(s[1].full, 1)
        r.ready(s[1])
        r.eng.sem_inc(sp.free, 1)
        r.eng.tensor_scalar(n["stab_d"][:, 0:HF], ident[0:HF, 0:HF], n["stab_d"][:, HF:HF + 1], None, ALU.mult)\
            .then_inc(s[2].full, 1)
    part.step("vector", at + 0.2, over_tokens)

    def to_all(r):
        r.ready(s[2])
        r.claim(sp2)
        r.eng.matmul(sp2.buf[:, 0:HF], n["ones16"], n["stab_d"][:, 0:HF], start=True, stop=True)\
            .then_inc(sp2.full, 1)
    part.step("tensor", at + 0.3, to_all, [sp2])

    def make_shift(r):
        r.ready(sp2)
        r.ready(dg)
        r.claim(u["shift"])
        r.eng.tensor_tensor(n["shift"].buf[:, :, :], n["diag"].buf[:, :, :],
                            sp2.buf[:, 0:HF].unsqueeze(1).to_broadcast([P, TPB, HF]), ALU.add)\
            .then_inc(u["shift"].full, 1)
        r.ready(u["shift"])
        r.eng.sem_inc(sp2.free, 1)
        r.eng.sem_inc(dg.free, 1)
    part.step("vector", at + 0.4, make_shift)

    for t in range(TPB):
        at = 7 + 0.6 * t
        kp, ex = part.use(n["kp"][t % 2]), part.use(n["kpx"][t % 2])

        def take_off(r, t=t, kp=kp, ex=ex):
            if t == 0:
                r.ready(u["shift"])
            r.claim(kp)
            r.eng.tensor_tensor(kp.buf[:, :].rearrange("p (h j) -> p h j", h=HF),
                                n["dd"].buf[:, t, :].rearrange("p (h j) -> p h j", h=HF),
                                spread(n["shift"].buf[:, t, :], JF), ALU.subtract).then_inc(ex.full, 1)

        def exps(r, kp=kp, ex=ex):
            r.ready(ex)
            r.eng.activation(kp.buf[:, :], kp.buf[:, :], ACT.Exp).then_inc(ex.free, 1)

        def plus_eps(r, t=t, kp=kp, ex=ex):
            r.eng.wait_ge(ex.free, r.nth(ex) + 2)
            if t == TPB - 1:
                r.eng.sem_inc(u["dd"].free, 1)
                r.eng.sem_inc(u["shift"].free, 1)
            r.eng.tensor_scalar(kp.buf[:, :], kp.buf[:, :], RATIO, EPS_FEAT, ALU.mult, ALU.add)\
                .then_inc(kp.full, 1)

        def sum_keys(r, t=t, kp=kp):
            r.ready(kp)
            if t == 0:
                r.ready(u["vext"])
                r.claim(u["kv_ps"])
            for f in range(FT):
                last = r.eng.matmul(n["kv_ps"].buf[:, f, :], kp.buf[:, f * P:(f + 1) * P],
                                    n["vext"].buf[:, t, f, :], start=(t == 0 and f == 0),
                                    stop=(t == TPB - 1), skip_group_check=True)
            last.then_inc(kp.free, 1)

        part.step("gpsimd", at, take_off)
        part.step("scalar", at + 0.1, exps)
        part.step("vector", at + 0.2, plus_eps)
        part.step("tensor", at + 0.3, sum_keys)

    last_kp = kp

    def keep_kv(r):
        r.eng.wait_ge(last_kp.free, r.nth(last_kp) + 2)
        r.eng.sem_inc(u["vext"].free, 1)
        r.claim(u["kv"])
        r.eng.tensor_tensor(n["kv"].buf[:, :, :], n["kv_ps"].buf[:, :, :],
                            n["vmask"][:, :].unsqueeze(1).to_broadcast([P, FT, 18]), ALU.mult)\
            .then_inc(u["kv"].full, 1)
        r.ready(u["kv"])
        r.eng.sem_inc(u["kv_ps"].free, 1)
    part.step("vector", 12, keep_kv)

    qt, q2, qg = side(6.5, "wqT", 0, "q")
    dq = part.use(n["diag"])

    def keep_diag_q(r):
        r.ready(qg)
        r.eng.sem_inc(q2.free, 1)
        r.claim(dq)
        r.eng.activation(n["diag"].buf[:, :, :], n["small"].buf[:, 0:P].rearrange("p (t h) -> p t h", t=TPB),
                         ACT.Copy).then_inc(dq.full, 1)
        r.ready(dq)
        r.eng.sem_inc(qg.free, 1)
    part.step("scalar", 7.15, keep_diag_q)

    for t in range(TPB):
        ps, at = part.ring(), 12.1 + 0.6 * t
        qd, qx, mx, sbt = part.use(n["qd"][t % 2]), part.use(n["qe"][t % 2]), part.use(n["qmax"]), part.use(n["qsub"])
        tp, qT, op = part.ring(), part.use(n["qpT"][t % 2]), part.use(n["small"])
        od = part.use(n["oden"])
        if t % 4 == 0:
            o1 = part.use(n["o1"])
        ochain = [part.use(n["ochain"]) for _ in range(2)]

        def features(r, t=t, ps=ps):
            if t == 0:
                r.ready(qt)
            r.claim(ps)
            for c in range(2):
                last = r.eng.matmul(ps.buf[:, c * 512:(c + 1) * 512], n["kT"].buf[:, t * P:(t + 1) * P],
                                    n["proj"][:, c * 512:(c + 1) * 512], start=True, stop=True)
            last.then_inc(ps.full, 1)
        part.step("tensor", at, features, [ps])

        def stabilise(r, t=t, ps=ps, qd=qd, mx=mx, sbt=sbt):
            v = r.eng
            r.ready(ps)
            if t == 0:
                r.ready(dq)
            if t == TPB - 1:
                v.sem_inc(qt.free, 1)
            view = ps.buf[:, :].rearrange("p (h j) -> p h j", h=HF)
            v.tensor_reduce(n["qmax"].buf[:, :], view, AX.X, ALU.max).then_inc(mx.full, 1)
            r.ready(mx)
            v.tensor_tensor(n["qsub"].buf[:, :], n["qmax"].buf[:, :], n["diag"].buf[:, t, :], ALU.add)\
                .then_inc(sbt.full, 1)
            r.ready(sbt)
            if t == TPB - 1:
                v.sem_inc(dq.free, 1)
            r.claim(qd)
            v.tensor_tensor(qd.buf[:, :].rearrange("p (h j) -> p h j", h=HF), view,
                            spread(n["qsub"].buf[:, :], JF), ALU.subtract).then_inc(qd.full, 1)
            r.ready(qd)
            v.sem_inc(ps.free, 1)
        part.step("vector", at + 0.1, stabilise)

        def exps(r, qd=qd, qx=qx):
            r.ready(qd)
            r.eng.activation(qd.buf[:, :], qd.buf[:, :], ACT.Exp).then_inc(qx.full, 1)
        part.step("scalar", at + 0.2, exps)

        def turn(r, qd=qd, qx=qx, tp=tp):
            r.ready(qx)
            r.claim(tp)
            for f in range(FT):
                last = r.eng.transpose(tp.buf[:, f * P:(f + 1) * P], qd.buf[:, f * P:(f + 1) * P], ident[:, :])
            last.then_inc(tp.full, 1)
        part.step("tensor", at + 0.3, turn, [tp])

        def plus_eps(r, qd=qd, tp=tp, qT=qT):
            r.ready(tp)
            r.eng.sem_inc(qd.free, 1)
            r.claim(qT)
            r.eng.activation(qT.buf[:, :, :], tp.buf[:, :].rearrange("p (f q) -> p f q", f=FT), ACT.Identity,
                             bias=n["eps"][:, :], scale=RATIO).then_inc(qT.full, 1)
            r.ready(qT)
            r.eng.sem_inc(tp.free, 1)
        part.step("scalar", at + 0.4, plus_eps)

        def weigh(r, t=t, qT=qT, op=op):
            if t == 0:
                r.ready(u["kv"])
            r.ready(qT)
            r.claim(op)
            for f in range(FT):
                last = r.eng.matmul(n["small"].buf[:, f * 18:(f + 1) * 18], qT.buf[:, f, :], n["kv"].buf[:, f, :],
                                    start=True, stop=True)
            last.then_inc(op.full, 1)
        part.step("tensor", at + 0.5, weigh)

        def divide(r, t=t, qT=qT, op=op, od=od, o1=o1, ochain=ochain):
            v, link = r.eng, Links(r, ochain)
            r.ready(op)
            v.sem_inc(qT.free, 1)
            if t == TPB - 1:
                v.sem_inc(u["kv"].free, 1)
            got = n["small"].buf[:, 0:FT * 18].rearrange("p (f k) -> p f k", f=FT)
            link(v.tensor_scalar(n["oden"].buf[:, :, :], got[:, :, 16:18], EPS_DEN, None, ALU.max))
            link(v.reciprocal(n["oden"].buf[:, :, :], n["oden"].buf[:, :, :]))
            if t % 4 == 0:
                r.claim(o1)
            v.tensor_tensor(n["o1"].buf[:, t % 4, :].rearrange("p (f h k) -> p f h k", f=FT, h=2),
                            got[:, :, 0:16].rearrange("p f (h k) -> p f h k", h=2),
                            spread(n["oden"].buf[:, :, :], HD), ALU.mult).then_inc(op.free, 1)
            if t % 4 == 3:
                v.wait_ge(op.free, r.nth(op) + 2)
                v.sem_inc(o1.full, 1)
        part.step("vector", at + 0.6, divide)

        if t % 4 == 3:
            t1, oT, t2 = part.ring(), part.use(n["o1T"]), part.ring()

            def turn_o(r, o1=o1, t1=t1):
                r.ready(o1)
                r.claim(t1)
                for k in range(4):
                    last = r.eng.transpose(t1.buf[:, k * P:(k + 1) * P], n["o1"].buf[:, k, :], ident[:, :])
                last.then_inc(t1.full, 1)
            part.step("tensor", at + 0.7, turn_o, [t1])

            def keep_oT(r, o1=o1, t1=t1, oT=oT):
                r.ready(t1)
                r.eng.sem_inc(o1.free, 1)
                r.claim(oT)
                r.eng.activation(n["o1T"].buf[:, :], t1.buf[:, 0:512], ACT.Copy).then_inc(oT.full, 1)
                r.ready(oT)
                r.eng.sem_inc(t1.free, 1)
            part.step("scalar", at + 0.75, keep_oT)

            def project(r, oT=oT, t2=t2):
                r.ready(oT)
                r.claim(t2)
                for k in range(4):
                    r.eng.matmul(t2.buf[:, k * P:(k + 1) * P], n["ones"][:, :], n["bo"][:, :], start=True, stop=False)
                    last = r.eng.matmul(t2.buf[:, k * P:(k + 1) * P], n["o1T"].buf[:, k * P:(k + 1) * P],
                                        n["woT"][:, :], start=False, stop=True)
                last.then_inc(t2.full, 1)
            part.step("tensor", at + 0.8, project, [t2])

            mx2 = part.use(n["attn"])

            def keep_out(r, oT=oT, t2=t2, mx2=mx2):
                r.ready(t2)
                r.eng.sem_inc(oT.free, 1)
                r.claim(mx2)
                r.eng.activation(n["attn"].buf[:, :], t2.buf[:, 0:512], ACT.Copy).then_inc(mx2.full, 1)
                r.ready(mx2)
                r.eng.sem_inc(t2.free, 1)
            part.step("scalar", at + 0.85, keep_out)

            def add(r, t=t, mx2=mx2):
                r.ready_apart(mx2, n["tally"])
                xt = x[:, bass.ds(r.i * TPB + (t - 3), 4), :].rearrange("p t d -> p (t d)")
                r.eng.tensor_tensor(xt, xt, n["attn"].buf[:, :], ALU.add).then_inc(mx2.free, 1)
                r.eng.wait_ge(mx2.free, r.nth(mx2) + 2)
            part.step("gpsimd", at + 0.9, add)


def experts(part, blk, n):
    (xnT, x, w, ident) = (n[k] for k in ("xnT", "x", "w", "ident"))
    for blkn in range(2):
        for e in range(EM + 1):
            at = 9 * blkn + e + 0.05
            hT = part.use(n["hT"][e % 2])
            hps = [part.ring() for _ in range(2)]

            def hidden(r, e=e, blkn=blkn, k=0, ps=None):
                r.claim(ps)
                for c in range(2):
                    last = r.eng.matmul(ps.buf[:, c * 512:(c + 1) * 512],
                                        n["w1"][:, e, (2 * k + c) * P:(2 * k + c + 1) * P],
                                        xnT[:, bass.ds(r.i * T + blkn * 512, 512)], start=True, stop=True)
                last.then_inc(ps.full, 1)

            def gelu(r, e=e, k=0, ps=None, hT=hT):
                r.ready(ps)
                if k == 0:
                    r.claim(hT)
                for c in range(2):
                    last = r.eng.activation(hT.buf[:, 2 * k + c, :], ps.buf[:, c * 512:(c + 1) * 512], ACT.Gelu,
                                            bias=n["b1"][:, e, 2 * k + c:2 * k + c + 1])
                last.then_inc(ps.free, 1)
                if k == 1:
                    r.eng.wait_ge(ps.free, r.nth(ps) + 2)
                    r.eng.sem_inc(hT.full, 1)
            for k in range(2):
                part.step("tensor", at + 0.2 * k, lambda r, f=hidden, k=k, ps=hps[k]: f(r, k=k, ps=ps), [hps[k]])
                part.step("scalar", at + 0.2 * k + 0.05, lambda r, f=gelu, k=k, ps=hps[k]: f(r, k=k, ps=ps))

            ops, mx = part.ring(), part.use(n["mixed"][e % 2])

            def output(r, e=e, hT=hT, ops=ops):
                r.ready(hT)
                r.claim(ops)
                for t in range(4):
                    for k in range(HT):
                        last = r.eng.matmul(ops.buf[:, t * P:(t + 1) * P], hT.buf[:, k, t * P:(t + 1) * P],
                                            n["w2"][:, e, k, :], start=(k == 0), stop=(k == HT - 1))
                last.then_inc(ops.full, 1)
            part.step("tensor", at + 1.1, output, [ops])

            def combine(r, e=e, blkn=blkn, hT=hT, ops=ops, mx=mx):
                r.ready(ops)
                r.eng.sem_inc(hT.free, 1)
                r.claim(mx)
                weights = w["combine"][:, bass.ds(r.i * TPB + 4 * blkn, 4), e]
                r.eng.tensor_tensor(mx.buf[:, :, :], ops.buf[:, 0:512].rearrange("p (t d) -> p t d", t=4),
                                    spread(weights, D), ALU.mult).then_inc(mx.full, 1)
                r.ready(mx)
                r.eng.sem_inc(ops.free, 1)
            part.step("vector", at + 1.2, combine)

            def add(r, blkn=blkn, mx=mx):
                r.ready_apart(mx, n["tally"])
                xt = x[:, bass.ds(r.i * TPB + 4 * blkn, 4), :]
                r.eng.tensor_tensor(xt, xt, mx.buf[:, :, :], ALU.add).then_inc(mx.free, 1)
                r.eng.wait_ge(mx.free, r.nth(mx) + 2)
            part.step("gpsimd", at + 1.3, add)

        at = 9 * blkn + 0.5
        cps, cT, bps = part.ring(), part.use(n["cT"]), part.ring()

        def turn(r, blkn=blkn, cps=cps):
            r.claim(cps)
            for t in range(4):
                last = r.eng.transpose(cps.buf[0:EM + 1, t * P:(t + 1) * P], n["cmb"].buf[:, t, :], ident[:, :])
            last.then_inc(cps.full, 1)
        cm = part.use(n["cmb"])

        def copy_combine(r, blkn=blkn, cm=cm):
            r.claim(cm)
            r.eng.tensor_copy(n["cmb"].buf[:, :, :], w["combine"][:, bass.ds(r.i * TPB + 4 * blkn, 4), :])\
                .then_inc(cm.full, 1)
        part.step("gpsimd", at - 0.01, copy_combine)
        part.step("tensor", at, lambda r, f=turn, cm=cm: (r.ready(cm), f(r)), [cps])

        def keep(r, cps=cps, cT=cT, cm=cm):
            r.ready(cps)
            r.eng.sem_inc(cm.free, 1)
            r.claim(cT)
            r.eng.activation(n["cT"].buf[:, :], cps.buf[0:EM + 1, 0:512], ACT.Copy).then_inc(cT.full, 1)
            r.ready(cT)
            r.eng.sem_inc(cps.free, 1)
        part.step("scalar", at + 0.01, keep)

        def biases(r, cT=cT, bps=bps):
            r.ready(cT)
            r.claim(bps)
            for t in range(4):
                last = r.eng.matmul(bps.buf[:, t * P:(t + 1) * P], n["cT"].buf[:, t * P:(t + 1) * P], n["b2"][:, :],
                                    start=True, stop=True)
            last.then_inc(bps.full, 1)
        part.step("tensor", at + 0.02, biases, [bps])
        bb = part.use(n["biased"])

        def keep_biases(r, cT=cT, bps=bps, bb=bb):
            r.ready(bps)
            r.eng.sem_inc(cT.free, 1)
            r.claim(bb)
            r.eng.activation(n["biased"].buf[:, :, :], bps.buf[:, 0:512].rearrange("p (t d) -> p t d", t=4), ACT.Copy)\
                .then_inc(bb.full, 1)
            r.ready(bb)
            r.eng.sem_inc(bps.free, 1)
        part.step("scalar", at + 0.03, keep_biases)

        def add(r, blkn=blkn, bb=bb):
            r.ready_apart(bb, n["tally"])
            xt = x[:, bass.ds(r.i * TPB + 4 * blkn, 4), :]
            r.eng.tensor_tensor(xt, xt, n["biased"].buf[:, :, :], ALU.add).then_inc(bb.free, 1)
            r.eng.wait_ge(bb.free, r.nth(bb) + 2)
        part.step("gpsimd", at + 0.04, add)


def build(nc, a):
    with ExitStack() as whole:
        def keep(name, shape, dt=F32):
            return whole.enter_context(nc.sbuf_tensor(name, shape, dt))

        x = keep("x", [P, NT, D])
        xnT = keep("xnT", [P, B * T])
        ident = keep("ident", [P, P])
        st = {"bn": keep("bn", [P, NT, 6])} | {
            k: keep(f"ln_{k}", [P, NT]) for k in ("mean", "rstd", "va", "t1", "y")}
        order = keep("order", [P, 8])
        with ExitStack() as l0:
            def keep0(name, shape, dt=F32):
                return l0.enter_context(nc.sbuf_tensor(name, shape, dt))
            w = {
                "gate": keep0("gate", [P, NT, 2 * HS * ES]),
                "ks": keep0("ks", [P, 2, B * T], BF16),
                "split": keep0("split", [P, 4]),
                "v32": keep0("v32", [P, NT, 32]),
                "qk": keep0("qk", [P, HS, P]),
                "o_all": keep0("o_all", [P, NT, H0, HD + 1]),
            }
            prepare0(nc, a, x, xnT, ident, st, order, w)
            main0(nc, a, x, xnT, ident, w)
            close0(nc, a, x, ident, w)

        with ExitStack() as l1:
            w = {"combine": l1.enter_context(nc.sbuf_tensor("combine", [P, NT, EM + 1], F32))}
            prepare1(nc, a, x, xnT, ident, st, order, w)
            main1(nc, a, x, xnT, ident, w)
        with nc.semaphore("stored") as stored, nc.Block() as block:
            @block.sync
            def _(eng):
                eng.dma_start(a["out"].rearrange("(t p) d -> p t d", p=P), x[:, :, :]).then_inc(stored, 16)
                eng.wait_ge(stored, 16)


def layout(i):
    f = np.float32
    get = {k: np.asarray(v) for k, v in i.items()}
    wq, bq = get["L0_attn_Wq"], get["L0_attn_bq"]
    wkv, bkv = get["L0_attn_Wkv"], get["L0_attn_bkv"]
    rows = SPLIT * HD
    wqs, bqs = np.zeros((H0 // 2, D, P), f), np.zeros((P, H0 // 2), f)
    wks, bks = np.zeros((D, 2, P), f), np.zeros((P, 2), f)
    for g in range(SPLIT):
        for hh in range(2):
            at = slice(hh * rows + g * HD, hh * rows + (g + 1) * HD)
            wks[:, hh, at] = wkv[:HD].T
            bks[at, hh] = bkv[:HD]
            for pair in range(H0 // 2):
                h = slice((2 * pair + hh) * HD, (2 * pair + hh + 1) * HD)
                wqs[pair][:, at] = wq[h].T
                bqs[at, pair] = bq[h]
    for hh in range(2):
        bks[96 + 3 * hh:99 + 3 * hh, hh] = 1
    split = np.zeros((P, 4), f)
    for col, classes in ((0, (0, 0, 0, 1, 1, 2)), (2, (0, 1, 2, 0, 1, 0))):
        for hh in range(2):
            for g, c in enumerate(classes):
                at = slice(hh * rows + g * HD, hh * rows + (g + 1) * HD)
                split[at, col], split[at, col + 1] = -(c >= 1), -(c == 2)
    proj, half, vmask = np.zeros((P, HF * JF), f), np.zeros((P, HF), f), np.zeros((P, 18), f)
    for h in range(HF):
        proj[h * HD:(h + 1) * HD, h * JF:(h + 1) * JF] = get["L1_attn_proj"][h].T
        half[h * HD:(h + 1) * HD, h] = 0.5
    for hh in range(2):
        vmask[hh * JF:(hh + 1) * JF, hh * HD:(hh + 1) * HD] = 1
        vmask[hh * JF:(hh + 1) * JF, 16 + hh] = 1
    selv = np.concatenate([get["L0_ffn_sel_v_w"].T, get["L0_ffn_sel_o_w"].T, wkv[HD:].T,
                           np.zeros((D, 32 - HD), f)], axis=1)
    bv = np.concatenate([bkv[HD:], np.ones(1, f), np.zeros(32 - HD - 1, f)])
    return {
        "x": get["L0_attn_x"].reshape(B * T, D),
        "q_w": get["L0_ffn_q_w"], "k_w": get["L0_ffn_k_w"],
        "v_w": get["L0_ffn_v_w"], "o_w": get["L0_ffn_o_w"],
        "selv": selv, "wk": wks, "bk": bks, "bv": bv, "wq": wqs, "split": split,
        "route": get["L0_ffn_route_scale"], "order": np.arange(8, 0, -1).astype(f),
        "wo": get["L0_attn_Wo"].T, "bo": get["L0_attn_bo"],
        "bq": bqs,
        "gate_w": get["L1_ffn_gate_w"], "gate_b": get["L1_ffn_gate_b"],
        "wqT": get["L1_attn_Wq"].T, "wkT": get["L1_attn_Wk"].T, "wvT": get["L1_attn_Wv"].T,
        "woT": get["L1_attn_Wo"].T, "bqk": np.stack([get["L1_attn_bq"], get["L1_attn_bk"]], axis=1),
        "bv1": get["L1_attn_bv"], "bo1": get["L1_attn_bo"], "proj": proj, "half": half, "vmask": vmask,
        "w1": get["L1_ffn_w1"], "ws1": get["L1_ffn_ws1"],
        "w2": np.concatenate([get["L1_ffn_w2"], get["L1_ffn_ws2"][None]]),
        "b1": np.concatenate([get["L1_ffn_b1"], get["L1_ffn_bs1"][None]]),
        "b2": np.concatenate([get["L1_ffn_b2"], get["L1_ffn_bs2"][None]]),
    }


def kernel(**inputs):
    import concourse.bacc as _bacc
    from concourse.bass_utils import run_bass_kernel_spmd as _run

    nc = _bacc.Bacc("TRN2", target_bir_lowering=False, num_devices=1)
    arrays = {f"in_{k}": np.ascontiguousarray(v) for k, v in layout(inputs).items()}
    a = {k[3:]: nc.dram_tensor(k, v.shape, mybir.dt.from_np(v.dtype), kind="ExternalInput").ap()
         for k, v in arrays.items()}
    a["out"] = nc.dram_tensor("out", (B * T, D), F32, kind="ExternalOutput").ap()
    build(nc, a)
    return _run(nc, [arrays], core_ids=[0]).results[0]["out"].reshape(B, T, D)
```

```python
from contextlib import ExitStack

import numpy as np

import concourse.bass as bass
from concourse import mybir

ALU = mybir.AluOpType
ACT = mybir.ActivationFunctionType
AX = mybir.AxisListType
F32 = mybir.dt.float32
BF16 = mybir.dt.bfloat16
F32R = mybir.dt.float32r

P = 128
B, T, D = 4, 1024, 128
NT = B * T // P
TPB = T // P
H0, HD = 16, 8
SPLIT = 6
HS, ES, PS = 8, 8, 128
SW_SCALE = PS ** -0.5
HF, JF = 16, 64
FT = HF * JF // P
DN = float(HD) ** -0.25
RATIO = float(JF) ** -0.5
EPS_FEAT, EPS_DEN, LN_EPS = 1e-4, 1e-2, 1e-5
EM, HID = 8, 512
HT = HID // P
ROUNDS = NT
ROUNDS1 = B


class Slot:

    def __init__(self, ctx, nc, name, buf=None, step=1):
        self.name, self.buf, self.step = name, buf, step
        self.full = ctx.enter_context(nc.semaphore(f"full_{name}"))
        self.free = ctx.enter_context(nc.semaphore(f"free_{name}"))
        self.start, self.uses = {}, {}


class Use:

    def __init__(self, slot=None, nth=None):
        self.slot, self.nth = slot, nth

    @property
    def buf(self):
        return self.slot.buf

    @property
    def full(self):
        return self.slot.full

    @property
    def free(self):
        return self.slot.free


class Part:

    def __init__(self, name, rounds=1, base=0):
        self.name, self.rounds, self.base, self.steps, self.count = name, rounds, base, [], {}

    def use(self, slot):
        n = self.count.get(slot, 0)
        self.count[slot] = n + 1
        return Use(slot, n)

    def ring(self):
        return Use()

    def chain(self, slot, n):
        return [self.use(slot) for _ in range(n)]

    def step(self, engine, tick, what, rings=()):
        self.steps.append((tick, len(self.steps), engine, what, rings))

    def settle(self, ring_slots):
        self.steps.sort(key=lambda s: (s[0], s[1]))
        n = 0
        for _, _, engine, _, rings in self.steps:
            for u in rings:
                got = self.use(ring_slots[n % len(ring_slots)])
                u.slot, u.nth = got.slot, got.nth
                n += 1


class Run:

    def __init__(self, eng, part, starts, i):
        self.eng, self.part, self.starts, self.i = eng, part, starts, i

    def nth(self, u):
        per = self.part.count[u.slot]
        return self.i * per + (self.starts.get(u.slot, 0) + u.nth)

    def claim(self, u):
        self.eng.wait_ge(u.free, self.nth(u) + 1)

    def ready(self, u):
        self.eng.wait_ge(u.full, (self.nth(u) + 1) * u.slot.step)

    def ready_apart(self, u, tally):
        self.ready(u)
        self.eng.sem_inc(tally.full, 1)

    def all_freed(self, slot):
        self.eng.wait_ge(slot.free, self.starts[slot] + 1)


class Links:

    def __init__(self, run, uses):
        self.run, self.uses, self.at = run, uses, 0

    def __call__(self, ins):
        u = self.uses[self.at]
        self.at += 1
        ins.then_inc(u.full, 1)
        self.run.ready(u)


def run_block(nc, parts, slots, ring_slots=()):
    starts, total = {}, {}
    for part in parts:
        part.settle(ring_slots)
        starts[part] = dict(total)
        for s, n in part.count.items():
            total[s] = total.get(s, 0) + n * part.rounds
    with nc.Block() as block:
        def program(name):
            def emit(eng):
                if name == "sync":
                    for s in slots:
                        eng.sem_inc(s.free, 1)
                for part in parts:
                    mine = [s for s in part.steps if s[2] == name]
                    if not mine:
                        continue
                    if part.rounds == 1:
                        r = Run(eng, part, starts[part], 0)
                        for s in mine:
                            s[3](r)
                    else:
                        with eng.Fori(0, part.rounds) as i:
                            r = Run(eng, part, starts[part], i)
                            for s in mine:
                                s[3](r)
            return emit

        block.sync(program("sync"))
        block.gpsimd(program("gpsimd"))
        block.scalar(program("scalar"))
        block.tensor(program("tensor"))
        block.vector(program("vector"))
    with nc.Block() as block:
        @block.gpsimd
        def _(eng):
            for s in slots:
                eng.sem_clear(s.full)
                eng.sem_clear(s.free)


def spread(ap, n):
    return ap.unsqueeze(len(ap.shape)).to_broadcast([*ap.shape, n])


class Block:

    def __init__(self, nc, ctx, name):
        self.nc, self.ctx, self.name, self.slots, self.parts, self.rings = nc, ctx, name, [], [], []

    def sbuf(self, name, shape, dt=F32):
        return self.ctx.enter_context(self.nc.sbuf_tensor(f"{self.name}_{name}", shape, dt))

    def psum(self, name, shape):
        return self.ctx.enter_context(self.nc.psum_tensor(f"{self.name}_{name}", shape, F32))

    def slot(self, name, shape=None, dt=F32, step=1):
        buf = self.sbuf(name, shape, dt) if shape else None
        return self.keep(Slot(self.ctx, self.nc, f"{self.name}_{name}", buf, step))

    def bank(self, name, shape):
        return self.keep(Slot(self.ctx, self.nc, f"{self.name}_{name}", self.psum(name, shape)))

    def keep(self, slot):
        self.slots.append(slot)
        return slot

    def ring(self, n, shape):
        self.rings = [self.bank(f"ring{k}", shape) for k in range(n)]

    def part(self, name, rounds=1, base=0):
        self.parts.append(Part(name, rounds, base))
        return self.parts[-1]

    def run(self):
        run_block(self.nc, self.parts, self.slots, self.rings)



def upper(eng, hi, src):
    return eng.tensor_copy(hi.bitcast(F32R), src)


def lower(eng, lo, src, hi):
    return eng.tensor_tensor(lo.bitcast(F32R), src, hi, ALU.subtract)


def matmul3(eng, out, w, x, start=True, stop=True):
    (wh, wl), (xh, xl) = ([t.bitcast(F32R) for t in pair] for pair in (w, x))
    eng.matmul(out, wh, xh, start=start, stop=False)
    eng.matmul(out, wh, xl, start=False, stop=False)
    return eng.matmul(out, wl, xh, start=False, stop=stop)


def layer_norm_stats(blk, part, tick, x, loaded):
    st = {"bn": blk.sbuf("bn", [P, NT, 6])} | {k: blk.sbuf(k, [P, NT]) for k in ("mean", "rstd", "va", "t1", "y")}
    chain = blk.slot("ln_chain")
    links = part.chain(chain, 7)
    sq, root, done = (part.use(blk.slot(f"ln_{k}")) for k in ("var", "root", "done"))
    bn, mean, rs, va, t1, y = (st[k] for k in ("bn", "mean", "rstd", "va", "t1", "y"))

    def moments(r):
        v, link = r.eng, Links(r, links)
        if loaded is not None:
            r.ready(loaded)
        for t in range(NT):
            last = v.bn_stats(bn[:, t, :], x[:, t, :])
        link(last)
        v.tensor_tensor(t1[:, :], bn[:, :, 1], bn[:, :, 4], ALU.subtract)
        v.tensor_tensor(va[:, :], bn[:, :, 2], bn[:, :, 5], ALU.add)
        link(v.tensor_tensor(mean[:, :], bn[:, :, 1], bn[:, :, 4], ALU.add))
        v.tensor_scalar(mean[:, :], mean[:, :], 0.5, None, ALU.mult)
        v.tensor_scalar(va[:, :], va[:, :], 1.0 / D, LN_EPS, ALU.mult, ALU.add)
        link(v.scalar_tensor_tensor(out=t1[:, :], in0=t1[:, :], scalar=0.25, in1=t1[:, :],
                                    op0=ALU.mult, op1=ALU.mult))
        v.tensor_tensor(va[:, :], va[:, :], t1[:, :], ALU.add).then_inc(sq.full, 1)

    def root_table(r):
        r.ready(sq)
        r.eng.activation(rs[:, :], va[:, :], ACT.Sqrt).then_inc(root.full, 1)

    def newton(r):
        v, link = r.eng, Links(r, links[3:])
        r.ready(root)
        link(v.reciprocal(y[:, :], rs[:, :]))
        link(v.tensor_tensor(t1[:, :], y[:, :], y[:, :], ALU.mult))
        link(v.scalar_tensor_tensor(out=t1[:, :], in0=t1[:, :], scalar=-0.5, in1=va[:, :],
                                    op0=ALU.mult, op1=ALU.mult))
        v.scalar_tensor_tensor(out=rs[:, :], in0=t1[:, :], scalar=1.5, in1=y[:, :],
                               op0=ALU.add, op1=ALU.mult).then_inc(done.full, 1)
        r.ready(done)
    part.step("vector", tick, moments)
    part.step("scalar", tick + 0.1, root_table)
    part.step("vector", tick + 0.2, newton)
    return st


TOP2_LINKS = 11


def top2(v, link, p, tmp, order):
    sel, c, q, m, first = (tmp[k] for k in ("sel", "c", "q", "m", "first"))
    g = m.shape[1]
    ob = order.unsqueeze(1).to_broadcast([P, g, 8])

    def choose(src, peak):
        link(v.tensor_reduce(peak, src, AX.X, ALU.max))
        link(v.tensor_tensor(c, src, spread(peak, 8), ALU.is_equal))
        link(v.tensor_tensor(c, c, ob, ALU.mult))
        link(v.tensor_reduce(m, c, AX.X, ALU.max))

    choose(p, first)
    link(v.tensor_tensor(sel, c, spread(m, 8), ALU.is_equal))
    link(v.scalar_tensor_tensor(out=q, in0=sel, scalar=-3.0e38, in1=p, op0=ALU.mult, op1=ALU.add))
    choose(q, tmp["second"])
    link(v.tensor_tensor(q, c, spread(m, 8), ALU.is_equal))
    return sel, q


def split_keys_or_queries(v, ready_hi, link, f, hi, minus_m1, minus_m2, out):
    ready_hi()
    link(v.scalar_tensor_tensor(out=f, in0=hi, scalar=minus_m1, in1=f, op0=ALU.mult, op1=ALU.add))
    link(v.tensor_copy(hi, f))
    return v.scalar_tensor_tensor(out=out, in0=hi, scalar=minus_m2, in1=f, op0=ALU.mult, op1=ALU.add)


def prepare0(nc, a, x, xnT, ident, order, w):
    with ExitStack() as ctx:
        blk = Block(nc, ctx, "p0")
        qw, kw = blk.sbuf("qw", [P, HS, D]), blk.sbuf("kw", [P, HS, D])
        selv, wk = blk.sbuf("selv", [D, 160]), blk.sbuf("wk", [D, 2, P])
        bv, bk = blk.sbuf("bv", [P, 32]), blk.sbuf("bk", [P, 2])
        route = blk.sbuf("route", [P, 1])
        loads_x, loads_w = blk.slot("loads_x", step=16), blk.slot("loads_w", step=16 * 9)
        eye = blk.slot("eye")
        xn = blk.slot("xn", [P, 4, D])
        xs = blk.slot("xs", [P, 4 * P])
        kf, kh = blk.slot("kf", [P, 2, 512]), blk.slot("kh", [P, 2, 512], BF16)
        v32, split, kept = blk.slot("v32"), blk.slot("split"), blk.slot("kept")
        turned = blk.bank("turned", [P, 512])
        logits = blk.bank("logits", [P, 4, 256])
        keys = blk.bank("keys", [P, 2, 512])
        qk_ps = blk.bank("qk", [P, HS, P])

        first = blk.part("first")
        ux, uw, ue, uq = first.use(loads_x), first.use(loads_w), first.use(eye), first.use(qk_ps)

        def load(r):
            e = r.eng
            e.dma_start(x[:, :, :], a["x"].rearrange("(t p) d -> p t d", p=P)).then_inc(ux.full, 16)
            for dst, src in (
                (qw[:, :, :], a["q_w"].rearrange("(h p) d -> p h d", p=PS)),
                (kw[:, :, :], a["k_w"].rearrange("(h p) d -> p h d", p=PS)),
                (selv[:, :], a["selv"]), (wk[:, :, :], a["wk"]),
                (bv[:, :], a["bv"].partition_broadcast(P)), (bk[:, :], a["bk"]),
                (route[:, :], a["route"].partition_broadcast(P)),
                (order[:, :], a["order"].partition_broadcast(P)), (w["split"][:, :], a["split"]),
            ):
                e.dma_start(dst, src).then_inc(uw.full, 16)
        first.step("sync", 0, load)

        def eye_zero(r):
            r.eng.memset(ident[:, :], 0.0).then_inc(ue.full, 1)
            r.ready(ue)
            r.eng.affine_select(out=ident[:, :], in_=ident[:, :], compare_op=ALU.not_equal, fill=1.0,
                                base=0, pattern=[[-1, P]], channel_multiplier=1).then_inc(ue2.full, 1)
        ue2 = first.use(eye)
        first.step("gpsimd", 0, eye_zero)
        st = layer_norm_stats(blk, first, 0, x, ux)

        def heads(r):
            r.ready(uw)
            r.ready(ue2)
            for h in range(HS):
                last = r.eng.matmul(qk_ps.buf[:, h, :], qw[:, h, :], kw[:, h, :], start=True, stop=True)
            last.then_inc(uq.full, 1)

        def keep_heads(r):
            r.ready(uq)
            r.eng.activation(w["qk"][:, :, :], qk_ps.buf[:, :, :], ACT.Copy).then_inc(uq.free, 1)
        first.step("tensor", 0, heads)
        first.step("scalar", 0.5, keep_heads)
        first.step("scalar", 0.6, lambda r: r.ready(uw))
        first.step("vector", 0.6, lambda r: r.ready(uw))

        tiles = blk.part("tiles", rounds=NT // 4)
        u = {n: tiles.use(s) for n, s in (
            ("xn", xn), ("xs", xs), ("kf", kf), ("kh", kh), ("v32", v32),
            ("turned", turned), ("logits", logits), ("keys", keys), ("kept", kept))}
        slinks = tiles.chain(split, 2)

        def normalise(r):
            v = r.eng
            r.claim(u["xn"])
            for j in range(4):
                last = v.tensor_scalar(xn.buf[:, j, :], x[:, r.i * 4 + j, :], st["mean"][:, bass.ds(r.i * 4 + j, 1)],
                                       st["rstd"][:, bass.ds(r.i * 4 + j, 1)], ALU.subtract, ALU.mult)
            last.then_inc(u["xn"].full, 1)
        tiles.step("vector", 0, normalise)

        def turn(r):
            r.ready(u["xn"])
            r.claim(u["turned"])
            for j in range(4):
                last = r.eng.transpose(turned.buf[:, j * P:(j + 1) * P], xn.buf[:, j, :], ident[:, :])
            last.then_inc(u["turned"].full, 1)
        tiles.step("tensor", 1, turn)

        def keep_turned(r):
            r.ready(u["turned"])
            r.claim(u["xs"])
            r.eng.activation(xs.buf[:, :], turned.buf[:, :], ACT.Copy).then_inc(u["xs"].full, 1)
        tiles.step("scalar", 2, keep_turned)

        def keep_xnT(r):
            r.ready(u["xs"])
            r.eng.tensor_copy(xnT[:, bass.ds(r.i * 512, 512)], xs.buf[:, :]).then_inc(u["kept"].full, 1)
        tiles.step("gpsimd", 3, keep_xnT)

        def project(r):
            r.ready(u["xs"])
            r.claim(u["logits"])
            for j in range(4):
                last = r.eng.matmul(logits.buf[:, j, 0:160], xs.buf[:, j * P:(j + 1) * P], selv[:, :],
                                    start=True, stop=True)
            last.then_inc(u["logits"].full, 1)
            r.claim(u["keys"])
            for hh in range(2):
                last = r.eng.matmul(keys.buf[:, hh, :], wk[:, hh, :], xs.buf[:, :], start=True, stop=True)
            last.then_inc(u["keys"].full, 1)
        tiles.step("tensor", 4, project)

        def keep_values(r):
            r.ready(u["logits"])
            r.eng.tensor_tensor(w["v32"][:, bass.ds(r.i * 4, 4), :], logits.buf[:, :, 128:160],
                                bv[:, :].unsqueeze(1).to_broadcast([P, 4, 32]), ALU.add)\
                .then_inc(u["v32"].full, 1)
            r.eng.sem_inc(u["xn"].free, 1)
        tiles.step("vector", 5, keep_values)

        def sigmoid_exps(r):
            r.ready(u["v32"])
            r.eng.sem_inc(u["turned"].free, 1)
            r.eng.activation(w["gate"][:, bass.ds(r.i * 4, 4), :], logits.buf[:, :, 0:128], ACT.Exp,
                             scale=-1.0).then_inc(u["logits"].free, 1)
            r.ready(u["keys"])
            r.claim(u["kf"])
            for hh in range(2):
                r.eng.activation(kf.buf[:, hh, :], keys.buf[:, hh, :], ACT.Identity, bias=bk[:, hh:hh + 1])
                last = r.eng.activation(kh.buf[:, hh, :], keys.buf[:, hh, :], ACT.Identity, bias=bk[:, hh:hh + 1])
            last.then_inc(u["kf"].full, 1)
        tiles.step("scalar", 6, sigmoid_exps)

        def split_keys(r):
            v, link = r.eng, Links(r, slinks)
            split_keys_or_queries(
                v, lambda: r.ready(u["kf"]), link, kf.buf[:, :, :], kh.buf[:, :, :], w["split"][:, 2:3],
                w["split"][:, 3:4], w["ks"][:, :, bass.ds(r.i * 512, 512)]).then_inc(u["kf"].free, 1)
            v.sem_inc(u["keys"].free, 1)
            r.ready(u["kept"])
            v.sem_inc(u["xs"].free, 1)
        tiles.step("vector", 7, split_keys)

        gates = blk.part("gates", rounds=4)
        tmp = {n: blk.sbuf(f"t2_{n}", [P, 128, 8]) for n in ("sel", "c", "q")} | {
            n: blk.sbuf(f"t2_{n}", [P, 128]) for n in ("m", "first", "second")}
        tmp = {k: (b[:, :, :] if len(b.shape) == 3 else b[:, :]) for k, b in tmp.items()}
        prob = blk.sbuf("t2_prob", [P, 128, 8])[:, :, :]
        glinks = gates.chain(blk.slot("gates"), 2 + TOP2_LINKS + 7)

        def route_gates(r):
            v, link = r.eng, Links(r, glinks)
            r.all_freed(logits)
            flat = w["gate"][:, bass.ds(r.i * 8, 8), :].rearrange("p t (g e) -> p (t g) e", e=8)
            link(v.tensor_scalar(prob, flat, 1.0, None, ALU.add))
            link(v.reciprocal(prob, prob))
            one, other = top2(v, link, prob, tmp, order[:, :])
            link(v.tensor_tensor(one, one, other, ALU.add))
            link(v.tensor_tensor(one, one, prob, ALU.mult))
            link(v.tensor_reduce(tmp["m"], one, AX.X, ALU.add))
            link(v.tensor_scalar(tmp["m"], tmp["m"], 1e-9, None, ALU.max))
            link(v.reciprocal(tmp["m"], tmp["m"]))
            link(v.tensor_scalar(tmp["m"], tmp["m"], route[:, 0:1], None, ALU.mult))
            link(v.tensor_tensor(flat, one, spread(tmp["m"], 8), ALU.mult))
        gates.step("vector", 0, route_gates)
        blk.run()


TICKS = {
    "queries": lambda t: 0.065,
    "split": lambda t: 0.4,
    "peaks": lambda t: [1, 2, 3, 4, 5, 6, 7, 8][t],
    "dpeaks": lambda t: 0,
    "values": lambda t: [1.5, 2.526, 3.551, 4.577, 5.602, 6.628, 7.653, 8.679][t],
    "dvalues": lambda t: 0.102,
    "cut": lambda t: 8.124,
    "turn_peaks": lambda t: 8.947,
    "hand": lambda t: 11,
    "scores": lambda t: [0.881, 1.264, 2.264, 3.264, 4.226, 5.006, 6.264, 7.264][t],
    "dlargest": lambda t: 0.02,
    "dsoftmax": lambda t: 0,
    "turn": lambda t: [1.079, 2.079, 3.079, 4.079, 5.079, 6.079, 7.079, 8.079][t],
    "dturn": lambda t: 0.012,
    "weigh": lambda t: [2.425, 3.425, 4.425, 5.425, 6.425, 7.425, 8.425, 9.425][t],
    "dweigh": lambda t: 0,
    "outputs": lambda t: [4.25, 4.55, 6.25, 6.55, 7.878, 8.25, 10.463, 10.55][t],
    "doutputs": lambda t: 0.001,
    "scoresT": lambda t: [0.631, 1.631, 2.631, 3.631, 4.631, 5.631, 6.631, 7.631][t],
    "dexps": lambda t: 0.001,
    "sums": lambda t: [1.651, 2.651, 3.651, 4.651, 5.651, 6.651, 7.651, 8.651][t],
    "dsums": lambda t: 0.01,
    "turn_sums": lambda t: 10.403,
    "y": lambda t: 8.93,
    "hand_x": lambda t: 10.458,
    "halve_wv": lambda t: 0.3,
    "halve_wo": lambda t: 1,
    "dsum": lambda t: 0.05,
}


def main0(nc, a, x, xnT, ident, w):
    with ExitStack() as ctx:
        blk = Block(nc, ctx, "m0")
        sb, slot = blk.sbuf, blk.slot
        bq = sb("bq", [P, H0 // 2])
        identb = sb("identb", [P, P], BF16)
        consts = slot("consts", step=16)
        eyeb = slot("eyeb")
        tally = slot("tally")
        wq, wqs = slot("wq", [D, P], step=16), slot("wqs", [D, 2, P])
        wraw = slot("wraw", [D, ES * PS], step=16)
        wvs = slot("wvs", [D, 2, ES * PS])
        wos = slot("wos", [PS, 2, ES * D])
        cut = {k: slot(f"cut_{k}") for k in ("wq", "wv", "wo", "x", "qk")}
        x_values, x_y = slot("x_values"), slot("x_y")
        xcur, xfin = slot("xcur", [D, 2, T]), slot("xfin", [D, 2, T])
        qf, qh = slot("qf", [P, T]), sb("qh", [P, T], BF16)
        qsplit = slot("qsplit")
        qnext, qcur = slot("qnext", [P, T], BF16), slot("qcur", [P, T], BF16)
        peaks = sb("peaks", [P, TPB, 2])
        mparts, mrest = slot("mparts", [P, TPB, 2, 3], BF16), sb("mrest", [P, TPB, 2])
        mchain, mrows = slot("mchain"), slot("mrows", [6, T], BF16)
        vnext, vcur = slot("vnext", [P, TPB, PS]), slot("vcur", [P, TPB, PS])
        qk, v32 = slot("qk", [D, 2, D]), slot("v32", [P, TPB, 32])
        yupper, yT = slot("yupper"), slot("yT", [D, 2, T])
        neg = [slot(f"neg{k}", [P, 1]) for k in range(2)]
        prob = [slot(f"prob{k}", [P, T]) for k in range(2)]
        den = sb("den", [P, TPB])
        probT = [slot(f"probT{k}", [P, TPB, 2 * P]) for k in range(2)]
        ctxT = [slot(f"ctxT{k}", [PS, 2, 2 * P]) for k in range(2)]
        cupper = slot("cupper")
        rden, go = slot("rden", [P, 2]), sb("go", [P, TPB, ES])
        expA = [slot(f"expA{k}", [P, T]) for k in range(2)]
        vprod, oprod = slot("vprod", [P, ES * P]), [slot(f"oprod{k}", [P, ES * P]) for k in range(2)]
        vchain, ochain = slot("vchain"), slot("ochain")
        sums = blk.bank("sums", [P, 512])
        ctx_ps = blk.bank("ctx", [P, 512])
        blk.ring(3, [P, T])

        at = {k: [f(t) for t in range(TPB)] for k, f in TICKS.items()}

        def of(r, n_is):
            n = r.i + (r.part.base + n_is)
            return n // HS, n % HS

        def both(buf, cols=slice(None)):
            return buf[:, 0, cols], buf[:, 1, cols]

        def halve(part, tick, raw, halves, mid, src):
            m = part.use(mid)
            hi, lo = both(halves.buf)

            def make_upper(r):
                if raw is not None:
                    r.ready(raw)
                r.claim(halves)
                upper(r.eng, hi, src(r)).then_inc(m.full, 1)
            part.step("vector", tick, make_upper)

            def make_lower(r):
                r.ready_apart(m, tally)
                lower(r.eng, lo, src(r), hi).then_inc(halves.full, 1)
                if raw is not None:
                    r.ready(halves)
                    r.eng.sem_inc(raw.free, 1)
            part.step("gpsimd", tick + 0.001, make_lower)

        def halve_sum(r, buf, link):
            for n in (4 * P, 2 * P):
                link(r.eng.tensor_tensor(buf[:, 0:n], buf[:, 0:n], buf[:, n:2 * n], ALU.add))

        def begin(part, ahead):
            u = {k: part.use(s) for k, s in (
                ("wq", wq), ("wqs", wqs), ("wraw", wraw), ("wvs", wvs), ("xcur", xcur), ("qf", qf), ("qnext", qnext),
                ("mparts", mparts), ("vnext", vnext), ("qk", qk), ("yT", yT), ("yupper", yupper))}
            yps = part.ring()
            split_links, m_links = part.chain(qsplit, 2), part.chain(mchain, 4)
            qps = part.ring()

            def load(r):
                b, h = of(r, ahead)
                r.claim(u["wq"])
                r.eng.dma_start(wq.buf[:, :], a["wq"][bass.ds(h, 1), :, :].rearrange("h d m -> (h d) m"))\
                    .then_inc(u["wq"].full, 16)
                r.claim(u["wraw"])
                r.eng.dma_start(wraw.buf[:, :].rearrange("d (e p) -> d e p", e=ES),
                                a["v_w"][bass.ds(h * ES, ES), :, :].rearrange("e d p -> d e p"))\
                    .then_inc(u["wraw"].full, 16)
            part.step("sync", 0, load)

            def sequence(r):
                b, _ = of(r, ahead)
                return xnT[:, bass.ds(b * T, T)]

            def head_qk(r):
                _, h = of(r, ahead)
                return w["qk"][:, bass.ds(h, 1), :].rearrange("d h e -> d (h e)")
            halve(part, 0.001, None, u["xcur"], cut["x"], sequence)
            halve(part, 0.003, u["wq"], u["wqs"], cut["wq"], lambda r: wq.buf[:, :])
            halve(part, at["halve_wv"][0], u["wraw"], u["wvs"], cut["wv"], lambda r: wraw.buf[:, :])
            halve(part, 0.301, None, u["qk"], cut["qk"], head_qk)

            def hand_x(r):
                r.claim(xf)
                r.ready(u["xcur"])
                for k in range(2):
                    last = r.eng.activation(xfin.buf[:, k, :].bitcast(F32R), xcur.buf[:, k, :], ACT.Copy)
                last.then_inc(xf.full, 1)
                r.ready(xf)
                r.ready(xread)
                r.ready(yread)
                r.eng.sem_inc(u["xcur"].free, 1)
            xf, xread, yread = part.use(xfin), part.use(x_values), part.use(x_y)
            part.step("scalar", at["hand_x"][0], hand_x)
            def make_y(r):
                r.ready(u["qk"])
                r.ready(u["xcur"])
                r.claim(yps)
                for c in range(2):
                    last = matmul3(r.eng, yps.buf[:, c * 512:(c + 1) * 512], both(qk.buf),
                                   both(xcur.buf, slice(c * 512, (c + 1) * 512)))
                last.then_inc(yps.full, 1)
            part.step("tensor", at["y"][0], make_y, [yps])

            def keep_y(r):
                r.ready(yps)
                r.eng.sem_inc(u["qk"].free, 1)
                r.eng.sem_inc(yread.full, 1)
                r.claim(u["yT"])
                r.eng.activation(yT.buf[:, 0, :].bitcast(F32R), yps.buf[:, :], ACT.Copy, scale=SW_SCALE)\
                    .then_inc(u["yupper"].full, 1)
            part.step("scalar", at["y"][0] + 0.01, keep_y)

            def halve_y(r):
                r.ready(u["yupper"])
                r.eng.scalar_tensor_tensor(out=yT.buf[:, 1, :].bitcast(F32R), in0=yps.buf[:, :], scalar=SW_SCALE,
                                           in1=yT.buf[:, 0, :], op0=ALU.mult, op1=ALU.subtract)\
                    .then_inc(u["yT"].full, 1)
                r.ready(u["yT"])
                r.eng.sem_inc(yps.free, 1)
            part.step("vector", at["y"][0] + 0.02, halve_y)

            def queries(r):
                r.ready(u["wqs"])
                r.ready(u["xcur"])
                r.claim(qps)
                for c in range(2):
                    last = matmul3(r.eng, qps.buf[:, c * 512:(c + 1) * 512], both(wqs.buf),
                                   both(xcur.buf, slice(c * 512, (c + 1) * 512)))
                last.then_inc(qps.full, 1)
            part.step("tensor", at["queries"][0], queries, [qps])

            def keep_queries(r):
                b, h = of(r, ahead)
                r.ready(qps)
                r.eng.sem_inc(u["wqs"].free, 1)
                r.claim(u["qf"])
                for out in (qf.buf, qh):
                    last = r.eng.activation(out[:, :], qps.buf[:, :], ACT.Identity, bias=bq[:, bass.ds(h, 1)],
                                            scale=HD ** -0.5)
                last.then_inc(qps.free, 1)
            part.step("scalar", at["queries"][0] + 0.01, keep_queries)

            def split_queries(r):
                v, link = r.eng, Links(r, split_links)

                def written():
                    v.wait_ge(qps.free, r.nth(qps) + 2)
                    r.claim(u["qnext"])
                split_keys_or_queries(v, written, link, qf.buf[:, :], qh[:, :], w["split"][:, 0:1],
                                      w["split"][:, 1:2], qnext.buf[:, :]).then_inc(u["qnext"].full, 1)
            part.step("vector", at["split"][0], split_queries)

            def free_qf(r):
                r.ready(u["qnext"])
                r.eng.sem_inc(u["qf"].free, 1)
            part.step("gpsimd", at["split"][0] + 0.01, free_qf)

            for t in range(TPB):
                for hh in range(2):
                    ps = part.ring()

                    def scores(r, t=t, hh=hh, ps=ps):
                        b, _ = of(r, ahead)
                        if t == 0 and hh == 0:
                            r.ready(u["qnext"])
                        r.claim(ps)
                        for c in range(2):
                            last = r.eng.matmul(ps.buf[:, c * 512:(c + 1) * 512],
                                                qnext.buf[:, t * P:(t + 1) * P],
                                                w["ks"][:, hh, bass.ds(b * T + c * 512, 512)],
                                                start=True, stop=True)
                        last.then_inc(ps.full, 1)
                    part.step("tensor", at["peaks"][t] + 0.1 * hh, scores, [ps])

                    def largest(r, t=t, hh=hh, ps=ps):
                        r.ready(ps)
                        r.eng.tensor_reduce(peaks[:, t, hh:hh + 1], ps.buf[:, :], AX.X, ALU.max)\
                            .then_inc(ps.free, 1)
                        if t == TPB - 1 and hh == 1:
                            r.eng.wait_ge(ps.free, r.nth(ps) + 2)
                    part.step("vector", at["peaks"][t] + 0.1 * hh + at["dpeaks"][0], largest)

                vps = part.ring()

                def values(r, t=t, vps=vps):
                    if t == 0:
                        r.ready(u["wvs"])
                        r.ready(u["xcur"])
                    r.claim(vps)
                    for c in range(2):
                        last = matmul3(r.eng, vps.buf[:, c * 512:(c + 1) * 512],
                                       both(xcur.buf, slice(t * P, (t + 1) * P)),
                                       both(wvs.buf, slice(c * 512, (c + 1) * 512)))
                    last.then_inc(vps.full, 1)
                part.step("tensor", at["values"][t], values, [vps])

                vp, links = part.use(vprod), part.chain(vchain, 2)

                def gate_values(r, t=t, vps=vps, vp=vp):
                    b, h = of(r, ahead)
                    r.ready(vps)
                    r.claim(vp)
                    gate = w["gate"][:, bass.ds(b * TPB + t, 1), bass.ds(h * ES, ES)]\
                        .rearrange("p o e -> p (o e)")
                    r.eng.tensor_tensor(vprod.buf[:, :].rearrange("p (e d) -> p e d", e=ES),
                                        vps.buf[:, :].rearrange("p (e d) -> p e d", e=ES),
                                        spread(gate, P), ALU.mult).then_inc(vp.full, 1)
                    if t == TPB - 1:
                        r.eng.sem_inc(u["wvs"].free, 1)
                        r.eng.sem_inc(xread.full, 1)
                    r.ready(vp)
                    r.eng.sem_inc(vps.free, 1)
                part.step("vector", at["values"][t] + at["dvalues"][0], gate_values)

                def sum_values(r, t=t, vp=vp, links=links):
                    r.ready(vp)
                    if t == 0:
                        r.claim(u["vnext"])
                    halve_sum(r, vprod.buf, Links(r, links))
                    r.eng.tensor_tensor(vnext.buf[:, t, :], vprod.buf[:, 0:P], vprod.buf[:, P:2 * P], ALU.add)\
                        .then_inc(vp.free, 1)
                    if t == TPB - 1:
                        r.eng.wait_ge(vp.free, r.nth(vp) + 2)
                        r.eng.sem_inc(u["vnext"].full, 1)
                part.step("gpsimd", at["values"][t] + at["dvalues"][0] + at["dsum"][0], sum_values)

            def cut_peaks(r):
                v, link = r.eng, Links(r, m_links)
                r.claim(u["mparts"])
                mp = mparts.buf
                link(v.tensor_scalar(mrest[:, :, :], peaks[:, :, :], -1.0, None, ALU.mult))
                link(v.tensor_copy(mp[:, :, :, 0], mrest[:, :, :]))
                link(v.tensor_tensor(mrest[:, :, :], mrest[:, :, :], mp[:, :, :, 0], ALU.subtract))
                link(v.tensor_copy(mp[:, :, :, 1], mrest[:, :, :]))
                v.tensor_tensor(mp[:, :, :, 2], mrest[:, :, :], mp[:, :, :, 1], ALU.subtract)\
                    .then_inc(u["mparts"].full, 1)
            part.step("vector", at["cut"][0], cut_peaks)
            mps = part.ring()

            def turn_peaks(r):
                r.ready(u["mparts"])
                r.claim(mps)
                rows = mps.buf[:, 0:512].bitcast(BF16)
                for t in range(TPB):
                    last = r.eng.transpose(rows[0:6, t * P:(t + 1) * P],
                                           mparts.buf[:, t, :, :].rearrange("p h c -> p (h c)"), identb[:, :])
                last.then_inc(mps.full, 1)
            part.step("tensor", at["turn_peaks"][0], turn_peaks, [mps])

            mr = part.use(mrows)

            def keep_peaks(r):
                r.ready(mps)
                r.eng.sem_inc(u["mparts"].free, 1)
                r.claim(mr)
                r.eng.activation(mrows.buf[:, :], mps.buf[0:6, 0:512].bitcast(BF16), ACT.Copy).then_inc(mr.full, 1)
                r.ready(mr)
                r.eng.sem_inc(mps.free, 1)
            part.step("scalar", at["turn_peaks"][0] + 0.01, keep_peaks)

            qc, vc = part.use(qcur), part.use(vcur)

            def hand_queries(r):
                r.claim(qc)
                r.eng.tensor_copy(qcur.buf[0:96, :], qnext.buf[0:96, :])
                r.ready(mr)
                r.eng.tensor_copy(qcur.buf[96:102, :], mrows.buf[:, :]).then_inc(qc.full, 1)
                r.ready(qc)
                r.eng.sem_inc(mr.free, 1)
                r.eng.sem_inc(u["qnext"].free, 1)
            part.step("vector", at["hand"][0], hand_queries)

            def hand_values(r):
                r.claim(vc)
                r.ready(u["vnext"])
                r.eng.activation(vcur.buf[:, :, :], vnext.buf[:, :, :], ACT.Copy).then_inc(vc.full, 1)
                r.ready(vc)
                r.eng.sem_inc(u["vnext"].free, 1)
            part.step("scalar", 11, hand_values)

        def finish(part):
            u = {k: part.use(s) for k, s in (
                ("wraw", wraw), ("wos", wos), ("v32", v32), ("sums", sums))}
            def load(r):
                _, h = of(r, 0)
                r.claim(u["wraw"])
                r.eng.dma_start(wraw.buf[:, :].rearrange("p (e d) -> p e d", e=ES),
                                a["o_w"][bass.ds(h * ES, ES), :, :].rearrange("e p d -> p e d"))\
                    .then_inc(u["wraw"].full, 16)
            part.step("sync", 0, load)

            def copies(r):
                b, h = of(r, 0)
                r.claim(u["v32"])
                r.eng.tensor_copy(v32.buf[:, :, :], w["v32"][:, bass.ds(b * TPB, TPB), :])\
                    .then_inc(u["v32"].full, 1)
            part.step("gpsimd", 0, copies)

            halve(part, at["halve_wo"][0], u["wraw"], u["wos"], cut["wo"], lambda r: wraw.buf[:, :])

            ctx_uses = []
            for t in range(TPB):
                ps, ng, pb = part.ring(), part.use(neg[t % 2]), part.use(prob[t % 2])

                def scores(r, t=t, ps=ps):
                    b, _ = of(r, 0)
                    if t == 0:
                        wait_handed(r, yT)
                        wait_handed(r, xfin)
                    r.claim(ps)
                    for c in range(2):
                        last = matmul3(r.eng, ps.buf[:, c * 512:(c + 1) * 512],
                                       both(yT.buf, slice(t * P, (t + 1) * P)),
                                       both(xfin.buf, slice(c * 512, (c + 1) * 512)))
                    last.then_inc(ps.full, 1)
                part.step("tensor", at["scores"][t], scores, [ps])

                def largest(r, t=t, ps=ps, ng=ng):
                    r.ready(ps)
                    r.claim(ng)
                    r.eng.tensor_reduce(ng.buf[:, :], ps.buf[:, :], AX.X, ALU.max, negate=True)\
                        .then_inc(ng.full, 1)
                part.step("vector", at["scores"][t] + at["dlargest"][0], largest)

                def softmax(r, t=t, ps=ps, ng=ng, pb=pb):
                    r.ready(ng)
                    r.claim(pb)
                    r.eng.activation(pb.buf[:, :], ps.buf[:, :], ACT.Exp, bias=ng.buf[:, :],
                                     accum_out=den[:, t:t + 1]).then_inc(pb.full, 1)
                    r.ready(pb)
                    r.eng.sem_inc(ps.free, 1)
                    r.eng.sem_inc(ng.free, 1)
                    if t == TPB - 1:
                        r.eng.sem_inc(yT.free, 1)
                        r.eng.sem_inc(xfin.free, 1)
                part.step("scalar", at["scores"][t] + at["dsoftmax"][0], softmax)

                tps = part.ring()
                if t % 2 == 0:
                    pT = part.use(probT[(t // 2) % 2])

                def turn(r, tps=tps, pb=pb):
                    r.ready(pb)
                    r.claim(tps)
                    for c in range(TPB):
                        last = r.eng.transpose(tps.buf[:, c * P:(c + 1) * P], pb.buf[:, c * P:(c + 1) * P],
                                               ident[:, :])
                    last.then_inc(tps.full, 1)
                part.step("tensor", at["turn"][t], turn, [tps])

                def keep_turned(r, t=t, tps=tps, pT=pT, pb=pb):
                    r.ready(tps)
                    r.eng.sem_inc(pb.free, 1)
                    if t % 2 == 0:
                        r.claim(pT)
                    ins = r.eng.activation(pT.buf[:, :, (t % 2) * P:(t % 2 + 1) * P],
                                           tps.buf[:, :].rearrange("p (c q) -> p c q", c=TPB), ACT.Copy)\
                        .then_inc(tps.free, 1)
                    if t % 2:
                        r.eng.wait_ge(tps.free, r.nth(tps) + 2)
                        r.eng.sem_inc(pT.full, 1)
                part.step("scalar", at["turn"][t] + at["dturn"][0], keep_turned)

                if t % 2:
                    g = t // 2
                    cp, ct = part.use(ctx_ps), part.use(ctxT[g % 2])
                    rd = part.use(rden)
                    cr = part.use(cupper)
                    ctx_uses.append((pT, cp, ct))

                    def weigh(r, g=g, pT=pT, cp=cp):
                        if g == 0:
                            wait_handed(r, vcur)
                        r.ready(pT)
                        r.claim(cp)
                        for k in range(TPB):
                            last = r.eng.matmul(cp.buf[:, 0:2 * P], vcur.buf[:, k, :], pT.buf[:, k, :],
                                                start=(k == 0), stop=(k == TPB - 1))
                        last.then_inc(cp.full, 1)
                    part.step("tensor", at["weigh"][t], weigh)

                    def keep_ctx(r, g=g, pT=pT, cp=cp, cr=cr, ct=ct):
                        r.ready(cp)
                        r.eng.sem_inc(pT.free, 1)
                        if g == TPB // 2 - 1:
                            r.eng.sem_inc(vcur.free, 1)
                        r.claim(ct)
                        r.eng.activation(ct.buf[:, 0, :].bitcast(F32R), cp.buf[:, 0:2 * P], ACT.Copy)\
                            .then_inc(cr.full, 1)
                    part.step("scalar", at["weigh"][t] + at["dweigh"][0], keep_ctx)

                    def halve_ctx(r, cp=cp, cr=cr, ct=ct):
                        r.ready(cr)
                        lower(r.eng, ct.buf[:, 1, :], cp.buf[:, 0:2 * P], ct.buf[:, 0, :]).then_inc(ct.full, 1)
                        r.ready(ct)
                        r.eng.sem_inc(cp.free, 1)
                    part.step("vector", at["weigh"][t] + at["dweigh"][0] + 0.001, halve_ctx)

                    def output_gates(r, g=g, rd=rd, pb=pb):
                        b, h = of(r, 0)
                        r.ready(pb)
                        r.eng.reciprocal(rden.buf[:, :], den[:, 2 * g:2 * g + 2]).then_inc(rd.full, 1)
                        r.ready(rd)
                        r.eng.tensor_tensor(go[:, 2 * g:2 * g + 2, :],
                                            w["gate"][:, bass.ds(b * TPB + 2 * g, 2), bass.ds((h + HS) * ES, ES)],
                                            spread(rden.buf[:, :], ES), ALU.mult).then_inc(rd.free, 1)
                        r.eng.wait_ge(rd.free, r.nth(rd) + 2)
                    part.step("vector", at["weigh"][t] + 0.05, output_gates)

                    for tt in (t - 1, t):
                        ops, pr, links = part.ring(), part.use(oprod[tt % 2]), part.chain(ochain, 3)

                        def outputs(r, tt=tt, ct=ct, ops=ops):
                            if tt == 0:
                                r.ready(u["wos"])
                            r.ready(ct)
                            r.claim(ops)
                            for c in range(2):
                                last = matmul3(r.eng, ops.buf[:, c * 512:(c + 1) * 512],
                                               both(ct.buf, slice((tt % 2) * P, (tt % 2 + 1) * P)),
                                               both(wos.buf, slice(c * 512, (c + 1) * 512)))
                            last.then_inc(ops.full, 1)
                        part.step("tensor", at["outputs"][tt], outputs, [ops])

                        def gate_outputs(r, tt=tt, ct=ct, ops=ops, pr=pr):
                            r.ready(ops)
                            if tt % 2:
                                r.eng.sem_inc(ct.free, 1)
                            if tt == TPB - 1:
                                r.eng.sem_inc(u["wos"].free, 1)
                            r.claim(pr)
                            r.eng.tensor_tensor(pr.buf[:, :].rearrange("p (e d) -> p e d", e=ES),
                                                ops.buf[:, :].rearrange("p (e d) -> p e d", e=ES),
                                                spread(go[:, tt, :], P), ALU.mult).then_inc(pr.full, 1)
                            r.ready(pr)
                            r.eng.sem_inc(ops.free, 1)
                        part.step("vector", at["outputs"][tt] + at["doutputs"][0], gate_outputs)

                        def sum_outputs(r, tt=tt, pr=pr, links=links):
                            b, _ = of(r, 0)
                            link = Links(r, links)
                            r.ready(pr)
                            halve_sum(r, pr.buf, link)
                            link(r.eng.tensor_tensor(pr.buf[:, 0:P], pr.buf[:, 0:P], pr.buf[:, P:2 * P], ALU.add))
                            r.eng.sem_inc(tally.full, 1)
                            xt = x[:, bass.ds(b * TPB + tt, 1), :].rearrange("p o d -> p (o d)")
                            r.eng.tensor_tensor(xt, xt, pr.buf[:, 0:P], ALU.add).then_inc(pr.free, 1)
                        part.step("gpsimd", at["outputs"][tt] + at["doutputs"][0] + at["dsum"][0], sum_outputs)

            for k in range(TPB):
                es = []
                for hh in range(2):
                    ps, e = part.ring(), part.use(expA[hh])
                    es.append(e)

                    def scoresT(r, k=k, hh=hh, ps=ps):
                        b, _ = of(r, 0)
                        if k == 0 and hh == 0:
                            wait_handed(r, qcur)
                        r.claim(ps)
                        for c in range(2):
                            last = r.eng.matmul(ps.buf[:, c * 512:(c + 1) * 512],
                                                w["ks"][:, hh, bass.ds(b * T + k * P, P)],
                                                qcur.buf[:, c * 512:(c + 1) * 512], start=True, stop=True)
                        last.then_inc(ps.full, 1)
                    part.step("tensor", at["scoresT"][k] + 0.2 * hh, scoresT, [ps])

                    def exps(r, k=k, hh=hh, ps=ps, e=e):
                        r.ready(ps)
                        if k == TPB - 1 and hh == 1:
                            r.eng.sem_inc(qcur.free, 1)
                        r.claim(e)
                        r.eng.activation(e.buf[:, :], ps.buf[:, :], ACT.Exp).then_inc(e.full, 1)
                        r.ready(e)
                        r.eng.sem_inc(ps.free, 1)
                    part.step("scalar", at["scoresT"][k] + 0.2 * hh + at["dexps"][0], exps)

                def sum_values(r, k=k, es=es):
                    if k == 0:
                        r.ready(u["v32"])
                        r.claim(u["sums"])
                    for e in es:
                        r.ready(e)
                    for hh in range(2):
                        for c in range(2):
                            j = 2 * hh + c
                            last = r.eng.matmul(sums.buf[32 * j:32 * j + 32, :], v32.buf[:, k, :],
                                                es[hh].buf[:, c * 512:(c + 1) * 512],
                                                start=(k == 0), stop=(k == TPB - 1))
                            if c == 1:
                                last.then_inc(es[hh].free, 1)
                part.step("tensor", at["sums"][k], sum_values)

            st = part.use(expA[1])
            sumsT = st.buf[:, 0:512]

            def keep_sums(r):
                r.claim(st)
                r.eng.sem_inc(u["v32"].free, 1)
                r.eng.activation(sumsT, sums.buf[:, :], ACT.Copy).then_inc(st.full, 1)
                r.ready(st)
                r.eng.sem_inc(u["sums"].free, 1)
            part.step("scalar", at["sums"][TPB - 1] + at["dsums"][0], keep_sums)
            sps = part.ring()

            def turn_sums(r):
                r.ready(st)
                r.claim(sps)
                for s in range(4):
                    last = r.eng.transpose(sps.buf[:, s * P:(s + 1) * P], sumsT[:, s * P:(s + 1) * P],
                                           ident[:, :])
                last.then_inc(sps.full, 1)
            part.step("tensor", at["turn_sums"][0], turn_sums, [sps])

            def keep_o(r):
                b, h = of(r, 0)
                r.ready(sps)
                r.eng.sem_inc(st.free, 1)
                v = sps.buf[:, 0:512].rearrange("p (s h c k) -> p h c s k", s=4, h=2, c=2)
                for hh in range(2):
                    for c in range(2):
                        ins = r.eng.activation(
                            w["o_all"][:, bass.ds(b * TPB + c * 4, 4), bass.ds(h * 2 + hh, 1), :]
                            .rearrange("p s o k -> p s (o k)"), v[:, hh, c, :, 0:HD + 1], ACT.Copy)
                ins.then_inc(sps.free, 1)
            part.step("scalar", at["turn_sums"][0] + 0.01, keep_o)

        def wait_handed(r, slot):
            r.eng.wait_ge(slot.full, r.i + (r.part.base + 1))

        first = blk.part("first")
        uc = first.use(consts)
        ub = [first.use(eyeb) for _ in range(2)]
        first.step("sync", -1, lambda r: r.eng.dma_start(bq[:, :], a["bq"]).then_inc(uc.full, 16))

        def eye_b(r):
            r.eng.memset(qcur.buf[96:128, :], 0.0)
            r.eng.tensor_copy(identb[:, :], ident[:, :]).then_inc(ub[0].full, 1)
        first.step("vector", -1, eye_b)

        def scale_bias(r):
            r.ready(uc)
            r.eng.tensor_scalar(bq[:, :], bq[:, :], HD ** -0.5, None, ALU.mult).then_inc(ub[1].full, 1)
        first.step("vector", -0.9, scale_bias)
        first.step("scalar", -1, lambda r: r.ready(ub[1]))
        first.step("tensor", -1, lambda r: r.ready(ub[0]))
        begin(first, 0)
        loop = blk.part("loop", rounds=ROUNDS - 1)
        begin(loop, 1)
        finish(loop)
        finish(blk.part("last", base=ROUNDS - 1))
        blk.run()


def close0(nc, a, x, ident, w):
    with ExitStack() as ctx:
        blk = Block(nc, ctx, "c0")
        half = T // H0
        wo, bo = blk.sbuf("wo", [P, D]), blk.sbuf("bo", [1, D])
        ones = blk.sbuf("ones", [1, P])
        loads = blk.slot("loads", step=32)
        rden = blk.slot("rden", [P, TPB, H0])
        o = blk.slot("o", [P, H0 // 2, TPB, 2, HD])
        oT = blk.slot("oT", [P, half, H0])
        turned = blk.bank("turned", [P, T])
        out = blk.bank("out", [P, TPB, D])

        first = blk.part("first")
        ul, u1 = first.use(loads), first.use(rden)

        def load(r):
            r.eng.dma_start(wo[:, :], a["wo"]).then_inc(ul.full, 16)
            r.eng.dma_start(bo[:, :], a["bo"].unsqueeze(0)).then_inc(ul.full, 16)
        first.step("sync", 0, load)
        first.step("vector", 0, lambda r: r.eng.memset(ones[:, :], 1.0).then_inc(u1.full, 1))

        def wait_consts(r):
            r.ready(ul)
            r.ready(u1)
        first.step("tensor", 0, wait_consts)

        loop = blk.part("loop", rounds=B)
        u = {k: loop.use(s) for k, s in (("rden", rden), ("o", o), ("oT", oT), ("turned", turned), ("out", out))}

        def divide(r):
            v = r.eng
            tiles = w["o_all"][:, bass.ds(r.i * TPB, TPB), :, :]
            v.reciprocal(rden.buf[:, :, :], tiles[:, :, :, HD]).then_inc(u["rden"].full, 1)
            r.ready(u["rden"])
            r.claim(u["o"])
            for side in range(2):
                rows = slice(side * half, (side + 1) * half)
                for odd in range(2):
                    last = v.tensor_tensor(
                        o.buf[odd * half:(odd + 1) * half, :, :, side, :],
                        w["o_all"][rows, bass.ds(r.i * TPB, TPB), odd::2, 0:HD].rearrange("p t h k -> p h t k"),
                        spread(rden.buf[rows, :, odd::2].rearrange("p t h -> p h t"), HD), ALU.mult)
            last.then_inc(u["o"].full, 1)
        loop.step("vector", 0, divide)

        def turn(r):
            r.ready(u["o"])
            r.claim(u["turned"])
            for h in range(H0 // 2):
                last = r.eng.transpose(turned.buf[:, h * P:(h + 1) * P],
                                       o.buf[:, h, :, :, :].rearrange("u t s k -> u (t s k)"), ident[:, :])
            last.then_inc(u["turned"].full, 1)
        loop.step("tensor", 1, turn)

        def keep(r):
            r.ready(u["turned"])
            r.eng.sem_inc(u["o"].free, 1)
            r.claim(u["oT"])
            r.eng.activation(oT.buf[:, :, :], turned.buf[:, :].rearrange("p (h u) -> p u h", h=H0), ACT.Copy)\
                .then_inc(u["oT"].full, 1)
            r.ready(u["oT"])
            r.eng.sem_inc(u["turned"].free, 1)
        loop.step("scalar", 2, keep)

        def project(r):
            r.ready(u["oT"])
            r.claim(u["out"])
            for t in range(TPB):
                r.eng.matmul(out.buf[:, t, :], ones[:, :], bo[:, :], start=True, stop=False)
                last = r.eng.matmul(out.buf[:, t, :],
                                    oT.buf[:, t * P // H0:(t + 1) * P // H0, :].rearrange("p u h -> p (u h)"),
                                    wo[:, :], start=False, stop=True)
            last.then_inc(u["out"].full, 1)
        loop.step("tensor", 3, project)

        def add(r):
            r.ready(u["out"])
            r.eng.sem_inc(u["oT"].free, 1)
            xt = x[:, bass.ds(r.i * TPB, TPB), :]
            r.eng.tensor_tensor(xt, xt, out.buf[:, :, :], ALU.add).then_inc(u["out"].free, 1)
        loop.step("vector", 4, add)
        blk.run()


def prepare1(nc, a, x, xnT, ident, order, w):
    with ExitStack() as ctx:
        blk = Block(nc, ctx, "p1")
        gw, gb = blk.sbuf("gw", [D, EM]), blk.sbuf("gb", [P, EM])
        lg = blk.sbuf("lg", [P, NT, EM])
        loads = blk.slot("loads", step=32)
        xn, xs = blk.slot("xn", [P, 4, D]), blk.slot("xs", [P, 4 * P])
        kept, lgs = blk.slot("kept"), blk.slot("lgs")
        turned, logits = blk.bank("turned", [P, 512]), blk.bank("logits", [P, 4, EM])

        first = blk.part("first")
        ul = first.use(loads)

        def load(r):
            r.eng.dma_start(gw[:, :], a["gate_w"]).then_inc(ul.full, 16)
            r.eng.dma_start(gb[:, :], a["gate_b"].partition_broadcast(P)).then_inc(ul.full, 16)
        first.step("sync", 0, load)
        first.step("tensor", 0, lambda r: r.ready(ul))
        first.step("vector", 0, lambda r: r.ready(ul))
        st = layer_norm_stats(blk, first, 0, x, None)

        tiles = blk.part("tiles", rounds=NT // 4)
        u = {n: tiles.use(s) for n, s in (("xn", xn), ("xs", xs), ("turned", turned), ("logits", logits),
                                          ("kept", kept))}

        def normalise(r):
            r.claim(u["xn"])
            for j in range(4):
                at = r.i * 4 + j
                last = r.eng.tensor_scalar(xn.buf[:, j, :], x[:, at, :], st["mean"][:, bass.ds(at, 1)],
                                           st["rstd"][:, bass.ds(at, 1)], ALU.subtract, ALU.mult)
            last.then_inc(u["xn"].full, 1)
        tiles.step("vector", 0, normalise)

        def turn(r):
            r.ready(u["xn"])
            r.claim(u["turned"])
            for j in range(4):
                last = r.eng.transpose(turned.buf[:, j * P:(j + 1) * P], xn.buf[:, j, :], ident[:, :])
            last.then_inc(u["turned"].full, 1)
        tiles.step("tensor", 1, turn)

        def keep_turned(r):
            r.ready(u["turned"])
            r.eng.sem_inc(u["xn"].free, 1)
            r.claim(u["xs"])
            r.eng.activation(xs.buf[:, :], turned.buf[:, :], ACT.Copy).then_inc(u["xs"].full, 1)
            r.ready(u["xs"])
            r.eng.sem_inc(u["turned"].free, 1)
        tiles.step("scalar", 2, keep_turned)

        def keep_xnT(r):
            r.ready(u["xs"])
            r.eng.tensor_copy(xnT[:, bass.ds(r.i * 512, 512)], xs.buf[:, :]).then_inc(u["kept"].full, 1)
        tiles.step("gpsimd", 3, keep_xnT)

        def route(r):
            r.ready(u["xs"])
            r.claim(u["logits"])
            for j in range(4):
                last = r.eng.matmul(logits.buf[:, j, :], xs.buf[:, j * P:(j + 1) * P], gw[:, :],
                                    start=True, stop=True)
            last.then_inc(u["logits"].full, 1)
        tiles.step("tensor", 4, route)

        def keep_logits(r):
            r.ready(u["logits"])
            r.eng.tensor_tensor(lg[:, bass.ds(r.i * 4, 4), :], logits.buf[:, :, :],
                                gb[:, :].unsqueeze(1).to_broadcast([P, 4, EM]), ALU.add)\
                .then_inc(u["logits"].free, 1)
            r.ready(u["kept"])
            r.eng.sem_inc(u["xs"].free, 1)
        tiles.step("vector", 5, keep_logits)

        mix = blk.part("mix")
        tmp = {n: blk.sbuf(f"t2_{n}", [P, NT, 8])[:, :, :] for n in ("sel", "c", "q")} | {
            n: blk.sbuf(f"t2_{n}", [P, NT])[:, :] for n in ("m", "first", "second")}
        chain = mix.chain(blk.slot("mix"), TOP2_LINKS + 6)
        e, e_of = mix.use(lgs), mix.use(blk.slot("exps"))

        def choose(r):
            v, link = r.eng, Links(r, chain)
            r.all_freed(logits)
            one, other = top2(v, link, lg[:, :, :], tmp, order[:, :])
            link(v.tensor_tensor(one, one, other, ALU.add))
            link(v.tensor_tensor(lg[:, :, :], lg[:, :, :], spread(tmp["first"], 8), ALU.subtract))
            v.sem_inc(e.full, 1)
            r.ready(e_of)
            link(v.tensor_tensor(lg[:, :, :], lg[:, :, :], one, ALU.mult))
            link(v.tensor_reduce(tmp["m"], lg[:, :, :], AX.X, ALU.add))
            link(v.reciprocal(tmp["m"], tmp["m"]))
            link(v.tensor_tensor(w["combine"][:, :, 0:EM], lg[:, :, :], spread(tmp["m"], 8), ALU.mult))
            v.memset(w["combine"][:, :, EM:EM + 1], 1.0)

        def exps(r):
            r.ready(e)
            r.eng.activation(lg[:, :, :], lg[:, :, :], ACT.Exp).then_inc(e_of.full, 1)
        mix.step("vector", 0, choose)
        mix.step("scalar", 0, exps)
        blk.run()


def main1(nc, a, x, xnT, ident, w):
    with ExitStack() as ctx:
        blk = Block(nc, ctx, "m1")
        sb, slot = blk.sbuf, blk.slot
        wqT, wkT, wvT, woT = (sb(n, [D, D]) for n in ("wqT", "wkT", "wvT", "woT"))
        bqk, bv, bo = sb("bqk", [P, 2]), sb("bv", [P, D]), sb("bo", [1, D])
        proj, half = sb("proj", [P, HF * JF]), sb("half", [P, HF])
        vmask = sb("vmask", [P, 18])
        eps, ones, ones_rows = sb("eps", [P, 1]), sb("ones", [1, P]), sb("ones_rows", [HF, P])
        w1, b1 = sb("w1", [D, EM + 1, HID]), sb("b1", [P, EM + 1, HT])
        w2, b2 = sb("w2", [P, EM + 1, HT, D]), sb("b2", [EM + 1, D])
        n_loads = 15
        loads = slot("loads", step=16 * n_loads)
        consts, tally = slot("consts"), slot("tally")
        xcur = slot("xcur", [D, T])
        kT, k2 = slot("kT", [P, T]), slot("k2", [P, T])
        diag, peaks = slot("diag", [P, TPB, HF]), sb("peaks", [P, TPB, HF])
        dd = slot("dd", [P, TPB, HF * JF])
        stab, stab_in, stab_d = slot("stab"), sb("stab_in", [P, HF]), sb("stab_d", [HF, HF + 1])
        shift = slot("shift", [P, TPB, HF])
        vext = slot("vext", [P, TPB, FT, 18])
        kp = [slot(f"kp{k}", [P, HF * JF]) for k in range(2)]
        kpe = slot("kpe")
        kv = slot("kv", [P, FT, 18])
        qd = [slot(f"qd{k}", [P, HF * JF]) for k in range(2)]
        qsub, qmax = slot("qsub", [P, HF]), slot("qmax", [P, HF])
        qe = [slot(f"qe{k}") for k in range(2)]
        qpT = [slot(f"qpT{k}", [P, FT, P]) for k in range(2)]
        oden, o1 = slot("oden", [P, FT, 2]), slot("o1", [P, 4, D])
        o1T = slot("o1T", [P, 4 * P])
        hT = [slot(f"hT{k}", [P, HT, 512]) for k in range(2)]
        mixed = [slot(f"mixed{k}", [P, 4, D]) for k in range(2)]
        cT = slot("cT", [EM + 1, 512])
        cmb, biased = slot("cmb", [P, 4, EM + 1]), slot("biased", [P, 4, D])
        attn = slot("attn", [P, 512])
        kpx = [slot(f"kpx{k}") for k in range(2)]
        ochain = slot("ochain")
        ones16 = ones_rows[:, :]
        kv_ps, small = blk.bank("kv_sums", [P, FT, 18]), blk.bank("small", [P, 512])
        blk.ring(3, [P, T])

        first = blk.part("first")
        ul, uc = first.use(loads), [first.use(consts) for _ in range(2)]

        def load(r):
            for dst, src in (
                (wqT, a["wqT"]), (wkT, a["wkT"]), (wvT, a["wvT"]), (woT, a["woT"]), (bqk, a["bqk"]),
                (bv, a["bv1"].partition_broadcast(P)), (bo, a["bo1"].unsqueeze(0)), (proj, a["proj"]),
                (half, a["half"]), (vmask, a["vmask"]), (b2, a["b2"]),
            ):
                r.eng.dma_start(dst[:, :], src).then_inc(ul.full, 16)
            r.eng.dma_start(b1[:, :, :], a["b1"].rearrange("e (t p) -> p e t", p=P), allow_slow_non_contiguous=True)\
                .then_inc(ul.full, 16)
            r.eng.dma_start(w1[:, 0:EM, :], a["w1"].rearrange("e d h -> d e h")).then_inc(ul.full, 16)
            r.eng.dma_start(w1[:, EM, :], a["ws1"]).then_inc(ul.full, 16)
            r.eng.dma_start(w2[:, :, :, :], a["w2"].rearrange("e (t p) d -> p e t d", p=P)).then_inc(ul.full, 16)
        first.step("sync", 0, load)

        def constants(r):
            v = r.eng
            v.memset(eps[:, :], EPS_FEAT)
            v.memset(ones[:, :], 1.0)
            v.memset(ones_rows[:, :], 1.0)
            v.memset(vext.buf[:, :, :, 16:18], 1.0)
            r.ready(ul)
            v.tensor_scalar(bqk[:, :], bqk[:, :], DN, None, ALU.mult).then_inc(uc[0].full, 1)
            r.ready(uc[0])
        first.step("vector", 0, constants)
        for engine in ("tensor", "scalar", "gpsimd"):
            first.step(engine, 0, lambda r: (r.ready(ul), r.ready(uc[0])))

        loop = blk.part("loop", rounds=ROUNDS1)
        performer(loop, blk, locals())
        experts(loop, blk, locals())
        blk.run()


TICKS1 = {
    "values": lambda t: 0.1,
    "kside": lambda t: 0.3,
    "kkeep": lambda t: -0.062,
    "ksquare": lambda t: 0.233,
    "khalf": lambda t: 0.5,
    "kdiag": lambda t: 0.817,
    "kfeat": lambda t: [1, 1.6, 2.2, 2.8, 3.4, 4, 4.6, 5.2][t],
    "dkfeat": lambda t: 0.1,
    "dkmax": lambda t: 0.125,
    "stab": lambda t: 6,
    "takeoff": lambda t: [7, 7.6, 8.2, 8.8, 9.4, 10, 10.6, 11.2][t],
    "dkexp": lambda t: 0.1,
    "dkeps": lambda t: 0.2,
    "dksum": lambda t: 0.544,
    "kv": lambda t: 12,
    "qside": lambda t: 6.5,
    "qdiag": lambda t: 7.106,
    "qfeat": lambda t: [12.1, 12.722, 13.344, 13.966, 14.588, 15.21, 15.831, 16.453][t],
    "dqstab": lambda t: 0.1,
    "dqexp": lambda t: 0.137,
    "qturn": lambda t: [12.4, 13, 13.6, 14.2, 14.8, 15.4, 16, 16.6][t],
    "dqeps": lambda t: 0.1,
    "qweigh": lambda t: [12.6, 13.2, 13.8, 14.4, 15, 15.796, 16.2, 16.8][t],
    "dqdiv": lambda t: 0.1,
    "oturn": lambda t: [12.8, 13.4, 14, 14.6, 15.2, 15.8, 16.4, 17][t],
}
TICKS2 = {
    "hidden": lambda t: [0.05, 1.05, 2.05, 3.05, 4.05, 5.05, 6.05, 7.05, 8.05, 9.05, 10.05, 11.05, 12.05, 13.05, 14.05, 15.05, 16.05, 17.05][t],
    "hidden2": lambda t: [0.25, 1.25, 2.25, 3.25, 4.25, 5.25, 6.146, 7.25, 8.25, 9.25, 10.25, 11.25, 12.25, 13.25, 14.25, 15.25, 16.25, 17.25][t],
    "dgelu": lambda t: 0.078,
    "output": lambda t: [1.15, 2.115, 3.081, 4.046, 5.011, 5.976, 6.942, 7.907, 8.872, 9.837, 10.803, 11.768, 12.733, 13.698, 14.664, 15.629, 16.594, 17.559][t],
    "dcomb": lambda t: 0.126,
    "bias": lambda t: [0.5, 9.556][t],
}


def performer(part, blk, n):
    (xnT, x, w, ident) = (n[k] for k in ("xnT", "x", "w", "ident"))
    u = {k: part.use(n[k]) for k in ("xcur", "diag", "dd", "shift", "vext", "kv", "kv_ps")}

    def copy_x(r):
        r.claim(u["xcur"])
        r.eng.tensor_copy(n["xcur"].buf[:, :], xnT[:, bass.ds(r.i * T, T)]).then_inc(u["xcur"].full, 1)
    part.step("gpsimd", 0, copy_x)

    vps = part.ring()

    def values(r):
        r.ready(u["xcur"])
        r.claim(vps)
        for t in range(TPB):
            last = r.eng.matmul(vps.buf[:, t * P:(t + 1) * P], n["xcur"].buf[:, t * P:(t + 1) * P],
                                n["wvT"][:, :], start=True, stop=True)
        last.then_inc(vps.full, 1)
    part.step("tensor", TICKS1["values"](0), values, [vps])

    def keep_values(r):
        r.ready(vps)
        r.claim(u["vext"])
        for t in range(TPB):
            last = r.eng.tensor_tensor(
                n["vext"].buf[:, t, :, 0:16], vps.buf[:, t * P:(t + 1) * P].rearrange("p (f k) -> p f k", f=FT),
                n["bv"][:, :].rearrange("p (f k) -> p f k", f=FT), ALU.add)
        last.then_inc(vps.free, 1)
        r.eng.wait_ge(vps.free, r.nth(vps) + 2)
        r.eng.sem_inc(u["vext"].full, 1)
    part.step("vector", TICKS1["values"](0) + 0.01, keep_values)

    def side(tick, weights, col, name):
        ps, t, sq, dps, dg = (part.ring(), part.use(n["kT"]), part.use(n["k2"]), part.use(n["small"]), None)

        def product(r):
            r.ready(u["xcur"])
            r.claim(ps)
            for c in range(2):
                last = r.eng.matmul(ps.buf[:, c * 512:(c + 1) * 512], n[weights][:, :],
                                    n["xcur"].buf[:, c * 512:(c + 1) * 512], start=True, stop=True)
            last.then_inc(ps.full, 1)
        part.step("tensor", tick, product, [ps])

        def keep(r):
            r.ready(ps)
            if col == 0:
                r.eng.sem_inc(u["xcur"].free, 1)
            r.claim(t)
            r.eng.activation(n["kT"].buf[:, :], ps.buf[:, :], ACT.Identity, bias=n["bqk"][:, col:col + 1],
                             scale=DN).then_inc(t.full, 1)
            r.ready(t)
            r.eng.sem_inc(ps.free, 1)
        part.step("scalar", tick + TICKS1["kkeep"](0), keep)

        def square(r):
            r.ready(t)
            r.claim(sq)
            r.eng.tensor_tensor(n["k2"].buf[:, :], n["kT"].buf[:, :], n["kT"].buf[:, :], ALU.mult)\
                .then_inc(sq.full, 1)
        part.step("gpsimd", tick + TICKS1["ksquare"](0), square)

        def half_sums(r):
            r.ready(sq)
            r.claim(dps)
            for k in range(TPB):
                last = r.eng.matmul(n["small"].buf[:, k * HF:(k + 1) * HF], n["k2"].buf[:, k * P:(k + 1) * P],
                                    n["half"][:, :], start=True, stop=True)
            last.then_inc(dps.full, 1)
        part.step("tensor", tick + TICKS1["khalf"](0), half_sums)
        return t, sq, dps

    kt, k2, kd = side(TICKS1["kside"](0), "wkT", 1, "k")
    dg = u["diag"]

    def keep_diag(r):
        r.ready(kd)
        r.eng.sem_inc(k2.free, 1)
        r.claim(dg)
        r.eng.activation(n["diag"].buf[:, :, :], n["small"].buf[:, 0:P].rearrange("p (t h) -> p t h", t=TPB),
                         ACT.Copy).then_inc(dg.full, 1)
        r.ready(dg)
        r.eng.sem_inc(kd.free, 1)
    part.step("scalar", TICKS1["kdiag"](0), keep_diag)

    for t in range(TPB):
        ps, at = part.ring(), TICKS1["kfeat"](t)

        def features(r, t=t, ps=ps):
            if t == 0:
                r.ready(kt)
            r.claim(ps)
            for c in range(2):
                last = r.eng.matmul(ps.buf[:, c * 512:(c + 1) * 512], n["kT"].buf[:, t * P:(t + 1) * P],
                                    n["proj"][:, c * 512:(c + 1) * 512], start=True, stop=True)
            last.then_inc(ps.full, 1)
        part.step("tensor", at, features, [ps])

        kept = part.use(n["kpe"])

        def keep_features(r, t=t, ps=ps, kept=kept):
            r.ready(ps)
            if t == 0:
                r.claim(u["dd"])
            if t == TPB - 1:
                r.eng.sem_inc(kt.free, 1)
            r.eng.activation(n["dd"].buf[:, t, :], ps.buf[:, :], ACT.Copy).then_inc(kept.full, 1)
            r.ready(kept)
            r.eng.sem_inc(ps.free, 1)
        part.step("scalar", at + TICKS1["dkfeat"](0), keep_features)

        def largest(r, t=t, kept=kept):
            r.ready(kept)
            ins = r.eng.tensor_reduce(n["peaks"][:, t, :], n["dd"].buf[:, t, :].rearrange("p (h j) -> p h j", h=HF),
                                      AX.X, ALU.max)
            if t == TPB - 1:
                ins.then_inc(u["dd"].full, 1)
        part.step("vector", at + TICKS1["dkmax"](0), largest)

    s = [part.use(n["stab"]) for _ in range(3)]
    sp, sp2 = part.ring(), part.ring()
    at = TICKS1["stab"](0)

    def over_tiles(r):
        r.ready(u["dd"])
        r.eng.tensor_reduce(n["stab_in"][:, :], n["peaks"][:, :, :].rearrange("p t h -> p h t"), AX.X, ALU.max)\
            .then_inc(s[0].full, 1)
    part.step("vector", at, over_tiles)

    def turn_stab(r):
        r.ready(s[0])
        r.claim(sp)
        r.eng.transpose(sp.buf[0:HF, 0:P], n["stab_in"][:, :], ident[:, :]).then_inc(sp.full, 1)
    part.step("tensor", at + 0.1, turn_stab, [sp])

    def over_tokens(r):
        r.ready(sp)
        r.eng.tensor_reduce(n["stab_d"][:, HF:HF + 1], sp.buf[0:HF, 0:P], AX.X, ALU.max).then_inc(s[1].full, 1)
        r.ready(s[1])
        r.eng.sem_inc(sp.free, 1)
        r.eng.tensor_scalar(n["stab_d"][:, 0:HF], ident[0:HF, 0:HF], n["stab_d"][:, HF:HF + 1], None, ALU.mult)\
            .then_inc(s[2].full, 1)
    part.step("vector", at + 0.2, over_tokens)

    def to_all(r):
        r.ready(s[2])
        r.claim(sp2)
        r.eng.matmul(sp2.buf[:, 0:HF], n["ones16"], n["stab_d"][:, 0:HF], start=True, stop=True)\
            .then_inc(sp2.full, 1)
    part.step("tensor", at + 0.3, to_all, [sp2])

    def make_shift(r):
        r.ready(sp2)
        r.ready(dg)
        r.claim(u["shift"])
        r.eng.tensor_tensor(n["shift"].buf[:, :, :], n["diag"].buf[:, :, :],
                            sp2.buf[:, 0:HF].unsqueeze(1).to_broadcast([P, TPB, HF]), ALU.add)\
            .then_inc(u["shift"].full, 1)
        r.ready(u["shift"])
        r.eng.sem_inc(sp2.free, 1)
        r.eng.sem_inc(dg.free, 1)
    part.step("vector", at + 0.4, make_shift)

    for t in range(TPB):
        at = TICKS1["takeoff"](t)
        kp, ex = part.use(n["kp"][t % 2]), part.use(n["kpx"][t % 2])

        def take_off(r, t=t, kp=kp, ex=ex):
            if t == 0:
                r.ready(u["shift"])
            r.claim(kp)
            r.eng.tensor_tensor(kp.buf[:, :].rearrange("p (h j) -> p h j", h=HF),
                                n["dd"].buf[:, t, :].rearrange("p (h j) -> p h j", h=HF),
                                spread(n["shift"].buf[:, t, :], JF), ALU.subtract).then_inc(ex.full, 1)

        def exps(r, kp=kp, ex=ex):
            r.ready(ex)
            r.eng.activation(kp.buf[:, :], kp.buf[:, :], ACT.Exp).then_inc(ex.free, 1)

        def plus_eps(r, t=t, kp=kp, ex=ex):
            r.eng.wait_ge(ex.free, r.nth(ex) + 2)
            if t == TPB - 1:
                r.eng.sem_inc(u["dd"].free, 1)
                r.eng.sem_inc(u["shift"].free, 1)
            r.eng.tensor_scalar(kp.buf[:, :], kp.buf[:, :], RATIO, EPS_FEAT, ALU.mult, ALU.add)\
                .then_inc(kp.full, 1)

        def sum_keys(r, t=t, kp=kp):
            r.ready(kp)
            if t == 0:
                r.ready(u["vext"])
                r.claim(u["kv_ps"])
            for f in range(FT):
                last = r.eng.matmul(n["kv_ps"].buf[:, f, :], kp.buf[:, f * P:(f + 1) * P],
                                    n["vext"].buf[:, t, f, :], start=(t == 0 and f == 0),
                                    stop=(t == TPB - 1), skip_group_check=True)
            last.then_inc(kp.free, 1)

        part.step("gpsimd", at, take_off)
        part.step("scalar", at + TICKS1["dkexp"](0), exps)
        part.step("vector", at + TICKS1["dkeps"](0), plus_eps)
        part.step("tensor", at + TICKS1["dksum"](0), sum_keys)

    last_kp = kp

    def keep_kv(r):
        r.eng.wait_ge(last_kp.free, r.nth(last_kp) + 2)
        r.eng.sem_inc(u["vext"].free, 1)
        r.claim(u["kv"])
        r.eng.tensor_tensor(n["kv"].buf[:, :, :], n["kv_ps"].buf[:, :, :],
                            n["vmask"][:, :].unsqueeze(1).to_broadcast([P, FT, 18]), ALU.mult)\
            .then_inc(u["kv"].full, 1)
        r.ready(u["kv"])
        r.eng.sem_inc(u["kv_ps"].free, 1)
    part.step("vector", TICKS1["kv"](0), keep_kv)

    qt, q2, qg = side(TICKS1["qside"](0), "wqT", 0, "q")
    dq = part.use(n["diag"])

    def keep_diag_q(r):
        r.ready(qg)
        r.eng.sem_inc(q2.free, 1)
        r.claim(dq)
        r.eng.activation(n["diag"].buf[:, :, :], n["small"].buf[:, 0:P].rearrange("p (t h) -> p t h", t=TPB),
                         ACT.Copy).then_inc(dq.full, 1)
        r.ready(dq)
        r.eng.sem_inc(qg.free, 1)
    part.step("scalar", TICKS1["qdiag"](0), keep_diag_q)

    for t in range(TPB):
        ps, at = part.ring(), TICKS1["qfeat"](t)
        qd, qx, mx, sbt = part.use(n["qd"][t % 2]), part.use(n["qe"][t % 2]), part.use(n["qmax"]), part.use(n["qsub"])
        tp, qT, op = part.ring(), part.use(n["qpT"][t % 2]), part.use(n["small"])
        od = part.use(n["oden"])
        if t % 4 == 0:
            o1 = part.use(n["o1"])
        ochain = [part.use(n["ochain"]) for _ in range(2)]

        def features(r, t=t, ps=ps):
            if t == 0:
                r.ready(qt)
            r.claim(ps)
            for c in range(2):
                last = r.eng.matmul(ps.buf[:, c * 512:(c + 1) * 512], n["kT"].buf[:, t * P:(t + 1) * P],
                                    n["proj"][:, c * 512:(c + 1) * 512], start=True, stop=True)
            last.then_inc(ps.full, 1)
        part.step("tensor", at, features, [ps])

        def stabilise(r, t=t, ps=ps, qd=qd, mx=mx, sbt=sbt):
            v = r.eng
            r.ready(ps)
            if t == 0:
                r.ready(dq)
            if t == TPB - 1:
                v.sem_inc(qt.free, 1)
            view = ps.buf[:, :].rearrange("p (h j) -> p h j", h=HF)
            v.tensor_reduce(n["qmax"].buf[:, :], view, AX.X, ALU.max).then_inc(mx.full, 1)
            r.ready(mx)
            v.tensor_tensor(n["qsub"].buf[:, :], n["qmax"].buf[:, :], n["diag"].buf[:, t, :], ALU.add)\
                .then_inc(sbt.full, 1)
            r.ready(sbt)
            if t == TPB - 1:
                v.sem_inc(dq.free, 1)
            r.claim(qd)
            v.tensor_tensor(qd.buf[:, :].rearrange("p (h j) -> p h j", h=HF), view,
                            spread(n["qsub"].buf[:, :], JF), ALU.subtract).then_inc(qd.full, 1)
            r.ready(qd)
            v.sem_inc(ps.free, 1)
        part.step("vector", at + TICKS1["dqstab"](0), stabilise)

        def exps(r, qd=qd, qx=qx):
            r.ready(qd)
            r.eng.activation(qd.buf[:, :], qd.buf[:, :], ACT.Exp).then_inc(qx.full, 1)
        part.step("scalar", at + TICKS1["dqexp"](0), exps)

        def turn(r, qd=qd, qx=qx, tp=tp):
            r.ready(qx)
            r.claim(tp)
            for f in range(FT):
                last = r.eng.transpose(tp.buf[:, f * P:(f + 1) * P], qd.buf[:, f * P:(f + 1) * P], ident[:, :])
            last.then_inc(tp.full, 1)
        part.step("tensor", TICKS1["qturn"](t), turn, [tp])

        def plus_eps(r, qd=qd, tp=tp, qT=qT):
            r.ready(tp)
            r.eng.sem_inc(qd.free, 1)
            r.claim(qT)
            r.eng.activation(qT.buf[:, :, :], tp.buf[:, :].rearrange("p (f q) -> p f q", f=FT), ACT.Identity,
                             bias=n["eps"][:, :], scale=RATIO).then_inc(qT.full, 1)
            r.ready(qT)
            r.eng.sem_inc(tp.free, 1)
        part.step("scalar", TICKS1["qturn"](t) + TICKS1["dqeps"](0), plus_eps)

        def weigh(r, t=t, qT=qT, op=op):
            if t == 0:
                r.ready(u["kv"])
            r.ready(qT)
            r.claim(op)
            for f in range(FT):
                last = r.eng.matmul(n["small"].buf[:, f * 18:(f + 1) * 18], qT.buf[:, f, :], n["kv"].buf[:, f, :],
                                    start=True, stop=True)
            last.then_inc(op.full, 1)
        part.step("tensor", TICKS1["qweigh"](t), weigh)

        def divide(r, t=t, qT=qT, op=op, od=od, o1=o1, ochain=ochain):
            v, link = r.eng, Links(r, ochain)
            r.ready(op)
            v.sem_inc(qT.free, 1)
            if t == TPB - 1:
                v.sem_inc(u["kv"].free, 1)
            got = n["small"].buf[:, 0:FT * 18].rearrange("p (f k) -> p f k", f=FT)
            link(v.tensor_scalar(n["oden"].buf[:, :, :], got[:, :, 16:18], EPS_DEN, None, ALU.max))
            link(v.reciprocal(n["oden"].buf[:, :, :], n["oden"].buf[:, :, :]))
            if t % 4 == 0:
                r.claim(o1)
            v.tensor_tensor(n["o1"].buf[:, t % 4, :].rearrange("p (f h k) -> p f h k", f=FT, h=2),
                            got[:, :, 0:16].rearrange("p f (h k) -> p f h k", h=2),
                            spread(n["oden"].buf[:, :, :], HD), ALU.mult).then_inc(op.free, 1)
            if t % 4 == 3:
                v.wait_ge(op.free, r.nth(op) + 2)
                v.sem_inc(o1.full, 1)
        part.step("vector", TICKS1["qweigh"](t) + TICKS1["dqdiv"](0), divide)

        if t % 4 == 3:
            t1, oT, t2 = part.ring(), part.use(n["o1T"]), part.ring()

            def turn_o(r, o1=o1, t1=t1):
                r.ready(o1)
                r.claim(t1)
                for k in range(4):
                    last = r.eng.transpose(t1.buf[:, k * P:(k + 1) * P], n["o1"].buf[:, k, :], ident[:, :])
                last.then_inc(t1.full, 1)
            part.step("tensor", TICKS1["oturn"](t), turn_o, [t1])

            def keep_oT(r, o1=o1, t1=t1, oT=oT):
                r.ready(t1)
                r.eng.sem_inc(o1.free, 1)
                r.claim(oT)
                r.eng.activation(n["o1T"].buf[:, :], t1.buf[:, 0:512], ACT.Copy).then_inc(oT.full, 1)
                r.ready(oT)
                r.eng.sem_inc(t1.free, 1)
            part.step("scalar", TICKS1["oturn"](t) + 0.05, keep_oT)

            def project(r, oT=oT, t2=t2):
                r.ready(oT)
                r.claim(t2)
                for k in range(4):
                    r.eng.matmul(t2.buf[:, k * P:(k + 1) * P], n["ones"][:, :], n["bo"][:, :], start=True, stop=False)
                    last = r.eng.matmul(t2.buf[:, k * P:(k + 1) * P], n["o1T"].buf[:, k * P:(k + 1) * P],
                                        n["woT"][:, :], start=False, stop=True)
                last.then_inc(t2.full, 1)
            part.step("tensor", TICKS1["oturn"](t) + 0.10, project, [t2])

            mx2 = part.use(n["attn"])

            def keep_out(r, oT=oT, t2=t2, mx2=mx2):
                r.ready(t2)
                r.eng.sem_inc(oT.free, 1)
                r.claim(mx2)
                r.eng.activation(n["attn"].buf[:, :], t2.buf[:, 0:512], ACT.Copy).then_inc(mx2.full, 1)
                r.ready(mx2)
                r.eng.sem_inc(t2.free, 1)
            part.step("scalar", TICKS1["oturn"](t) + 0.15, keep_out)

            def add(r, t=t, mx2=mx2):
                r.ready_apart(mx2, n["tally"])
                xt = x[:, bass.ds(r.i * TPB + (t - 3), 4), :].rearrange("p t d -> p (t d)")
                r.eng.tensor_tensor(xt, xt, n["attn"].buf[:, :], ALU.add).then_inc(mx2.free, 1)
                r.eng.wait_ge(mx2.free, r.nth(mx2) + 2)
            part.step("gpsimd", TICKS1["oturn"](t) + 0.20, add)


def experts(part, blk, n):
    (xnT, x, w, ident) = (n[k] for k in ("xnT", "x", "w", "ident"))
    for blkn in range(2):
        for e in range(EM + 1):
            at = [TICKS2[k](9 * blkn + e) for k in ("hidden", "hidden2", "output", "dgelu", "dcomb")]
            hT = part.use(n["hT"][e % 2])
            hps = [part.ring() for _ in range(2)]

            def hidden(r, e=e, blkn=blkn, k=0, ps=None):
                r.claim(ps)
                for c in range(2):
                    last = r.eng.matmul(ps.buf[:, c * 512:(c + 1) * 512],
                                        n["w1"][:, e, (2 * k + c) * P:(2 * k + c + 1) * P],
                                        xnT[:, bass.ds(r.i * T + blkn * 512, 512)], start=True, stop=True)
                last.then_inc(ps.full, 1)

            def gelu(r, e=e, k=0, ps=None, hT=hT):
                r.ready(ps)
                if k == 0:
                    r.claim(hT)
                for c in range(2):
                    last = r.eng.activation(hT.buf[:, 2 * k + c, :], ps.buf[:, c * 512:(c + 1) * 512], ACT.Gelu,
                                            bias=n["b1"][:, e, 2 * k + c:2 * k + c + 1])
                last.then_inc(ps.free, 1)
                if k == 1:
                    r.eng.wait_ge(ps.free, r.nth(ps) + 2)
                    r.eng.sem_inc(hT.full, 1)
            for k in range(2):
                part.step("tensor", at[k], lambda r, f=hidden, k=k, ps=hps[k]: f(r, k=k, ps=ps), [hps[k]])
                part.step("scalar", at[k] + at[3], lambda r, f=gelu, k=k, ps=hps[k]: f(r, k=k, ps=ps))

            ops, mx = part.ring(), part.use(n["mixed"][e % 2])

            def output(r, e=e, hT=hT, ops=ops):
                r.ready(hT)
                r.claim(ops)
                for t in range(4):
                    for k in range(HT):
                        last = r.eng.matmul(ops.buf[:, t * P:(t + 1) * P], hT.buf[:, k, t * P:(t + 1) * P],
                                            n["w2"][:, e, k, :], start=(k == 0), stop=(k == HT - 1))
                last.then_inc(ops.full, 1)
            part.step("tensor", at[2], output, [ops])

            def combine(r, e=e, blkn=blkn, hT=hT, ops=ops, mx=mx):
                r.ready(ops)
                r.eng.sem_inc(hT.free, 1)
                r.claim(mx)
                weights = w["combine"][:, bass.ds(r.i * TPB + 4 * blkn, 4), e]
                r.eng.tensor_tensor(mx.buf[:, :, :], ops.buf[:, 0:512].rearrange("p (t d) -> p t d", t=4),
                                    spread(weights, D), ALU.mult).then_inc(mx.full, 1)
                r.ready(mx)
                r.eng.sem_inc(ops.free, 1)
            part.step("vector", at[2] + at[4], combine)

            def add(r, blkn=blkn, mx=mx):
                r.ready_apart(mx, n["tally"])
                xt = x[:, bass.ds(r.i * TPB + 4 * blkn, 4), :]
                r.eng.tensor_tensor(xt, xt, mx.buf[:, :, :], ALU.add).then_inc(mx.free, 1)
                r.eng.wait_ge(mx.free, r.nth(mx) + 2)
            part.step("gpsimd", at[2] + at[4] + 0.05, add)

        at = TICKS2["bias"](blkn)
        cps, cT, bps = part.ring(), part.use(n["cT"]), part.ring()

        def turn(r, blkn=blkn, cps=cps):
            r.claim(cps)
            for t in range(4):
                last = r.eng.transpose(cps.buf[0:EM + 1, t * P:(t + 1) * P], n["cmb"].buf[:, t, :], ident[:, :])
            last.then_inc(cps.full, 1)
        cm = part.use(n["cmb"])

        def copy_combine(r, blkn=blkn, cm=cm):
            r.claim(cm)
            r.eng.tensor_copy(n["cmb"].buf[:, :, :], w["combine"][:, bass.ds(r.i * TPB + 4 * blkn, 4), :])\
                .then_inc(cm.full, 1)
        part.step("gpsimd", at - 0.01, copy_combine)
        part.step("tensor", at, lambda r, f=turn, cm=cm: (r.ready(cm), f(r)), [cps])

        def keep(r, cps=cps, cT=cT, cm=cm):
            r.ready(cps)
            r.eng.sem_inc(cm.free, 1)
            r.claim(cT)
            r.eng.activation(n["cT"].buf[:, :], cps.buf[0:EM + 1, 0:512], ACT.Copy).then_inc(cT.full, 1)
            r.ready(cT)
            r.eng.sem_inc(cps.free, 1)
        part.step("scalar", at + 0.01, keep)

        def biases(r, cT=cT, bps=bps):
            r.ready(cT)
            r.claim(bps)
            for t in range(4):
                last = r.eng.matmul(bps.buf[:, t * P:(t + 1) * P], n["cT"].buf[:, t * P:(t + 1) * P], n["b2"][:, :],
                                    start=True, stop=True)
            last.then_inc(bps.full, 1)
        part.step("tensor", at + 0.02, biases, [bps])
        bb = part.use(n["biased"])

        def keep_biases(r, cT=cT, bps=bps, bb=bb):
            r.ready(bps)
            r.eng.sem_inc(cT.free, 1)
            r.claim(bb)
            r.eng.activation(n["biased"].buf[:, :, :], bps.buf[:, 0:512].rearrange("p (t d) -> p t d", t=4), ACT.Copy)\
                .then_inc(bb.full, 1)
            r.ready(bb)
            r.eng.sem_inc(bps.free, 1)
        part.step("scalar", at + 0.03, keep_biases)

        def add(r, blkn=blkn, bb=bb):
            r.ready_apart(bb, n["tally"])
            xt = x[:, bass.ds(r.i * TPB + 4 * blkn, 4), :]
            r.eng.tensor_tensor(xt, xt, n["biased"].buf[:, :, :], ALU.add).then_inc(bb.free, 1)
            r.eng.wait_ge(bb.free, r.nth(bb) + 2)
        part.step("gpsimd", at + 0.04, add)


def build(nc, a):
    with ExitStack() as whole:
        def keep(name, shape, dt=F32):
            return whole.enter_context(nc.sbuf_tensor(name, shape, dt))

        x = keep("x", [P, NT, D])
        xnT = keep("xnT", [P, B * T])
        ident = keep("ident", [P, P])
        order = keep("order", [P, 8])
        with ExitStack() as l0:
            def keep0(name, shape, dt=F32):
                return l0.enter_context(nc.sbuf_tensor(name, shape, dt))
            w = {
                "gate": keep0("gate", [P, NT, 2 * HS * ES]),
                "ks": keep0("ks", [P, 2, B * T], BF16),
                "split": keep0("split", [P, 4]),
                "v32": keep0("v32", [P, NT, 32]),
                "qk": keep0("qk", [P, HS, P]),
                "o_all": keep0("o_all", [P, NT, H0, HD + 1]),
            }
            prepare0(nc, a, x, xnT, ident, order, w)
            main0(nc, a, x, xnT, ident, w)
            close0(nc, a, x, ident, w)

        with ExitStack() as l1:
            w = {"combine": l1.enter_context(nc.sbuf_tensor("combine", [P, NT, EM + 1], F32))}
            prepare1(nc, a, x, xnT, ident, order, w)
            main1(nc, a, x, xnT, ident, w)
        with nc.semaphore("stored") as stored, nc.Block() as block:
            @block.sync
            def _(eng):
                eng.dma_start(a["out"].rearrange("(t p) d -> p t d", p=P), x[:, :, :]).then_inc(stored, 16)
                eng.wait_ge(stored, 16)


def build1(nc, a):
    with ExitStack() as whole:
        def keep(name, shape, dt=F32):
            return whole.enter_context(nc.sbuf_tensor(name, shape, dt))

        x = keep("x", [P, NT, D])
        xnT = keep("xnT", [P, B * T])
        ident = keep("ident", [P, P])
        order = keep("order", [P, 8])
        with nc.semaphore("xl") as xl, nc.Block() as block:
            @block.sync
            def _(eng):
                eng.dma_start(x[:, :, :], a["x"].rearrange("(t p) d -> p t d", p=P)).then_inc(xl, 16)
                eng.dma_start(order[:, :], a["order"].partition_broadcast(P)).then_inc(xl, 16)
                eng.dma_start(ident[:, :], a["identity"]).then_inc(xl, 16)
                eng.wait_ge(xl, 48)
        with ExitStack() as l1:
            w = {"combine": l1.enter_context(nc.sbuf_tensor("combine", [P, NT, EM + 1], F32))}
            prepare1(nc, a, x, xnT, ident, order, w)
            main1(nc, a, x, xnT, ident, w)
        with nc.semaphore("stored") as stored, nc.Block() as block:
            @block.sync
            def _(eng):
                eng.dma_start(a["out"].rearrange("(t p) d -> p t d", p=P), x[:, :, :]).then_inc(stored, 16)
                eng.wait_ge(stored, 16)


def build0(nc, a):
    with ExitStack() as whole:
        def keep(name, shape, dt=F32):
            return whole.enter_context(nc.sbuf_tensor(name, shape, dt))

        x = keep("x", [P, NT, D])
        xnT = keep("xnT", [P, B * T])
        ident = keep("ident", [P, P])
        order = keep("order", [P, 8])
        with ExitStack() as l0:
            def keep0(name, shape, dt=F32):
                return l0.enter_context(nc.sbuf_tensor(name, shape, dt))
            w = {
                "gate": keep0("gate", [P, NT, 2 * HS * ES]),
                "ks": keep0("ks", [P, 2, B * T], BF16),
                "split": keep0("split", [P, 4]),
                "v32": keep0("v32", [P, NT, 32]),
                "qk": keep0("qk", [P, HS, P]),
                "o_all": keep0("o_all", [P, NT, H0, HD + 1]),
            }
            prepare0(nc, a, x, xnT, ident, order, w)
            main0(nc, a, x, xnT, ident, w)
        with nc.semaphore("stored") as stored, nc.Block() as block:
            @block.sync
            def _(eng):
                eng.dma_start(a["out"].rearrange("(t p) d -> p t d", p=P), x[:, :, :]).then_inc(stored, 16)
                eng.wait_ge(stored, 16)


def layout(i):
    f = np.float32
    get = {k: np.asarray(v) for k, v in i.items()}
    wq, bq = get["L0_attn_Wq"], get["L0_attn_bq"]
    wkv, bkv = get["L0_attn_Wkv"], get["L0_attn_bkv"]
    rows = SPLIT * HD
    wqs, bqs = np.zeros((H0 // 2, D, P), f), np.zeros((P, H0 // 2), f)
    wks, bks = np.zeros((D, 2, P), f), np.zeros((P, 2), f)
    for g in range(SPLIT):
        for hh in range(2):
            at = slice(hh * rows + g * HD, hh * rows + (g + 1) * HD)
            wks[:, hh, at] = wkv[:HD].T
            bks[at, hh] = bkv[:HD]
            for pair in range(H0 // 2):
                h = slice((2 * pair + hh) * HD, (2 * pair + hh + 1) * HD)
                wqs[pair][:, at] = wq[h].T
                bqs[at, pair] = bq[h]
    for hh in range(2):
        bks[96 + 3 * hh:99 + 3 * hh, hh] = 1
    split = np.zeros((P, 4), f)
    for col, classes in ((0, (0, 0, 0, 1, 1, 2)), (2, (0, 1, 2, 0, 1, 0))):
        for hh in range(2):
            for g, c in enumerate(classes):
                at = slice(hh * rows + g * HD, hh * rows + (g + 1) * HD)
                split[at, col], split[at, col + 1] = -(c >= 1), -(c == 2)
    proj, half, vmask = np.zeros((P, HF * JF), f), np.zeros((P, HF), f), np.zeros((P, 18), f)
    for h in range(HF):
        proj[h * HD:(h + 1) * HD, h * JF:(h + 1) * JF] = get["L1_attn_proj"][h].T
        half[h * HD:(h + 1) * HD, h] = 0.5
    for hh in range(2):
        vmask[hh * JF:(hh + 1) * JF, hh * HD:(hh + 1) * HD] = 1
        vmask[hh * JF:(hh + 1) * JF, 16 + hh] = 1
    selv = np.concatenate([get["L0_ffn_sel_v_w"].T, get["L0_ffn_sel_o_w"].T, wkv[HD:].T,
                           np.zeros((D, 32 - HD), f)], axis=1)
    bv = np.concatenate([bkv[HD:], np.ones(1, f), np.zeros(32 - HD - 1, f)])
    return {
        "x": get["L0_attn_x"].reshape(B * T, D),
        "q_w": get["L0_ffn_q_w"], "k_w": get["L0_ffn_k_w"],
        "v_w": get["L0_ffn_v_w"], "o_w": get["L0_ffn_o_w"],
        "selv": selv, "wk": wks, "bk": bks, "bv": bv, "wq": wqs, "split": split,
        "route": get["L0_ffn_route_scale"], "order": np.arange(8, 0, -1).astype(f),
        "wo": get["L0_attn_Wo"].T, "bo": get["L0_attn_bo"],
        "bq": bqs,
        "gate_w": get["L1_ffn_gate_w"], "gate_b": get["L1_ffn_gate_b"],
        "wqT": get["L1_attn_Wq"].T, "wkT": get["L1_attn_Wk"].T, "wvT": get["L1_attn_Wv"].T,
        "woT": get["L1_attn_Wo"].T, "bqk": np.stack([get["L1_attn_bq"], get["L1_attn_bk"]], axis=1),
        "bv1": get["L1_attn_bv"], "bo1": get["L1_attn_bo"], "proj": proj, "half": half, "vmask": vmask,
        "w1": get["L1_ffn_w1"], "ws1": get["L1_ffn_ws1"],
        "w2": np.concatenate([get["L1_ffn_w2"], get["L1_ffn_ws2"][None]]),
        "b1": np.concatenate([get["L1_ffn_b1"], get["L1_ffn_bs1"][None]]),
        "b2": np.concatenate([get["L1_ffn_b2"], get["L1_ffn_bs2"][None]]),
    }


def kernel(**inputs):
    import concourse.bacc as _bacc
    from concourse.bass_utils import run_bass_kernel_spmd as _run

    nc = _bacc.Bacc("TRN2", target_bir_lowering=False, num_devices=1)
    arrays = {f"in_{k}": np.ascontiguousarray(v) for k, v in layout(inputs).items()}
    a = {k[3:]: nc.dram_tensor(k, v.shape, mybir.dt.from_np(v.dtype), kind="ExternalInput").ap()
         for k, v in arrays.items()}
    a["out"] = nc.dram_tensor("out", (B * T, D), F32, kind="ExternalOutput").ap()
    build(nc, a)
    return _run(nc, [arrays], core_ids=[0]).results[0]["out"].reshape(B, T, D)
```

```python
from contextlib import ExitStack
from functools import partial

import numpy as np

import concourse.bass as bass
from concourse import mybir

ALU = mybir.AluOpType
ACT = mybir.ActivationFunctionType
AX = mybir.AxisListType
F32 = mybir.dt.float32
BF16 = mybir.dt.bfloat16
F32R = mybir.dt.float32r

P = 128
B, T, D = 4, 1024, 128
NT = B * T // P
TPB = T // P
H0, HD = 16, 8
SPLIT = 6
HS, ES, PS = 8, 8, 128
SW_SCALE = PS ** -0.5
HF, JF = 16, 64
FT = HF * JF // P
DN = float(HD) ** -0.25
RATIO = float(JF) ** -0.5
EPS_FEAT, EPS_DEN, LN_EPS = 1e-4, 1e-2, 1e-5
EM, HID = 8, 512
HT = HID // P


class Slot:

    def __init__(self, ctx, nc, name, buf=None, step=1):
        self.name, self.buf, self.step = name, buf, step
        self.full = ctx.enter_context(nc.semaphore(f"full_{name}"))
        self.free = ctx.enter_context(nc.semaphore(f"free_{name}"))


class Use:

    def __init__(self, slot=None, nth=None):
        self.slot, self.nth = slot, nth

    @property
    def buf(self):
        return self.slot.buf

    @property
    def full(self):
        return self.slot.full

    @property
    def free(self):
        return self.slot.free


class Part:

    def __init__(self, name, rounds=1, base=0):
        self.name, self.rounds, self.base, self.steps, self.count = name, rounds, base, [], {}

    def use(self, slot):
        n = self.count.get(slot, 0)
        self.count[slot] = n + 1
        return Use(slot, n)

    def ring(self):
        return Use()

    def chain(self, slot, n):
        return [self.use(slot) for _ in range(n)]

    def step(self, engine, tick, what, rings=()):
        self.steps.append((tick, len(self.steps), engine, what, rings))

    def settle(self, ring_slots):
        self.steps.sort(key=lambda s: (s[0], s[1]))
        n = 0
        for _, _, _, _, rings in self.steps:
            for u in rings:
                got = self.use(ring_slots[n % len(ring_slots)])
                u.slot, u.nth = got.slot, got.nth
                n += 1


class Run:

    def __init__(self, eng, part, starts, i):
        self.eng, self.part, self.starts, self.i = eng, part, starts, i


    def nth(self, u):
        per = self.part.count[u.slot]
        return self.i * per + (self.starts.get(u.slot, 0) + u.nth)

    def claim(self, u):
        self.eng.wait_ge(u.free, self.nth(u) + 1)

    def ready(self, u):
        self.eng.wait_ge(u.full, (self.nth(u) + 1) * u.slot.step)

    def handed(self, slot):
        before = self.i * self.part.count[slot] + self.starts[slot]
        self.eng.wait_ge(slot.full, before * slot.step)

    def claim_apart(self, u, tally):
        self.claim(u)
        self.eng.sem_inc(tally.full, 1)

    def ready_apart(self, u, tally):
        self.ready(u)
        self.eng.sem_inc(tally.full, 1)

    def freed(self, slot):
        self.eng.wait_ge(slot.free, self.i * self.part.count.get(slot, 0) + (self.starts[slot] + 1))


class Links:

    def __init__(self, run, uses):
        self.run, self.uses, self.at = run, uses, 0

    def __call__(self, ins):
        u = self.uses[self.at]
        self.at += 1
        ins.then_inc(u.full, 1)
        self.run.ready(u)


def run_block(nc, parts, slots, ring_slots=()):
    starts, total = {}, {}
    for part in parts:
        part.settle(ring_slots)
        starts[part] = dict(total)
        for s, n in part.count.items():
            total[s] = total.get(s, 0) + n * part.rounds
    with nc.Block() as block:
        def program(name):
            def emit(eng):
                if name == "sync":
                    for s in slots:
                        eng.sem_inc(s.free, 1)
                for part in parts:
                    mine = [s for s in part.steps if s[2] == name]
                    if not mine:
                        continue
                    if part.rounds == 1:
                        r = Run(eng, part, starts[part], 0)
                        for s in mine:
                            s[3](r)
                    else:
                        with eng.Fori(0, part.rounds) as i:
                            r = Run(eng, part, starts[part], i)
                            for s in mine:
                                s[3](r)
            return emit

        block.sync(program("sync"))
        block.gpsimd(program("gpsimd"))
        block.scalar(program("scalar"))
        block.tensor(program("tensor"))
        block.vector(program("vector"))
    with nc.Block() as block:
        @block.gpsimd
        def _(eng):
            for s in slots:
                eng.sem_clear(s.full)
                eng.sem_clear(s.free)


def spread(ap, n):
    return ap.unsqueeze(len(ap.shape)).to_broadcast([*ap.shape, n])


class Block:

    def __init__(self, nc, ctx, name):
        self.nc, self.ctx, self.name, self.slots, self.parts, self.rings = nc, ctx, name, [], [], []

    def sbuf(self, name, shape, dt=F32):
        return self.ctx.enter_context(self.nc.sbuf_tensor(f"{self.name}_{name}", shape, dt))

    def psum(self, name, shape):
        return self.ctx.enter_context(self.nc.psum_tensor(f"{self.name}_{name}", shape, F32))

    def slot(self, name, shape=None, dt=F32, step=1):
        buf = self.sbuf(name, shape, dt) if shape else None
        return self.keep(Slot(self.ctx, self.nc, f"{self.name}_{name}", buf, step))

    def bank(self, name, shape):
        return self.keep(Slot(self.ctx, self.nc, f"{self.name}_{name}", self.psum(name, shape)))

    def keep(self, slot):
        self.slots.append(slot)
        return slot

    def ring(self, n, shape):
        self.rings = [self.bank(f"ring{k}", shape) for k in range(n)]

    def part(self, name, rounds=1, base=0):
        self.parts.append(Part(name, rounds, base))
        return self.parts[-1]

    def run(self):
        run_block(self.nc, self.parts, self.slots, self.rings)



def upper(eng, hi, src):
    return eng.tensor_copy(hi.bitcast(F32R), src)


def lower(eng, lo, src, hi):
    return eng.tensor_tensor(lo.bitcast(F32R), src, hi, ALU.subtract)


def matmul3(eng, out, w, x, start=True, stop=True):
    (wh, wl), (xh, xl) = ([t.bitcast(F32R) for t in pair] for pair in (w, x))
    eng.matmul(out, wh, xh, start=start, stop=False)
    eng.matmul(out, wh, xl, start=False, stop=False)
    return eng.matmul(out, wl, xh, start=False, stop=stop)


def layer_norm_stats(blk, part, tick, x, loaded):
    st = {"bn": blk.sbuf("bn", [P, NT, 6])} | {k: blk.sbuf(k, [P, NT]) for k in ("mean", "rstd", "va", "t1", "y")}
    chain = blk.slot("ln_chain")
    links = part.chain(chain, 7)
    sq, root, done = (part.use(blk.slot(f"ln_{k}")) for k in ("var", "root", "done"))
    bn, mean, rs, va, t1, y = (st[k] for k in ("bn", "mean", "rstd", "va", "t1", "y"))

    def moments(r):
        v, link = r.eng, Links(r, links)
        if loaded is not None:
            r.ready(loaded)
        for t in range(NT):
            last = v.bn_stats(bn[:, t, :], x[:, t, :])
        link(last)
        v.tensor_tensor(t1[:, :], bn[:, :, 1], bn[:, :, 4], ALU.subtract)
        v.tensor_tensor(va[:, :], bn[:, :, 2], bn[:, :, 5], ALU.add)
        link(v.tensor_tensor(mean[:, :], bn[:, :, 1], bn[:, :, 4], ALU.add))
        v.tensor_scalar(mean[:, :], mean[:, :], 0.5, None, ALU.mult)
        v.tensor_scalar(va[:, :], va[:, :], 1.0 / D, LN_EPS, ALU.mult, ALU.add)
        link(v.scalar_tensor_tensor(out=t1[:, :], in0=t1[:, :], scalar=0.25, in1=t1[:, :],
                                    op0=ALU.mult, op1=ALU.mult))
        v.tensor_tensor(va[:, :], va[:, :], t1[:, :], ALU.add).then_inc(sq.full, 1)

    def root_table(r):
        r.ready(sq)
        r.eng.activation(rs[:, :], va[:, :], ACT.Sqrt).then_inc(root.full, 1)

    def newton(r):
        v, link = r.eng, Links(r, links[3:])
        r.ready(root)
        link(v.reciprocal(y[:, :], rs[:, :]))
        link(v.tensor_tensor(t1[:, :], y[:, :], y[:, :], ALU.mult))
        link(v.scalar_tensor_tensor(out=t1[:, :], in0=t1[:, :], scalar=-0.5, in1=va[:, :],
                                    op0=ALU.mult, op1=ALU.mult))
        v.scalar_tensor_tensor(out=rs[:, :], in0=t1[:, :], scalar=1.5, in1=y[:, :],
                               op0=ALU.add, op1=ALU.mult).then_inc(done.full, 1)
        r.ready(done)
    part.step("vector", tick, moments)
    part.step("scalar", tick + 0.1, root_table)
    part.step("vector", tick + 0.2, newton)
    return st


TOP2_LINKS = 11


def top2(v, link, p, tmp, order):
    sel, c, q, m, first = (tmp[k] for k in ("sel", "c", "q", "m", "first"))
    g = m.shape[1]
    ob = order.unsqueeze(1).to_broadcast([P, g, 8])

    def choose(src, peak):
        link(v.tensor_reduce(peak, src, AX.X, ALU.max))
        link(v.tensor_tensor(c, src, spread(peak, 8), ALU.is_equal))
        link(v.tensor_tensor(c, c, ob, ALU.mult))
        link(v.tensor_reduce(m, c, AX.X, ALU.max))

    choose(p, first)
    link(v.tensor_tensor(sel, c, spread(m, 8), ALU.is_equal))
    link(v.scalar_tensor_tensor(out=q, in0=sel, scalar=-3.0e38, in1=p, op0=ALU.mult, op1=ALU.add))
    choose(q, tmp["second"])
    link(v.tensor_tensor(q, c, spread(m, 8), ALU.is_equal))
    return sel, q


def split_keys_or_queries(v, ready_hi, link, f, hi, minus_m1, minus_m2, out):
    ready_hi()
    link(v.scalar_tensor_tensor(out=f, in0=hi, scalar=minus_m1, in1=f, op0=ALU.mult, op1=ALU.add))
    link(v.tensor_copy(hi, f))
    return v.scalar_tensor_tensor(out=out, in0=hi, scalar=minus_m2, in1=f, op0=ALU.mult, op1=ALU.add)


def prepare0(nc, a, x, xnT, ident, order, w):
    with ExitStack() as ctx:
        blk = Block(nc, ctx, "p0")
        qw, kw = blk.sbuf("qw", [P, HS, D]), blk.sbuf("kw", [P, HS, D])
        selv, wk = blk.sbuf("selv", [D, 160]), blk.sbuf("wk", [D, 2, P])
        bv, bk = blk.sbuf("bv", [P, 32]), blk.sbuf("bk", [P, 2])
        route = blk.sbuf("route", [P, 1])
        loads_x, loads_w = blk.slot("loads_x", step=16), blk.slot("loads_w", step=16 * 9)
        eye = blk.slot("eye")
        xn = [blk.slot(f"xn{g}", [P, 4, D]) for g in range(2)]
        xs = [blk.slot(f"xs{g}", [P, 4 * P]) for g in range(2)]
        kf, kh = blk.slot("kf", [P, 2, 512]), blk.slot("kh", [P, 2, 512], BF16)
        v32, split, kept = blk.slot("v32"), blk.slot("split"), blk.slot("kept")
        turned = [blk.bank(f"turned{g}", [P, 512]) for g in range(2)]
        logits = blk.bank("logits", [P, 4, 256])
        keys = blk.bank("keys", [P, 2, 512])
        qk_ps = blk.bank("qk", [P, HS, P])

        first = blk.part("first")
        ux, uw, ue, uq = first.use(loads_x), first.use(loads_w), first.use(eye), first.use(qk_ps)

        def load(r):
            e = r.eng
            e.dma_start(x[:, :, :], a["x"].rearrange("(t p) d -> p t d", p=P)).then_inc(ux.full, 16)
            for dst, src in (
                (qw[:, :, :], a["q_w"].rearrange("(h p) d -> p h d", p=PS)),
                (kw[:, :, :], a["k_w"].rearrange("(h p) d -> p h d", p=PS)),
                (selv[:, :], a["selv"]), (wk[:, :, :], a["wk"]),
                (bv[:, :], a["bv"].partition_broadcast(P)), (bk[:, :], a["bk"]),
                (route[:, :], a["route"].partition_broadcast(P)),
                (order[:, :], a["order"].partition_broadcast(P)), (w["split"][:, :], a["split"]),
            ):
                e.dma_start(dst, src).then_inc(uw.full, 16)
        first.step("sync", 0, load)

        def eye_zero(r):
            r.eng.memset(ident[:, :], 0.0).then_inc(ue.full, 1)
            r.ready(ue)
            r.eng.affine_select(out=ident[:, :], in_=ident[:, :], compare_op=ALU.not_equal, fill=1.0,
                                base=0, pattern=[[-1, P]], channel_multiplier=1).then_inc(ue2.full, 1)
        ue2 = first.use(eye)
        first.step("gpsimd", 0, eye_zero)
        st = layer_norm_stats(blk, first, 0, x, ux)

        def heads(r):
            r.ready(uw)
            r.ready(ue2)
            for h in range(HS):
                last = r.eng.matmul(qk_ps.buf[:, h, :], qw[:, h, :], kw[:, h, :], start=True, stop=True)
            last.then_inc(uq.full, 1)

        def keep_heads(r):
            r.ready(uq)
            r.eng.activation(w["qk"][:, :, :], qk_ps.buf[:, :, :], ACT.Copy).then_inc(uq.free, 1)
        first.step("tensor", 0, heads)
        first.step("scalar", 0.5, keep_heads)
        first.step("scalar", 0.6, lambda r: r.ready(uw))
        first.step("vector", 0.6, lambda r: r.ready(uw))

        tally = blk.slot("tally")

        def four_tiles(tiles, g):
            def at(r):
                return (r.i + r.part.base) * 2 + g

            u = {n: tiles.use(s) for n, s in (
                ("xn", xn[g]), ("xs", xs[g]), ("kf", kf), ("kh", kh), ("v32", v32),
                ("turned", turned[g]), ("logits", logits), ("keys", keys), ("kept", kept))}
            slinks = tiles.chain(split, 2)

            def normalise(r):
                v = r.eng
                r.claim(u["xn"])
                for j in range(4):
                    last = v.tensor_scalar(u["xn"].buf[:, j, :], x[:, at(r) * 4 + j, :], st["mean"][:, bass.ds(at(r) * 4 + j, 1)],
                                           st["rstd"][:, bass.ds(at(r) * 4 + j, 1)], ALU.subtract, ALU.mult)
                last.then_inc(u["xn"].full, 1)
            tiles.step("vector", 0 + 0.5 * g, normalise)

            def turn(r):
                r.ready(u["xn"])
                r.claim(u["turned"])
                for j in range(4):
                    last = r.eng.transpose(u["turned"].buf[:, j * P:(j + 1) * P], u["xn"].buf[:, j, :], ident[:, :])
                last.then_inc(u["turned"].full, 1)
            tiles.step("tensor", 1 + 0.5 * g, turn)

            def keep_turned(r):
                r.ready(u["turned"])
                r.claim(u["xs"])
                r.eng.activation(u["xs"].buf[:, :], u["turned"].buf[:, :], ACT.Copy).then_inc(u["xs"].full, 1)
            tiles.step("scalar", 2 + 0.5 * g, keep_turned)

            def keep_xnT(r):
                r.ready_apart(u["xs"], tally)
                r.eng.tensor_copy(xnT[:, bass.ds(at(r) * 512, 512)], u["xs"].buf[:, :]).then_inc(u["kept"].full, 1)
            tiles.step("gpsimd", 3 + 0.5 * g, keep_xnT)

            def project(r):
                r.ready(u["xs"])
                r.claim(u["logits"])
                for j in range(4):
                    last = r.eng.matmul(logits.buf[:, j, 0:160], u["xs"].buf[:, j * P:(j + 1) * P], selv[:, :],
                                        start=True, stop=True)
                last.then_inc(u["logits"].full, 1)
                r.claim(u["keys"])
                for hh in range(2):
                    last = r.eng.matmul(keys.buf[:, hh, :], wk[:, hh, :], u["xs"].buf[:, :], start=True, stop=True)
                last.then_inc(u["keys"].full, 1)
            tiles.step("tensor", 4 + 0.5 * g, project)

            def keep_values(r):
                r.ready(u["logits"])
                r.eng.tensor_tensor(w["v32"][:, bass.ds(at(r) * 4, 4), :], logits.buf[:, :, 128:160],
                                    bv[:, :].unsqueeze(1).to_broadcast([P, 4, 32]), ALU.add)\
                    .then_inc(u["v32"].full, 1)
                r.eng.sem_inc(u["xn"].free, 1)
            tiles.step("vector", 5 + 0.5 * g, keep_values)

            def sigmoid_exps(r):
                r.ready(u["v32"])
                r.eng.sem_inc(u["turned"].free, 1)
                r.eng.activation(w["gate"][:, bass.ds(at(r) * 4, 4), :], logits.buf[:, :, 0:128], ACT.Exp,
                                 scale=-1.0).then_inc(u["logits"].free, 1)
                r.ready(u["keys"])
                r.claim(u["kf"])
                for hh in range(2):
                    r.eng.activation(kf.buf[:, hh, :], keys.buf[:, hh, :], ACT.Identity, bias=bk[:, hh:hh + 1])
                    last = r.eng.activation(kh.buf[:, hh, :], keys.buf[:, hh, :], ACT.Identity, bias=bk[:, hh:hh + 1])
                last.then_inc(u["kf"].full, 1)
            tiles.step("scalar", 6 + 0.5 * g, sigmoid_exps)

            def split_keys(r):
                v, link = r.eng, Links(r, slinks)
                split_keys_or_queries(
                    v, lambda: r.ready(u["kf"]), link, kf.buf[:, :, :], kh.buf[:, :, :], w["split"][:, 2:3],
                    w["split"][:, 3:4], w["ks"][:, :, bass.ds(at(r) * 512, 512)]).then_inc(u["kf"].free, 1)
                v.sem_inc(u["keys"].free, 1)
                r.ready(u["kept"])
                v.sem_inc(u["xs"].free, 1)
            tiles.step("vector", 7 + 0.5 * g, split_keys)

        tmp = {n: blk.sbuf(f"t2_{n}", [P, 128, 8]) for n in ("sel", "c", "q")} | {
            n: blk.sbuf(f"t2_{n}", [P, 128]) for n in ("m", "first", "second")}
        tmp = {k: (b[:, :, :] if len(b.shape) == 3 else b[:, :]) for k, b in tmp.items()}
        prob = blk.sbuf("t2_prob", [P, 128, 8])[:, :, :]
        gate_chain = blk.slot("gate_chain")

        def gates(part):
            glinks = part.chain(gate_chain, 2 + TOP2_LINKS + 7)

            def route_gates(r):
                v, link = r.eng, Links(r, glinks)
                r.freed(logits)
                flat = w["gate"][:, bass.ds((r.i + (r.part.base - 1)) * TPB, TPB), :].rearrange("p t (g e) -> p (t g) e", e=8)
                link(v.tensor_scalar(prob, flat, 1.0, None, ALU.add))
                link(v.reciprocal(prob, prob))
                one, other = top2(v, link, prob, tmp, order[:, :])
                link(v.tensor_tensor(one, one, other, ALU.add))
                link(v.tensor_tensor(one, one, prob, ALU.mult))
                link(v.tensor_reduce(tmp["m"], one, AX.X, ALU.add))
                link(v.tensor_scalar(tmp["m"], tmp["m"], 1e-9, None, ALU.max))
                link(v.reciprocal(tmp["m"], tmp["m"]))
                link(v.tensor_scalar(tmp["m"], tmp["m"], route[:, 0:1], None, ALU.mult))
                link(v.tensor_tensor(flat, one, spread(tmp["m"], 8), ALU.mult))
            part.step("vector", 0.8, route_gates)

        for part in (blk.part("tiles0"), blk.part("tiles", rounds=B - 1, base=1)):
            if part.base:
                gates(part)
            four_tiles(part, 0)
            four_tiles(part, 1)
        gates(blk.part("gates", base=B))
        blk.run()


TICKS = {
    "queries": (0.72,),
    "split": (0.91,),
    "peaks": (1.5, 2.058, 3, 4, 5, 6, 7, 8),
    "dpeaks": (0,),
    "values": (0.95, 2.529, 3.559, 4.588, 5.618, 6.647, 7.677, 8.706),
    "dvalues": (0.185,),
    "cut": (8.124,),
    "turn_peaks": (9.118,),
    "hand": (10.847,),
    "scores": (0.881, 1.264, 2.264, 3.264, 4.226, 5.006, 6.264, 7.264),
    "dlargest": (0.02,),
    "dsoftmax": (0.002,),
    "turn": (1.079, 2.079, 3.079, 4.079, 4.884, 6.079, 7.079, 8.079),
    "dturn": (0,),
    "weigh": (2.425, 3.425, 4.425, 5.425, 6.425, 7.425, 8.425, 9.425),
    "dweigh": (0.205,),
    "outputs": (4.25, 4.562, 6.33, 6.642, 8.594, 8.981, 11.282, 11.373),
    "doutputs": (0,),
    "scoresT": (0.631, 1.69, 2.749, 3.808, 4.867, 5.926, 6.985, 8.045),
    "dexps": (0,),
    "sums": (1.651, 2.712, 3.773, 4.834, 5.895, 6.956, 8.018, 9.21),
    "dsums": (0.01,),
    "turn_sums": (10.403,),
    "y": (9.042,),
    "hand_x": (10.296,),
    "halve_wv": (0.331,),
    "halve_wo": (1,),
    "dsum": (0.162,),
    "late": (0.3, 0.6),
    "halve_x": (-0.033,),
    "halve_wq": (-0.041,),
    "halve_qk": (0.479,),
}


def main0(nc, a, x, xnT, ident, w):
    with ExitStack() as ctx:
        blk = Block(nc, ctx, "m0")
        sb, slot = blk.sbuf, blk.slot
        bq = sb("bq", [P, H0 // 2])
        identb = sb("identb", [P, P], BF16)
        consts = slot("consts", step=16)
        eyeb = slot("eyeb")
        tally = slot("tally")
        wq, wqs = slot("wq", [D, P], step=16), slot("wqs", [D, 2, P])
        wraw = slot("wraw", [D, ES * PS], step=16)
        wvs = slot("wvs", [D, 2, ES * PS])
        wos = slot("wos", [PS, 2, ES * D])
        cut = {k: slot(f"cut_{k}") for k in ("wq", "wv", "wo", "x", "qk")}
        x_values, x_y = slot("x_values"), slot("x_y")
        xcur, xfin = slot("xcur", [D, 2, T]), slot("xfin", [D, 2, T])
        qf, qh = slot("qf", [P, T]), sb("qh", [P, T], BF16)
        qsplit = slot("qsplit")
        qnext, qcur = slot("qnext", [P, T], BF16), slot("qcur", [P, T], BF16)
        peaks = sb("peaks", [P, TPB, 2])
        mparts, mrest = slot("mparts", [P, TPB, 2, 3], BF16), sb("mrest", [P, TPB, 2])
        mchain, mrows = slot("mchain"), slot("mrows", [6, T], BF16)
        vnext, vcur = slot("vnext", [P, TPB, PS]), slot("vcur", [P, TPB, PS])
        qk, v32 = slot("qk", [D, 2, D]), slot("v32", [P, TPB, 32])
        yupper, yT = slot("yupper"), slot("yT", [D, 2, T])
        neg = [slot(f"neg{k}", [P, 1]) for k in range(2)]
        prob = [slot(f"prob{k}", [P, T]) for k in range(2)]
        den = sb("den", [P, TPB])
        probT = [slot(f"probT{k}", [P, TPB, 2 * P]) for k in range(2)]
        ctxT = [slot(f"ctxT{k}", [PS, 2, 2 * P]) for k in range(2)]
        cupper = slot("cupper")
        rden, go = slot("rden", [P, 2]), sb("go", [P, TPB, ES])
        expA = [slot(f"expA{k}", [P, T]) for k in range(2)]
        vprod, oprod = slot("vprod", [P, ES * P]), [slot(f"oprod{k}", [P, ES * P]) for k in range(2)]
        vchain, ochain = slot("vchain"), slot("ochain")
        sums = blk.bank("sums", [P, 512])
        ctx_ps = blk.bank("ctx", [P, 512])
        blk.ring(3, [P, T])

        at = TICKS

        def of(r, n_is):
            n = r.i + (r.part.base + n_is)
            return n // HS, n % HS

        def both(buf, cols=slice(None)):
            return buf[:, 0, cols], buf[:, 1, cols]

        def halve(part, tick, raw, halves, mid, src):
            m = part.use(mid)
            hi, lo = both(halves.buf)

            def make_upper(r):
                if raw is not None:
                    r.ready(raw)
                r.claim(halves)
                upper(r.eng, hi, src(r)).then_inc(m.full, 1)
            part.step("vector", tick, make_upper)

            def make_lower(r):
                r.ready_apart(m, tally)
                lower(r.eng, lo, src(r), hi).then_inc(halves.full, 1)
                if raw is not None:
                    r.ready(halves)
                    r.eng.sem_inc(raw.free, 1)
            part.step("gpsimd", tick + 0.001, make_lower)

        def halve_sum(r, buf, link):
            for n in (4 * P, 2 * P):
                link(r.eng.tensor_tensor(buf[:, 0:n], buf[:, 0:n], buf[:, n:2 * n], ALU.add))

        def begin(part, ahead):
            u = {k: part.use(s) for k, s in (
                ("wq", wq), ("wqs", wqs), ("wraw", wraw), ("wvs", wvs), ("xcur", xcur), ("qf", qf), ("qnext", qnext),
                ("mparts", mparts), ("vnext", vnext), ("qk", qk), ("yT", yT), ("yupper", yupper))}
            yps = part.ring()
            split_links, m_links = part.chain(qsplit, 2), part.chain(mchain, 4)
            qps = part.ring()

            def load(r):
                b, h = of(r, ahead)
                r.claim(u["wq"])
                r.eng.dma_start(wq.buf[:, :], a["wq"][bass.ds(h, 1), :, :].rearrange("h d m -> (h d) m"))\
                    .then_inc(u["wq"].full, 16)
                r.claim(u["wraw"])
                r.eng.dma_start(wraw.buf[:, :].rearrange("d (e p) -> d e p", e=ES),
                                a["v_w"][bass.ds(h * ES, ES), :, :].rearrange("e d p -> d e p"))\
                    .then_inc(u["wraw"].full, 16)
            part.step("sync", 0, load)

            def sequence(r):
                b, _ = of(r, ahead)
                return xnT[:, bass.ds(b * T, T)]

            def head_qk(r):
                _, h = of(r, ahead)
                return w["qk"][:, bass.ds(h, 1), :].rearrange("d h e -> d (h e)")
            halve(part, at["halve_x"][0], None, u["xcur"], cut["x"], sequence)
            halve(part, at["halve_wq"][0], u["wq"], u["wqs"], cut["wq"], lambda r: wq.buf[:, :])
            halve(part, at["halve_wv"][0], u["wraw"], u["wvs"], cut["wv"], lambda r: wraw.buf[:, :])
            halve(part, at["halve_qk"][0], None, u["qk"], cut["qk"], head_qk)

            def hand_x(r):
                r.claim(xf)
                r.ready(u["xcur"])
                for k in range(2):
                    last = r.eng.activation(xfin.buf[:, k, :].bitcast(F32R), xcur.buf[:, k, :], ACT.Copy)
                last.then_inc(xf.full, 1)
                r.ready(xf)
                r.ready(xread)
                r.ready(yread)
                r.eng.sem_inc(u["xcur"].free, 1)
            xf, xread, yread = part.use(xfin), part.use(x_values), part.use(x_y)
            part.step("scalar", at["hand_x"][0], hand_x)

            def make_y(r):
                r.ready(u["qk"])
                r.ready(u["xcur"])
                r.claim(yps)
                for c in range(2):
                    last = matmul3(r.eng, yps.buf[:, c * 512:(c + 1) * 512], both(qk.buf),
                                   both(xcur.buf, slice(c * 512, (c + 1) * 512)))
                last.then_inc(yps.full, 1)
            part.step("tensor", at["y"][0], make_y, [yps])

            def keep_y(r):
                r.ready(yps)
                r.eng.sem_inc(u["qk"].free, 1)
                r.eng.sem_inc(yread.full, 1)
                r.claim(u["yT"])
                r.eng.activation(yT.buf[:, 0, :].bitcast(F32R), yps.buf[:, :], ACT.Copy, scale=SW_SCALE)\
                    .then_inc(u["yupper"].full, 1)
            part.step("scalar", at["y"][0] + 0.01, keep_y)

            def halve_y(r):
                r.ready(u["yupper"])
                r.eng.scalar_tensor_tensor(out=yT.buf[:, 1, :].bitcast(F32R), in0=yps.buf[:, :], scalar=SW_SCALE,
                                           in1=yT.buf[:, 0, :], op0=ALU.mult, op1=ALU.subtract)\
                    .then_inc(u["yT"].full, 1)
                r.ready(u["yT"])
                r.eng.sem_inc(yps.free, 1)
            part.step("vector", at["y"][0] + 0.02, halve_y)

            def queries(r):
                r.ready(u["wqs"])
                r.ready(u["xcur"])
                r.claim(qps)
                for c in range(2):
                    last = matmul3(r.eng, qps.buf[:, c * 512:(c + 1) * 512], both(wqs.buf),
                                   both(xcur.buf, slice(c * 512, (c + 1) * 512)))
                last.then_inc(qps.full, 1)
            part.step("tensor", at["queries"][0], queries, [qps])

            def keep_queries(r):
                b, h = of(r, ahead)
                r.ready(qps)
                r.eng.sem_inc(u["wqs"].free, 1)
                r.claim(u["qf"])
                for out in (qf.buf, qh):
                    last = r.eng.activation(out[:, :], qps.buf[:, :], ACT.Identity, bias=bq[:, bass.ds(h, 1)],
                                            scale=HD ** -0.5)
                last.then_inc(qps.free, 1)
            part.step("scalar", at["queries"][0] + 0.01, keep_queries)

            def split_queries(r):
                v, link = r.eng, Links(r, split_links)

                def written():
                    v.wait_ge(qps.free, r.nth(qps) + 2)
                    r.claim(u["qnext"])
                split_keys_or_queries(v, written, link, qf.buf[:, :], qh[:, :], w["split"][:, 0:1],
                                      w["split"][:, 1:2], qnext.buf[:, :]).then_inc(u["qnext"].full, 1)
            part.step("vector", at["split"][0], split_queries)

            def free_qf(r):
                r.ready(u["qnext"])
                r.eng.sem_inc(u["qf"].free, 1)
            part.step("gpsimd", at["split"][0] + 0.01, free_qf)

            for t in range(TPB):
                for hh in range(2):
                    ps = part.ring()

                    def scores(r, t=t, hh=hh, ps=ps):
                        b, _ = of(r, ahead)
                        if t == 0 and hh == 0:
                            r.ready(u["qnext"])
                        r.claim(ps)
                        for c in range(2):
                            last = r.eng.matmul(ps.buf[:, c * 512:(c + 1) * 512],
                                                qnext.buf[:, t * P:(t + 1) * P],
                                                w["ks"][:, hh, bass.ds(b * T + c * 512, 512)],
                                                start=True, stop=True)
                        last.then_inc(ps.full, 1)
                    part.step("tensor", at["peaks"][t] + 0.1 * hh, scores, [ps])

                    def largest(r, t=t, hh=hh, ps=ps):
                        r.ready(ps)
                        r.eng.tensor_reduce(peaks[:, t, hh:hh + 1], ps.buf[:, :], AX.X, ALU.max)\
                            .then_inc(ps.free, 1)
                        if t == TPB - 1 and hh == 1:
                            r.eng.wait_ge(ps.free, r.nth(ps) + 2)
                    part.step("vector", at["peaks"][t] + 0.1 * hh + at["dpeaks"][0], largest)

                vps = part.ring()

                def values(r, t=t, vps=vps):
                    if t == 0:
                        r.ready(u["wvs"])
                        r.ready(u["xcur"])
                    r.claim(vps)
                    for c in range(2):
                        last = matmul3(r.eng, vps.buf[:, c * 512:(c + 1) * 512],
                                       both(xcur.buf, slice(t * P, (t + 1) * P)),
                                       both(wvs.buf, slice(c * 512, (c + 1) * 512)))
                    last.then_inc(vps.full, 1)
                part.step("tensor", at["values"][t], values, [vps])

                vp, links = part.use(vprod), part.chain(vchain, 2)

                def gate_values(r, t=t, vps=vps, vp=vp):
                    b, h = of(r, ahead)
                    r.ready(vps)
                    r.claim(vp)
                    gate = w["gate"][:, bass.ds(b * TPB + t, 1), bass.ds(h * ES, ES)]\
                        .rearrange("p o e -> p (o e)")
                    r.eng.tensor_tensor(vprod.buf[:, :].rearrange("p (e d) -> p e d", e=ES),
                                        vps.buf[:, :].rearrange("p (e d) -> p e d", e=ES),
                                        spread(gate, P), ALU.mult).then_inc(vp.full, 1)
                    if t == TPB - 1:
                        r.eng.sem_inc(u["wvs"].free, 1)
                        r.eng.sem_inc(xread.full, 1)
                    r.ready(vp)
                    r.eng.sem_inc(vps.free, 1)
                part.step("vector", at["values"][t] + at["dvalues"][0], gate_values)

                def sum_values(r, t=t, vp=vp, links=links):
                    r.ready(vp)
                    if t == 0:
                        r.claim(u["vnext"])
                    halve_sum(r, vprod.buf, Links(r, links))
                    r.eng.tensor_tensor(vnext.buf[:, t, :], vprod.buf[:, 0:P], vprod.buf[:, P:2 * P], ALU.add)\
                        .then_inc(vp.free, 1)
                    if t == TPB - 1:
                        r.eng.wait_ge(vp.free, r.nth(vp) + 2)
                        r.eng.sem_inc(u["vnext"].full, 1)
                part.step("gpsimd", at["values"][t] + at["dvalues"][0] + at["dsum"][0], sum_values)

            def cut_peaks(r):
                v, link = r.eng, Links(r, m_links)
                r.claim(u["mparts"])
                mp = mparts.buf
                link(v.tensor_scalar(mrest[:, :, :], peaks[:, :, :], -1.0, None, ALU.mult))
                link(v.tensor_copy(mp[:, :, :, 0], mrest[:, :, :]))
                link(v.tensor_tensor(mrest[:, :, :], mrest[:, :, :], mp[:, :, :, 0], ALU.subtract))
                link(v.tensor_copy(mp[:, :, :, 1], mrest[:, :, :]))
                v.tensor_tensor(mp[:, :, :, 2], mrest[:, :, :], mp[:, :, :, 1], ALU.subtract)\
                    .then_inc(u["mparts"].full, 1)
            part.step("vector", at["cut"][0], cut_peaks)
            mps = part.ring()

            def turn_peaks(r):
                r.ready(u["mparts"])
                r.claim(mps)
                rows = mps.buf[:, 0:512].bitcast(BF16)
                for t in range(TPB):
                    last = r.eng.transpose(rows[0:6, t * P:(t + 1) * P],
                                           mparts.buf[:, t, :, :].rearrange("p h c -> p (h c)"), identb[:, :])
                last.then_inc(mps.full, 1)
            part.step("tensor", at["turn_peaks"][0], turn_peaks, [mps])

            mr = part.use(mrows)

            def keep_peaks(r):
                r.ready(mps)
                r.eng.sem_inc(u["mparts"].free, 1)
                r.claim(mr)
                r.eng.activation(mrows.buf[:, :], mps.buf[0:6, 0:512].bitcast(BF16), ACT.Copy).then_inc(mr.full, 1)
                r.ready(mr)
                r.eng.sem_inc(mps.free, 1)
            part.step("scalar", at["turn_peaks"][0] + 0.01, keep_peaks)

            qc, vc = part.use(qcur), part.use(vcur)

            def hand_queries(r):
                r.claim(qc)
                r.eng.tensor_copy(qcur.buf[0:96, :], qnext.buf[0:96, :])
                r.ready(mr)
                r.eng.tensor_copy(qcur.buf[96:102, :], mrows.buf[:, :]).then_inc(qc.full, 1)
                r.ready(qc)
                r.eng.sem_inc(mr.free, 1)
                r.eng.sem_inc(u["qnext"].free, 1)
            part.step("vector", at["hand"][0], hand_queries)

            def hand_values(r):
                r.claim(vc)
                r.ready(u["vnext"])
                r.eng.activation(vcur.buf[:, :, :], vnext.buf[:, :, :], ACT.Copy).then_inc(vc.full, 1)
                r.ready(vc)
                r.eng.sem_inc(u["vnext"].free, 1)
            part.step("scalar", 11, hand_values)

        def output(part, tt, tick, n_is, ready_ctx):
            ops, pr, links = part.ring(), part.use(oprod[tt % 2]), part.chain(ochain, 3)
            ct = ctxT[(tt // 2) % 2]

            def outputs(r):
                ready_ctx(r)
                r.claim(ops)
                for c in range(2):
                    last = matmul3(r.eng, ops.buf[:, c * 512:(c + 1) * 512],
                                   both(ct.buf, slice((tt % 2) * P, (tt % 2 + 1) * P)),
                                   both(wos.buf, slice(c * 512, (c + 1) * 512)))
                last.then_inc(ops.full, 1)
            part.step("tensor", tick, outputs, [ops])

            def gate_outputs(r):
                r.ready(ops)
                if tt % 2:
                    r.eng.sem_inc(ct.free, 1)
                if tt == TPB - 1:
                    r.eng.sem_inc(wos.free, 1)
                r.claim(pr)
                r.eng.tensor_tensor(pr.buf[:, :].rearrange("p (e d) -> p e d", e=ES),
                                    ops.buf[:, :].rearrange("p (e d) -> p e d", e=ES),
                                    spread(go[:, tt, :], P), ALU.mult).then_inc(pr.full, 1)
                r.ready(pr)
                r.eng.sem_inc(ops.free, 1)
            part.step("vector", tick + at["doutputs"][0], gate_outputs)

            def sum_outputs(r):
                b, _ = of(r, n_is)
                link = Links(r, links)
                r.ready(pr)
                halve_sum(r, pr.buf, link)
                link(r.eng.tensor_tensor(pr.buf[:, 0:P], pr.buf[:, 0:P], pr.buf[:, P:2 * P], ALU.add))
                r.eng.sem_inc(tally.full, 1)
                xt = x[:, bass.ds(b * TPB + tt, 1), :].rearrange("p o d -> p (o d)")
                r.eng.tensor_tensor(xt, xt, pr.buf[:, 0:P], ALU.add).then_inc(pr.free, 1)
            part.step("gpsimd", tick + at["doutputs"][0] + at["dsum"][0], sum_outputs)

        def finish_last_tiles(part):
            def ready_ctx(r):
                r.handed(ctxT[1])
                r.handed(wos)
            for k, tt in enumerate((TPB - 2, TPB - 1)):
                output(part, tt, at["late"][k], -1, ready_ctx)

        def finish(part, ahead=True):
            u = {k: part.use(s) for k, s in (
                ("wraw", wraw), ("wos", wos), ("v32", v32), ("sums", sums))}
            def load(r):
                _, h = of(r, 0)
                r.claim(u["wraw"])
                r.eng.dma_start(wraw.buf[:, :].rearrange("p (e d) -> p e d", e=ES),
                                a["o_w"][bass.ds(h * ES, ES), :, :].rearrange("e p d -> p e d"))\
                    .then_inc(u["wraw"].full, 16)
            part.step("sync", 0, load)

            def copies(r):
                b, h = of(r, 0)
                r.claim_apart(u["v32"], tally)
                r.eng.tensor_copy(v32.buf[:, :, :], w["v32"][:, bass.ds(b * TPB, TPB), :])\
                    .then_inc(u["v32"].full, 1)
            part.step("gpsimd", 0, copies)

            halve(part, at["halve_wo"][0], u["wraw"], u["wos"], cut["wo"], lambda r: wraw.buf[:, :])

            for t in range(TPB):
                ps, ng, pb = part.ring(), part.use(neg[t % 2]), part.use(prob[t % 2])

                def scores(r, t=t, ps=ps):
                    b, _ = of(r, 0)
                    if t == 0:
                        wait_handed(r, yT)
                        wait_handed(r, xfin)
                    r.claim(ps)
                    for c in range(2):
                        last = matmul3(r.eng, ps.buf[:, c * 512:(c + 1) * 512],
                                       both(yT.buf, slice(t * P, (t + 1) * P)),
                                       both(xfin.buf, slice(c * 512, (c + 1) * 512)))
                    last.then_inc(ps.full, 1)
                part.step("tensor", at["scores"][t], scores, [ps])

                def largest(r, t=t, ps=ps, ng=ng):
                    r.ready(ps)
                    r.claim(ng)
                    r.eng.tensor_reduce(ng.buf[:, :], ps.buf[:, :], AX.X, ALU.max, negate=True)\
                        .then_inc(ng.full, 1)
                part.step("vector", at["scores"][t] + at["dlargest"][0], largest)

                def softmax(r, t=t, ps=ps, ng=ng, pb=pb):
                    r.ready(ng)
                    r.claim(pb)
                    r.eng.activation(pb.buf[:, :], ps.buf[:, :], ACT.Exp, bias=ng.buf[:, :],
                                     accum_out=den[:, t:t + 1]).then_inc(pb.full, 1)
                    r.ready(pb)
                    r.eng.sem_inc(ps.free, 1)
                    r.eng.sem_inc(ng.free, 1)
                    if t == TPB - 1:
                        r.eng.sem_inc(yT.free, 1)
                        r.eng.sem_inc(xfin.free, 1)
                part.step("scalar", at["scores"][t] + at["dsoftmax"][0], softmax)

                tps = part.ring()
                if t % 2 == 0:
                    pT = part.use(probT[(t // 2) % 2])

                def turn(r, tps=tps, pb=pb):
                    r.ready(pb)
                    r.claim(tps)
                    for c in range(TPB):
                        last = r.eng.transpose(tps.buf[:, c * P:(c + 1) * P], pb.buf[:, c * P:(c + 1) * P],
                                               ident[:, :])
                    last.then_inc(tps.full, 1)
                part.step("tensor", at["turn"][t], turn, [tps])

                def keep_turned(r, t=t, tps=tps, pT=pT, pb=pb):
                    r.ready(tps)
                    r.eng.sem_inc(pb.free, 1)
                    if t % 2 == 0:
                        r.claim(pT)
                    r.eng.activation(pT.buf[:, :, (t % 2) * P:(t % 2 + 1) * P],
                                           tps.buf[:, :].rearrange("p (c q) -> p c q", c=TPB), ACT.Copy)\
                        .then_inc(tps.free, 1)
                    if t % 2:
                        r.eng.wait_ge(tps.free, r.nth(tps) + 2)
                        r.eng.sem_inc(pT.full, 1)
                part.step("scalar", at["turn"][t] + at["dturn"][0], keep_turned)

                if t % 2:
                    g = t // 2
                    cp, ct = part.use(ctx_ps), part.use(ctxT[g % 2])
                    rd = part.use(rden)
                    cr = part.use(cupper)

                    def weigh(r, g=g, pT=pT, cp=cp):
                        if g == 0:
                            wait_handed(r, vcur)
                        r.ready(pT)
                        r.claim(cp)
                        for k in range(TPB):
                            last = r.eng.matmul(cp.buf[:, 0:2 * P], vcur.buf[:, k, :], pT.buf[:, k, :],
                                                start=(k == 0), stop=(k == TPB - 1))
                        last.then_inc(cp.full, 1)
                    part.step("tensor", at["weigh"][t], weigh)

                    def keep_ctx(r, g=g, pT=pT, cp=cp, cr=cr, ct=ct):
                        r.ready(cp)
                        r.eng.sem_inc(pT.free, 1)
                        if g == TPB // 2 - 1:
                            r.eng.sem_inc(vcur.free, 1)
                        r.claim(ct)
                        r.eng.activation(ct.buf[:, 0, :].bitcast(F32R), cp.buf[:, 0:2 * P], ACT.Copy)\
                            .then_inc(cr.full, 1)
                    part.step("scalar", at["weigh"][t] + at["dweigh"][0], keep_ctx)

                    def halve_ctx(r, cp=cp, cr=cr, ct=ct):
                        r.ready(cr)
                        lower(r.eng, ct.buf[:, 1, :], cp.buf[:, 0:2 * P], ct.buf[:, 0, :]).then_inc(ct.full, 1)
                        r.ready(ct)
                        r.eng.sem_inc(cp.free, 1)
                    part.step("vector", at["weigh"][t] + at["dweigh"][0] + 0.001, halve_ctx)

                    def output_gates(r, g=g, rd=rd, pb=pb):
                        b, h = of(r, 0)
                        r.ready(pb)
                        r.eng.reciprocal(rden.buf[:, :], den[:, 2 * g:2 * g + 2]).then_inc(rd.full, 1)
                        r.ready(rd)
                        r.eng.tensor_tensor(go[:, 2 * g:2 * g + 2, :],
                                            w["gate"][:, bass.ds(b * TPB + 2 * g, 2), bass.ds((h + HS) * ES, ES)],
                                            spread(rden.buf[:, :], ES), ALU.mult).then_inc(rd.free, 1)
                        r.eng.wait_ge(rd.free, r.nth(rd) + 2)
                    part.step("vector", at["weigh"][t] + 0.05, output_gates)

                    if g < TPB // 2 - 1 or not ahead:
                        for tt in (t - 1, t):
                            def ready_ctx(r, tt=tt, ct=ct):
                                if tt == 0:
                                    r.ready(u["wos"])
                                r.ready(ct)
                            output(part, tt, at["outputs"][tt], 0, ready_ctx)

            for k in range(TPB):
                es = []
                for hh in range(2):
                    ps, e = part.ring(), part.use(expA[hh])
                    es.append(e)

                    def scoresT(r, k=k, hh=hh, ps=ps):
                        b, _ = of(r, 0)
                        if k == 0 and hh == 0:
                            wait_handed(r, qcur)
                        r.claim(ps)
                        for c in range(2):
                            last = r.eng.matmul(ps.buf[:, c * 512:(c + 1) * 512],
                                                w["ks"][:, hh, bass.ds(b * T + k * P, P)],
                                                qcur.buf[:, c * 512:(c + 1) * 512], start=True, stop=True)
                        last.then_inc(ps.full, 1)
                    part.step("tensor", at["scoresT"][k] + 0.2 * hh, scoresT, [ps])

                    def exps(r, k=k, hh=hh, ps=ps, e=e):
                        r.ready(ps)
                        if k == TPB - 1 and hh == 1:
                            r.eng.sem_inc(qcur.free, 1)
                        r.claim(e)
                        r.eng.activation(e.buf[:, :], ps.buf[:, :], ACT.Exp).then_inc(e.full, 1)
                        r.ready(e)
                        r.eng.sem_inc(ps.free, 1)
                    part.step("scalar", at["scoresT"][k] + 0.2 * hh + at["dexps"][0], exps)

                def sum_values(r, k=k, es=es):
                    if k == 0:
                        r.ready(u["v32"])
                        r.claim(u["sums"])
                    for e in es:
                        r.ready(e)
                    for hh in range(2):
                        for c in range(2):
                            j = 2 * hh + c
                            last = r.eng.matmul(sums.buf[32 * j:32 * j + 32, :], v32.buf[:, k, :],
                                                es[hh].buf[:, c * 512:(c + 1) * 512],
                                                start=(k == 0), stop=(k == TPB - 1))
                            if c == 1:
                                last.then_inc(es[hh].free, 1)
                part.step("tensor", at["sums"][k], sum_values)

            st = part.use(expA[1])
            sumsT = st.buf[:, 0:512]

            def keep_sums(r):
                r.claim(st)
                r.eng.sem_inc(u["v32"].free, 1)
                r.eng.activation(sumsT, sums.buf[:, :], ACT.Copy).then_inc(st.full, 1)
                r.ready(st)
                r.eng.sem_inc(u["sums"].free, 1)
            part.step("scalar", at["sums"][TPB - 1] + at["dsums"][0], keep_sums)
            sps = part.ring()

            def turn_sums(r):
                r.ready(st)
                r.claim(sps)
                for s in range(4):
                    last = r.eng.transpose(sps.buf[:, s * P:(s + 1) * P], sumsT[:, s * P:(s + 1) * P],
                                           ident[:, :])
                last.then_inc(sps.full, 1)
            part.step("tensor", at["turn_sums"][0], turn_sums, [sps])

            def keep_o(r):
                b, h = of(r, 0)
                r.ready(sps)
                r.eng.sem_inc(st.free, 1)
                v = sps.buf[:, 0:512].rearrange("p (s h c k) -> p h c s k", s=4, h=2, c=2)
                for hh in range(2):
                    for c in range(2):
                        ins = r.eng.activation(
                            w["o_all"][:, bass.ds(b * TPB + c * 4, 4), bass.ds(h * 2 + hh, 1), :]
                            .rearrange("p s o k -> p s (o k)"), v[:, hh, c, :, 0:HD + 1], ACT.Copy)
                ins.then_inc(sps.free, 1)
            part.step("scalar", at["turn_sums"][0] + 0.01, keep_o)

        def wait_handed(r, slot):
            r.eng.wait_ge(slot.full, r.i + (r.part.base + 1))

        first = blk.part("first")
        uc = first.use(consts)
        ub = [first.use(eyeb) for _ in range(2)]
        first.step("sync", -1, lambda r: r.eng.dma_start(bq[:, :], a["bq"]).then_inc(uc.full, 16))

        def eye_b(r):
            r.eng.memset(qcur.buf[96:128, :], 0.0)
            r.eng.tensor_copy(identb[:, :], ident[:, :]).then_inc(ub[0].full, 1)
        first.step("vector", -1, eye_b)

        def scale_bias(r):
            r.ready(uc)
            r.eng.tensor_scalar(bq[:, :], bq[:, :], HD ** -0.5, None, ALU.mult).then_inc(ub[1].full, 1)
        first.step("vector", -0.9, scale_bias)
        first.step("scalar", -1, lambda r: r.ready(ub[1]))
        first.step("tensor", -1, lambda r: r.ready(ub[0]))
        begin(first, 0)
        opening = blk.part("opening")
        begin(opening, 1)
        finish(opening)
        loop = blk.part("loop", rounds=B * HS - 2, base=1)
        begin(loop, 1)
        finish_last_tiles(loop)
        finish(loop)
        last = blk.part("last", base=B * HS - 1)
        finish_last_tiles(last)
        finish(last, ahead=False)
        blk.run()


def close0(nc, a, x, ident, w):
    with ExitStack() as ctx:
        blk = Block(nc, ctx, "c0")
        half = T // H0
        wo, bo = blk.sbuf("wo", [P, D]), blk.sbuf("bo", [1, D])
        ones = blk.sbuf("ones", [1, P])
        loads = blk.slot("loads", step=32)
        rden = blk.slot("rden", [P, TPB, H0])
        o = blk.slot("o", [P, H0 // 2, TPB, 2, HD])
        oT = blk.slot("oT", [P, half, H0])
        turned = blk.bank("turned", [P, T])
        out = blk.bank("out", [P, TPB, D])

        first = blk.part("first")
        ul, u1 = first.use(loads), first.use(rden)

        def load(r):
            r.eng.dma_start(wo[:, :], a["wo"]).then_inc(ul.full, 16)
            r.eng.dma_start(bo[:, :], a["bo"].unsqueeze(0)).then_inc(ul.full, 16)
        first.step("sync", 0, load)
        first.step("vector", 0, lambda r: r.eng.memset(ones[:, :], 1.0).then_inc(u1.full, 1))

        def wait_consts(r):
            r.ready(ul)
            r.ready(u1)
        first.step("tensor", 0, wait_consts)

        loop = blk.part("loop", rounds=B)
        u = {k: loop.use(s) for k, s in (("rden", rden), ("o", o), ("oT", oT), ("turned", turned), ("out", out))}

        def divide(r):
            v = r.eng
            tiles = w["o_all"][:, bass.ds(r.i * TPB, TPB), :, :]
            v.reciprocal(rden.buf[:, :, :], tiles[:, :, :, HD]).then_inc(u["rden"].full, 1)
            r.ready(u["rden"])
            r.claim(u["o"])
            for side in range(2):
                rows = slice(side * half, (side + 1) * half)
                for odd in range(2):
                    last = v.tensor_tensor(
                        o.buf[odd * half:(odd + 1) * half, :, :, side, :],
                        w["o_all"][rows, bass.ds(r.i * TPB, TPB), odd::2, 0:HD].rearrange("p t h k -> p h t k"),
                        spread(rden.buf[rows, :, odd::2].rearrange("p t h -> p h t"), HD), ALU.mult)
            last.then_inc(u["o"].full, 1)
        loop.step("vector", 0, divide)

        def turn(r):
            r.ready(u["o"])
            r.claim(u["turned"])
            for h in range(H0 // 2):
                last = r.eng.transpose(turned.buf[:, h * P:(h + 1) * P],
                                       o.buf[:, h, :, :, :].rearrange("u t s k -> u (t s k)"), ident[:, :])
            last.then_inc(u["turned"].full, 1)
        loop.step("tensor", 1, turn)

        def keep(r):
            r.ready(u["turned"])
            r.eng.sem_inc(u["o"].free, 1)
            r.claim(u["oT"])
            r.eng.activation(oT.buf[:, :, :], turned.buf[:, :].rearrange("p (h u) -> p u h", h=H0), ACT.Copy)\
                .then_inc(u["oT"].full, 1)
            r.ready(u["oT"])
            r.eng.sem_inc(u["turned"].free, 1)
        loop.step("scalar", 2, keep)

        def project(r):
            r.ready(u["oT"])
            r.claim(u["out"])
            for t in range(TPB):
                r.eng.matmul(out.buf[:, t, :], ones[:, :], bo[:, :], start=True, stop=False)
                last = r.eng.matmul(out.buf[:, t, :],
                                    oT.buf[:, t * P // H0:(t + 1) * P // H0, :].rearrange("p u h -> p (u h)"),
                                    wo[:, :], start=False, stop=True)
            last.then_inc(u["out"].full, 1)
        loop.step("tensor", 3, project)

        def add(r):
            r.ready(u["out"])
            r.eng.sem_inc(u["oT"].free, 1)
            xt = x[:, bass.ds(r.i * TPB, TPB), :]
            r.eng.tensor_tensor(xt, xt, out.buf[:, :, :], ALU.add).then_inc(u["out"].free, 1)
        loop.step("vector", 4, add)
        blk.run()


def prepare1(nc, a, x, xnT, ident, order, w):
    with ExitStack() as ctx:
        blk = Block(nc, ctx, "p1")
        gw, gb = blk.sbuf("gw", [D, EM]), blk.sbuf("gb", [P, EM])
        lg = blk.sbuf("lg", [P, NT, EM])
        loads = blk.slot("loads", step=32)
        xn = [blk.slot(f"xn{g}", [P, 4, D]) for g in range(2)]
        xs = [blk.slot(f"xs{g}", [P, 4 * P]) for g in range(2)]
        kept, lgs = blk.slot("kept"), blk.slot("lgs")
        turned = [blk.bank(f"turned{g}", [P, 512]) for g in range(2)]
        logits = blk.bank("logits", [P, 4, EM])

        first = blk.part("first")
        ul = first.use(loads)

        def load(r):
            r.eng.dma_start(gw[:, :], a["gate_w"]).then_inc(ul.full, 16)
            r.eng.dma_start(gb[:, :], a["gate_b"].partition_broadcast(P)).then_inc(ul.full, 16)
        first.step("sync", 0, load)
        w1 = blk.sbuf("w1", [D, EM + 1, HID])
        ue, uh = first.use(blk.slot("experts", step=16 * 4)), blk.slot("w1_upper")

        def load_experts(r):
            for dst, src in (
                (w1[:, 0:EM, :], a["w1"].rearrange("e d h -> d e h")), (w1[:, EM, :], a["ws1"]),
                (w["w2"][:, :, :, :], a["w2"].rearrange("e (t p) d -> p e t d", p=P)),
            ):
                r.eng.dma_start(dst, src).then_inc(ue.full, 16)
            r.eng.dma_start(w["b1"][:, :, :], a["b1"].rearrange("e (t p) -> p e t", p=P),
                            allow_slow_non_contiguous=True).then_inc(ue.full, 16)
        first.step("sync", 1, load_experts)
        first.step("tensor", 0, lambda r: r.ready(ul))
        first.step("vector", 0, lambda r: r.ready(ul))
        st = layer_norm_stats(blk, first, 0, x, None)

        tally = blk.slot("tally")

        def four_tiles(tiles, g):
            def at(r):
                return r.i * 2 + g

            u = {n: tiles.use(s) for n, s in (("xn", xn[g]), ("xs", xs[g]), ("turned", turned[g]), ("logits", logits),
                                              ("kept", kept))}

            def normalise(r):
                r.claim(u["xn"])
                for j in range(4):
                    t = at(r) * 4 + j
                    last = r.eng.tensor_scalar(u["xn"].buf[:, j, :], x[:, t, :], st["mean"][:, bass.ds(t, 1)],
                                               st["rstd"][:, bass.ds(t, 1)], ALU.subtract, ALU.mult)
                last.then_inc(u["xn"].full, 1)
            tiles.step("vector", 0 + 0.5 * g, normalise)

            def turn(r):
                r.ready(u["xn"])
                r.claim(u["turned"])
                for j in range(4):
                    last = r.eng.transpose(u["turned"].buf[:, j * P:(j + 1) * P], u["xn"].buf[:, j, :], ident[:, :])
                last.then_inc(u["turned"].full, 1)
            tiles.step("tensor", 1 + 0.5 * g, turn)

            def keep_turned(r):
                r.ready(u["turned"])
                r.eng.sem_inc(u["xn"].free, 1)
                r.claim(u["xs"])
                r.eng.activation(u["xs"].buf[:, :], u["turned"].buf[:, :], ACT.Copy).then_inc(u["xs"].full, 1)
                r.ready(u["xs"])
                r.eng.sem_inc(u["turned"].free, 1)
            tiles.step("scalar", 2 + 0.5 * g, keep_turned)

            def keep_xnT(r):
                r.ready_apart(u["xs"], tally)
                r.eng.tensor_copy(xnT[:, bass.ds(at(r) * 512, 512)], u["xs"].buf[:, :]).then_inc(u["kept"].full, 1)
            tiles.step("gpsimd", 3 + 0.5 * g, keep_xnT)

            def route(r):
                r.ready(u["xs"])
                r.claim(u["logits"])
                for j in range(4):
                    last = r.eng.matmul(logits.buf[:, j, :], u["xs"].buf[:, j * P:(j + 1) * P], gw[:, :],
                                        start=True, stop=True)
                last.then_inc(u["logits"].full, 1)
            tiles.step("tensor", 4 + 0.5 * g, route)

            def keep_logits(r):
                r.ready(u["logits"])
                r.eng.tensor_tensor(lg[:, bass.ds(at(r) * 4, 4), :], logits.buf[:, :, :],
                                    gb[:, :].unsqueeze(1).to_broadcast([P, 4, EM]), ALU.add)\
                    .then_inc(u["logits"].free, 1)
                r.ready(u["kept"])
                r.eng.sem_inc(u["xs"].free, 1)
            tiles.step("vector", 5 + 0.5 * g, keep_logits)

        tiles = blk.part("tiles", rounds=B)
        four_tiles(tiles, 0)
        four_tiles(tiles, 1)

        mix = blk.part("mix")
        tmp = {n: blk.sbuf(f"t2_{n}", [P, NT, 8])[:, :, :] for n in ("sel", "c", "q")} | {
            n: blk.sbuf(f"t2_{n}", [P, NT])[:, :] for n in ("m", "first", "second")}
        chain = mix.chain(blk.slot("mix"), TOP2_LINKS + 6)
        e, e_of = mix.use(lgs), mix.use(blk.slot("exps"))

        def choose(r):
            v, link = r.eng, Links(r, chain)
            r.freed(logits)
            one, other = top2(v, link, lg[:, :, :], tmp, order[:, :])
            link(v.tensor_tensor(one, one, other, ALU.add))
            link(v.tensor_tensor(lg[:, :, :], lg[:, :, :], spread(tmp["first"], 8), ALU.subtract))
            v.sem_inc(e.full, 1)
            r.ready(e_of)
            link(v.tensor_tensor(lg[:, :, :], lg[:, :, :], one, ALU.mult))
            link(v.tensor_reduce(tmp["m"], lg[:, :, :], AX.X, ALU.add))
            link(v.reciprocal(tmp["m"], tmp["m"]))
            link(v.tensor_tensor(w["combine"][:, :, 0:EM], lg[:, :, :], spread(tmp["m"], 8), ALU.mult))
            v.memset(w["combine"][:, :, EM:EM + 1], 1.0)

        def exps(r):
            r.ready(e)
            r.eng.activation(lg[:, :, :], lg[:, :, :], ACT.Exp).then_inc(e_of.full, 1)
        uh = mix.use(uh)

        def upper_w1(r):
            r.eng.wait_ge(ue.full, ue.slot.step)
            upper(r.eng, w["w1"][:, 0, :, :], w1[:, :, :]).then_inc(uh.full, 1)

        def lower_w1(r):
            r.ready(uh)
            lower(r.eng, w["w1"][:, 1, :, :], w1[:, :, :], w["w1"][:, 0, :, :])
        mix.step("vector", -1, upper_w1)
        mix.step("gpsimd", -1, lower_w1)
        mix.step("vector", 0, choose)
        mix.step("scalar", 0, exps)
        blk.run()


def main1(nc, a, x, xnT, ident, w):
    with ExitStack() as ctx:
        blk = Block(nc, ctx, "m1")
        sb, slot = blk.sbuf, blk.slot
        wqT, wkT, wvT, woT = (sb(n, [D, D]) for n in ("wqT", "wkT", "wvT", "woT"))
        bqk, bv, bo = sb("bqk", [P, 2]), sb("bv", [P, D]), sb("bo", [1, D])
        proj, half = sb("proj", [P, HF * JF]), sb("half", [P, HF])
        vmask = sb("vmask", [P, 18])
        eps, ones, ones_rows = sb("eps", [P, 1]), sb("ones", [1, P]), sb("ones_rows", [HF, P])
        w1, b1, w2, b2 = w["w1"], w["b1"], w["w2"], sb("b2", [EM + 1, D])
        n_loads = 11
        loads = slot("loads", step=16 * n_loads)
        consts, tally = slot("consts"), slot("tally")
        xcur = slot("xcur", [D, T])
        xhalf, xupper = slot("xhalf", [D, 2, 512]), slot("xupper")
        kT, k2 = slot("kT", [P, T]), slot("k2", [P, T])
        diag, peaks = slot("diag", [P, TPB, HF]), sb("peaks", [P, TPB, HF])
        dd = slot("dd", [P, TPB, HF * JF])
        stab, stab_in, stab_d = slot("stab"), sb("stab_in", [P, HF]), sb("stab_d", [HF, HF + 1])
        shift = slot("shift", [P, TPB, HF])
        vext = slot("vext", [P, TPB, FT, 18])
        kp = [slot(f"kp{k}", [P, HF * JF]) for k in range(2)]
        kpe = slot("kpe")
        kv = slot("kv", [P, FT, 18])
        qd = [slot(f"qd{k}", [P, HF * JF]) for k in range(2)]
        qsub, qmax = slot("qsub", [P, HF]), slot("qmax", [P, HF])
        qe = [slot(f"qe{k}") for k in range(2)]
        qpT = [slot(f"qpT{k}", [P, FT, P]) for k in range(2)]
        oden, o1 = slot("oden", [P, FT, 2]), slot("o1", [P, 4, D])
        o1T = slot("o1T", [P, 4 * P])
        hT = [slot(f"hT{k}", [P, HT, 512]) for k in range(2)]
        mixed = [slot(f"mixed{k}", [P, 4, D]) for k in range(2)]
        cT = slot("cT", [EM + 1, 512])
        cmb, biased = slot("cmb", [P, 4, EM + 1]), slot("biased", [P, 4, D])
        attn = slot("attn", [P, 512])
        kpx = [slot(f"kpx{k}") for k in range(2)]
        ochain = slot("ochain")
        ones16 = ones_rows[:, :]
        kv_ps, small = blk.bank("kv_sums", [P, FT, 18]), blk.bank("small", [P, 512])
        blk.ring(3, [P, T])

        first = blk.part("first")
        ul, uc = first.use(loads), [first.use(consts)]

        def load(r):
            for dst, src in (
                (wqT, a["wqT"]), (wkT, a["wkT"]), (wvT, a["wvT"]), (woT, a["woT"]), (bqk, a["bqk"]),
                (bv, a["bv1"].partition_broadcast(P)), (bo, a["bo1"].unsqueeze(0)), (proj, a["proj"]),
                (half, a["half"]), (vmask, a["vmask"]), (b2, a["b2"]),
            ):
                r.eng.dma_start(dst[:, :], src).then_inc(ul.full, 16)

        first.step("sync", 0, load)

        def constants(r):
            v = r.eng
            v.memset(eps[:, :], EPS_FEAT)
            v.memset(ones[:, :], 1.0)
            v.memset(ones_rows[:, :], 1.0)
            v.memset(vext.buf[:, :, :, 16:18], 1.0)
            r.ready(ul)
            v.tensor_scalar(bqk[:, :], bqk[:, :], DN, None, ALU.mult).then_inc(uc[0].full, 1)
            r.ready(uc[0])
        first.step("vector", 0, constants)

        def wait_consts(r):
            r.ready(ul)
            r.ready(uc[0])
        for engine in ("tensor", "scalar", "gpsimd"):
            first.step(engine, 0, wait_consts)

        loop = blk.part("loop", rounds=B)
        buffers = locals()
        performer(loop, buffers)
        experts(loop, buffers)
        blk.run()


TICKS1 = {
    "values": (0.1,),
    "kside": (0.064,),
    "kkeep": (-0.022,),
    "ksquare": (0.233,),
    "khalf": (0.333,),
    "kdiag": (0.957,),
    "kfeat": (1.347, 1.947, 2.547, 3.147, 3.747, 4.57, 4.947, 4.958),
    "dkfeat": (0.1,),
    "dkmax": (0.12,),
    "stab": (6.53,),
    "takeoff": (7.189, 7.816, 8.443, 8.55, 9.742, 10.324, 10.951, 11.577),
    "dkexp": (0,),
    "dkeps": (0.2,),
    "dksum": (0.534,),
    "kv": (11.944,),
    "qside": (6.745,),
    "qdiag": (7.204,),
    "qfeat": (11.297, 12.318, 12.707, 13.562, 14.184, 14.805, 15.427, 16.049),
    "dqstab": (0.134,),
    "dqexp": (0.163,),
    "qturn": (12.33, 12.93, 13.53, 14.13, 14.73, 15.33, 15.93, 16.53),
    "dqeps": (0.1,),
    "qweigh": (12.723, 13.323, 13.923, 14.523, 15.123, 15.919, 16.323, 16.923),
    "dqdiv": (0,),
    "oturn": (12.984, 13.584, 14.184, 14.784, 15.384, 15.984, 16.584, 17.184),
}
TICKS2 = {
    "hidden": (0.05, 1.05, 2.05, 3.05, 4.05, 5.05, 6.05, 7.05, 8.05, 9.05, 10.05, 11.05, 12.05, 13.05, 14.05, 15.05, 16.05, 17.05),
    "hidden2": (0.25, 1.25, 2.25, 3.25, 4.25, 5.25, 6.146, 7.25, 8.25, 9.25, 10.25, 11.25, 12.25, 13.25, 14.25, 15.25, 16.25, 17.25),
    "dgelu": (0.056,),
    "output": (1.15, 2.115, 3.081, 4.046, 5.011, 5.976, 6.942, 7.907, 8.872, 9.837, 10.803, 11.768, 12.733, 13.698, 14.664, 15.629, 16.707, 17.559),
    "dcomb": (0.126,),
    "bias": (0.5, 9.919),
    "xhalf": (-0.05, 8.9),
}


def performer(part, n):
    xnT, x, ident = (n[k] for k in ("xnT", "x", "ident"))
    u = {k: part.use(n[k]) for k in ("xcur", "diag", "dd", "shift", "vext", "kv", "kv_ps")}

    def copy_x(r):
        r.claim_apart(u["xcur"], n["tally"])
        r.eng.tensor_copy(n["xcur"].buf[:, :], xnT[:, bass.ds(r.i * T, T)]).then_inc(u["xcur"].full, 1)
    part.step("gpsimd", 0, copy_x)

    vps = part.ring()

    def values(r):
        r.ready(u["xcur"])
        r.claim(vps)
        for t in range(TPB):
            last = r.eng.matmul(vps.buf[:, t * P:(t + 1) * P], n["xcur"].buf[:, t * P:(t + 1) * P],
                                n["wvT"][:, :], start=True, stop=True)
        last.then_inc(vps.full, 1)
    part.step("tensor", TICKS1["values"][0], values, [vps])

    def keep_values(r):
        r.ready(vps)
        r.claim(u["vext"])
        for t in range(TPB):
            last = r.eng.tensor_tensor(
                n["vext"].buf[:, t, :, 0:16], vps.buf[:, t * P:(t + 1) * P].rearrange("p (f k) -> p f k", f=FT),
                n["bv"][:, :].rearrange("p (f k) -> p f k", f=FT), ALU.add)
        last.then_inc(vps.free, 1)
        r.eng.wait_ge(vps.free, r.nth(vps) + 2)
        r.eng.sem_inc(u["vext"].full, 1)
    part.step("vector", TICKS1["values"][0] + 0.01, keep_values)

    def side(tick, weights, col):
        ps, t, sq, dps = part.ring(), part.use(n["kT"]), part.use(n["k2"]), part.use(n["small"])

        def product(r):
            r.ready(u["xcur"])
            r.claim(ps)
            for c in range(2):
                last = r.eng.matmul(ps.buf[:, c * 512:(c + 1) * 512], n[weights][:, :],
                                    n["xcur"].buf[:, c * 512:(c + 1) * 512], start=True, stop=True)
            last.then_inc(ps.full, 1)
        part.step("tensor", tick, product, [ps])

        def keep(r):
            r.ready(ps)
            if col == 0:
                r.eng.sem_inc(u["xcur"].free, 1)
            r.claim(t)
            r.eng.activation(n["kT"].buf[:, :], ps.buf[:, :], ACT.Identity, bias=n["bqk"][:, col:col + 1],
                             scale=DN).then_inc(t.full, 1)
            r.ready(t)
            r.eng.sem_inc(ps.free, 1)
        part.step("scalar", tick + TICKS1["kkeep"][0], keep)

        def square(r):
            r.ready(t)
            r.claim(sq)
            r.eng.tensor_tensor(n["k2"].buf[:, :], n["kT"].buf[:, :], n["kT"].buf[:, :], ALU.mult)\
                .then_inc(sq.full, 1)
        part.step("gpsimd", tick + TICKS1["ksquare"][0], square)

        def half_sums(r):
            r.ready(sq)
            r.claim(dps)
            for k in range(TPB):
                last = r.eng.matmul(n["small"].buf[:, k * HF:(k + 1) * HF], n["k2"].buf[:, k * P:(k + 1) * P],
                                    n["half"][:, :], start=True, stop=True)
            last.then_inc(dps.full, 1)
        part.step("tensor", tick + TICKS1["khalf"][0], half_sums)
        return t, sq, dps

    kt, k2, kd = side(TICKS1["kside"][0], "wkT", 1)
    dg = u["diag"]

    def keep_diag(r):
        r.ready(kd)
        r.eng.sem_inc(k2.free, 1)
        r.claim(dg)
        r.eng.activation(n["diag"].buf[:, :, :], n["small"].buf[:, 0:P].rearrange("p (t h) -> p t h", t=TPB),
                         ACT.Copy).then_inc(dg.full, 1)
        r.ready(dg)
        r.eng.sem_inc(kd.free, 1)
    part.step("scalar", TICKS1["kdiag"][0], keep_diag)

    for t in range(TPB):
        ps, at = part.ring(), TICKS1["kfeat"][t]

        def features(r, t=t, ps=ps):
            if t == 0:
                r.ready(kt)
            r.claim(ps)
            for c in range(2):
                last = r.eng.matmul(ps.buf[:, c * 512:(c + 1) * 512], n["kT"].buf[:, t * P:(t + 1) * P],
                                    n["proj"][:, c * 512:(c + 1) * 512], start=True, stop=True)
            last.then_inc(ps.full, 1)
        part.step("tensor", at, features, [ps])

        kept = part.use(n["kpe"])

        def keep_features(r, t=t, ps=ps, kept=kept):
            r.ready(ps)
            if t == 0:
                r.claim(u["dd"])
            if t == TPB - 1:
                r.eng.sem_inc(kt.free, 1)
            r.eng.activation(n["dd"].buf[:, t, :], ps.buf[:, :], ACT.Copy).then_inc(kept.full, 1)
            r.ready(kept)
            r.eng.sem_inc(ps.free, 1)
        part.step("scalar", at + TICKS1["dkfeat"][0], keep_features)

        def largest(r, t=t, kept=kept):
            r.ready(kept)
            ins = r.eng.tensor_reduce(n["peaks"][:, t, :], n["dd"].buf[:, t, :].rearrange("p (h j) -> p h j", h=HF),
                                      AX.X, ALU.max)
            if t == TPB - 1:
                ins.then_inc(u["dd"].full, 1)
        part.step("vector", at + TICKS1["dkmax"][0], largest)

    s = [part.use(n["stab"]) for _ in range(3)]
    sp, sp2 = part.ring(), part.ring()
    at = TICKS1["stab"][0]

    def over_tiles(r):
        r.ready(u["dd"])
        r.eng.tensor_reduce(n["stab_in"][:, :], n["peaks"][:, :, :].rearrange("p t h -> p h t"), AX.X, ALU.max)\
            .then_inc(s[0].full, 1)
    part.step("vector", at, over_tiles)

    def turn_stab(r):
        r.ready(s[0])
        r.claim(sp)
        r.eng.transpose(sp.buf[0:HF, 0:P], n["stab_in"][:, :], ident[:, :]).then_inc(sp.full, 1)
    part.step("tensor", at + 0.1, turn_stab, [sp])

    def over_tokens(r):
        r.ready(sp)
        r.eng.tensor_reduce(n["stab_d"][:, HF:HF + 1], sp.buf[0:HF, 0:P], AX.X, ALU.max).then_inc(s[1].full, 1)
        r.ready(s[1])
        r.eng.sem_inc(sp.free, 1)
        r.eng.tensor_scalar(n["stab_d"][:, 0:HF], ident[0:HF, 0:HF], n["stab_d"][:, HF:HF + 1], None, ALU.mult)\
            .then_inc(s[2].full, 1)
    part.step("vector", at + 0.2, over_tokens)

    def to_all(r):
        r.ready(s[2])
        r.claim(sp2)
        r.eng.matmul(sp2.buf[:, 0:HF], n["ones16"], n["stab_d"][:, 0:HF], start=True, stop=True)\
            .then_inc(sp2.full, 1)
    part.step("tensor", at + 0.3, to_all, [sp2])

    def make_shift(r):
        r.ready(sp2)
        r.ready(dg)
        r.claim(u["shift"])
        r.eng.tensor_tensor(n["shift"].buf[:, :, :], n["diag"].buf[:, :, :],
                            sp2.buf[:, 0:HF].unsqueeze(1).to_broadcast([P, TPB, HF]), ALU.add)\
            .then_inc(u["shift"].full, 1)
        r.ready(u["shift"])
        r.eng.sem_inc(sp2.free, 1)
        r.eng.sem_inc(dg.free, 1)
    part.step("vector", at + 0.4, make_shift)

    for t in range(TPB):
        at = TICKS1["takeoff"][t]
        kp, ex = part.use(n["kp"][t % 2]), part.use(n["kpx"][t % 2])

        def take_off(r, t=t, kp=kp, ex=ex):
            if t == 0:
                r.ready(u["shift"])
            r.claim(kp)
            r.eng.tensor_tensor(kp.buf[:, :].rearrange("p (h j) -> p h j", h=HF),
                                n["dd"].buf[:, t, :].rearrange("p (h j) -> p h j", h=HF),
                                spread(n["shift"].buf[:, t, :], JF), ALU.subtract).then_inc(ex.full, 1)

        def exps(r, kp=kp, ex=ex):
            r.ready(ex)
            r.eng.activation(kp.buf[:, :], kp.buf[:, :], ACT.Exp).then_inc(ex.free, 1)

        def plus_eps(r, t=t, kp=kp, ex=ex):
            r.eng.wait_ge(ex.free, r.nth(ex) + 2)
            if t == TPB - 1:
                r.eng.sem_inc(u["dd"].free, 1)
                r.eng.sem_inc(u["shift"].free, 1)
            r.eng.tensor_scalar(kp.buf[:, :], kp.buf[:, :], RATIO, EPS_FEAT, ALU.mult, ALU.add)\
                .then_inc(kp.full, 1)

        def sum_keys(r, t=t, kp=kp):
            r.ready(kp)
            if t == 0:
                r.ready(u["vext"])
                r.claim(u["kv_ps"])
            for f in range(FT):
                last = r.eng.matmul(n["kv_ps"].buf[:, f, :], kp.buf[:, f * P:(f + 1) * P],
                                    n["vext"].buf[:, t, f, :], start=(t == 0 and f == 0),
                                    stop=(t == TPB - 1), skip_group_check=True)
            last.then_inc(kp.free, 1)

        part.step("gpsimd", at, take_off)
        part.step("scalar", at + TICKS1["dkexp"][0], exps)
        part.step("vector", at + TICKS1["dkeps"][0], plus_eps)
        part.step("tensor", at + TICKS1["dksum"][0], sum_keys)

    last_kp = kp

    def keep_kv(r):
        r.eng.wait_ge(last_kp.free, r.nth(last_kp) + 2)
        r.eng.sem_inc(u["vext"].free, 1)
        r.claim(u["kv"])
        r.eng.tensor_tensor(n["kv"].buf[:, :, :], n["kv_ps"].buf[:, :, :],
                            n["vmask"][:, :].unsqueeze(1).to_broadcast([P, FT, 18]), ALU.mult)\
            .then_inc(u["kv"].full, 1)
        r.ready(u["kv"])
        r.eng.sem_inc(u["kv_ps"].free, 1)
    part.step("vector", TICKS1["kv"][0], keep_kv)

    qt, q2, qg = side(TICKS1["qside"][0], "wqT", 0)
    dq = part.use(n["diag"])

    def keep_diag_q(r):
        r.ready(qg)
        r.eng.sem_inc(q2.free, 1)
        r.claim(dq)
        r.eng.activation(n["diag"].buf[:, :, :], n["small"].buf[:, 0:P].rearrange("p (t h) -> p t h", t=TPB),
                         ACT.Copy).then_inc(dq.full, 1)
        r.ready(dq)
        r.eng.sem_inc(qg.free, 1)
    part.step("scalar", TICKS1["qdiag"][0], keep_diag_q)

    for t in range(TPB):
        ps, at = part.ring(), TICKS1["qfeat"][t]
        qd, qx, mx, sbt = part.use(n["qd"][t % 2]), part.use(n["qe"][t % 2]), part.use(n["qmax"]), part.use(n["qsub"])
        tp, qT, op = part.ring(), part.use(n["qpT"][t % 2]), part.use(n["small"])
        od = part.use(n["oden"])
        if t % 4 == 0:
            o1 = part.use(n["o1"])
        ochain = [part.use(n["ochain"]) for _ in range(2)]

        def features(r, t=t, ps=ps):
            if t == 0:
                r.ready(qt)
            r.claim(ps)
            for c in range(2):
                last = r.eng.matmul(ps.buf[:, c * 512:(c + 1) * 512], n["kT"].buf[:, t * P:(t + 1) * P],
                                    n["proj"][:, c * 512:(c + 1) * 512], start=True, stop=True)
            last.then_inc(ps.full, 1)
        part.step("tensor", at, features, [ps])

        def stabilise(r, t=t, ps=ps, qd=qd, mx=mx, sbt=sbt):
            v = r.eng
            r.ready(ps)
            if t == 0:
                r.ready(dq)
            if t == TPB - 1:
                v.sem_inc(qt.free, 1)
            view = ps.buf[:, :].rearrange("p (h j) -> p h j", h=HF)
            v.tensor_reduce(n["qmax"].buf[:, :], view, AX.X, ALU.max).then_inc(mx.full, 1)
            r.ready(mx)
            v.tensor_tensor(n["qsub"].buf[:, :], n["qmax"].buf[:, :], n["diag"].buf[:, t, :], ALU.add)\
                .then_inc(sbt.full, 1)
            r.ready(sbt)
            if t == TPB - 1:
                v.sem_inc(dq.free, 1)
            r.claim(qd)
            v.tensor_tensor(qd.buf[:, :].rearrange("p (h j) -> p h j", h=HF), view,
                            spread(n["qsub"].buf[:, :], JF), ALU.subtract).then_inc(qd.full, 1)
            r.ready(qd)
            v.sem_inc(ps.free, 1)
        part.step("vector", at + TICKS1["dqstab"][0], stabilise)

        def exps(r, qd=qd, qx=qx):
            r.ready(qd)
            r.eng.activation(qd.buf[:, :], qd.buf[:, :], ACT.Exp).then_inc(qx.full, 1)
        part.step("scalar", at + TICKS1["dqexp"][0], exps)

        def turn(r, qd=qd, qx=qx, tp=tp):
            r.ready(qx)
            r.claim(tp)
            for f in range(FT):
                last = r.eng.transpose(tp.buf[:, f * P:(f + 1) * P], qd.buf[:, f * P:(f + 1) * P], ident[:, :])
            last.then_inc(tp.full, 1)
        part.step("tensor", TICKS1["qturn"][t], turn, [tp])

        def plus_eps(r, qd=qd, tp=tp, qT=qT):
            r.ready(tp)
            r.eng.sem_inc(qd.free, 1)
            r.claim(qT)
            r.eng.activation(qT.buf[:, :, :], tp.buf[:, :].rearrange("p (f q) -> p f q", f=FT), ACT.Identity,
                             bias=n["eps"][:, :], scale=RATIO).then_inc(qT.full, 1)
            r.ready(qT)
            r.eng.sem_inc(tp.free, 1)
        part.step("scalar", TICKS1["qturn"][t] + TICKS1["dqeps"][0], plus_eps)

        def weigh(r, t=t, qT=qT, op=op):
            if t == 0:
                r.ready(u["kv"])
            r.ready(qT)
            r.claim(op)
            for f in range(FT):
                last = r.eng.matmul(n["small"].buf[:, f * 18:(f + 1) * 18], qT.buf[:, f, :], n["kv"].buf[:, f, :],
                                    start=True, stop=True)
            last.then_inc(op.full, 1)
        part.step("tensor", TICKS1["qweigh"][t], weigh)

        def divide(r, t=t, qT=qT, op=op, od=od, o1=o1, ochain=ochain):
            v, link = r.eng, Links(r, ochain)
            r.ready(op)
            v.sem_inc(qT.free, 1)
            if t == TPB - 1:
                v.sem_inc(u["kv"].free, 1)
            got = n["small"].buf[:, 0:FT * 18].rearrange("p (f k) -> p f k", f=FT)
            link(v.tensor_scalar(n["oden"].buf[:, :, :], got[:, :, 16:18], EPS_DEN, None, ALU.max))
            link(v.reciprocal(n["oden"].buf[:, :, :], n["oden"].buf[:, :, :]))
            if t % 4 == 0:
                r.claim(o1)
            v.tensor_tensor(n["o1"].buf[:, t % 4, :].rearrange("p (f h k) -> p f h k", f=FT, h=2),
                            got[:, :, 0:16].rearrange("p f (h k) -> p f h k", h=2),
                            spread(n["oden"].buf[:, :, :], HD), ALU.mult).then_inc(op.free, 1)
            if t % 4 == 3:
                v.wait_ge(op.free, r.nth(op) + 2)
                v.sem_inc(o1.full, 1)
        part.step("vector", TICKS1["qweigh"][t] + TICKS1["dqdiv"][0], divide)

        if t % 4 == 3:
            t1, oT, t2 = part.ring(), part.use(n["o1T"]), part.ring()

            def turn_o(r, o1=o1, t1=t1):
                r.ready(o1)
                r.claim(t1)
                for k in range(4):
                    last = r.eng.transpose(t1.buf[:, k * P:(k + 1) * P], n["o1"].buf[:, k, :], ident[:, :])
                last.then_inc(t1.full, 1)
            part.step("tensor", TICKS1["oturn"][t], turn_o, [t1])

            def keep_oT(r, o1=o1, t1=t1, oT=oT):
                r.ready(t1)
                r.eng.sem_inc(o1.free, 1)
                r.claim(oT)
                r.eng.activation(n["o1T"].buf[:, :], t1.buf[:, 0:512], ACT.Copy).then_inc(oT.full, 1)
                r.ready(oT)
                r.eng.sem_inc(t1.free, 1)
            part.step("scalar", TICKS1["oturn"][t] + 0.05, keep_oT)

            def project(r, oT=oT, t2=t2):
                r.ready(oT)
                r.claim(t2)
                for k in range(4):
                    r.eng.matmul(t2.buf[:, k * P:(k + 1) * P], n["ones"][:, :], n["bo"][:, :], start=True, stop=False)
                    last = r.eng.matmul(t2.buf[:, k * P:(k + 1) * P], n["o1T"].buf[:, k * P:(k + 1) * P],
                                        n["woT"][:, :], start=False, stop=True)
                last.then_inc(t2.full, 1)
            part.step("tensor", TICKS1["oturn"][t] + 0.10, project, [t2])

            mx2 = part.use(n["attn"])

            def keep_out(r, oT=oT, t2=t2, mx2=mx2):
                r.ready(t2)
                r.eng.sem_inc(oT.free, 1)
                r.claim(mx2)
                r.eng.activation(n["attn"].buf[:, :], t2.buf[:, 0:512], ACT.Copy).then_inc(mx2.full, 1)
                r.ready(mx2)
                r.eng.sem_inc(t2.free, 1)
            part.step("scalar", TICKS1["oturn"][t] + 0.15, keep_out)

            def add(r, t=t, mx2=mx2):
                r.ready_apart(mx2, n["tally"])
                xt = x[:, bass.ds(r.i * TPB + (t - 3), 4), :].rearrange("p t d -> p (t d)")
                r.eng.tensor_tensor(xt, xt, n["attn"].buf[:, :], ALU.add).then_inc(mx2.free, 1)
                r.eng.wait_ge(mx2.free, r.nth(mx2) + 2)
            part.step("gpsimd", TICKS1["oturn"][t] + 0.20, add)


def experts(part, n):
    xnT, x, w, ident = (n[k] for k in ("xnT", "x", "w", "ident"))
    for blkn in range(2):
        xh, xu = part.use(n["xhalf"]), part.use(n["xupper"])

        def upper_x(r, blkn=blkn, xh=xh, xu=xu):
            r.claim(xh)
            r.eng.activation(xh.buf[:, 0, :].bitcast(F32R), xnT[:, bass.ds(r.i * T + blkn * 512, 512)], ACT.Copy)\
                .then_inc(xu.full, 1)

        def lower_x(r, blkn=blkn, xh=xh, xu=xu):
            r.ready_apart(xu, n["tally"])
            lower(r.eng, xh.buf[:, 1, :], xnT[:, bass.ds(r.i * T + blkn * 512, 512)], xh.buf[:, 0, :])\
                .then_inc(xh.full, 1)
        part.step("scalar", TICKS2["xhalf"][blkn], upper_x)
        part.step("gpsimd", TICKS2["xhalf"][blkn] + 0.001, lower_x)

        for e in range(EM + 1):
            at = [(TICKS2[k][9 * blkn + e] if len(TICKS2[k]) > 1 else TICKS2[k][0]) for k in ("hidden", "hidden2", "output", "dgelu", "dcomb")]
            hT = part.use(n["hT"][e % 2])
            hps = [part.ring() for _ in range(2)]

            def hidden(r, e=e, k=0, ps=None, xh=xh):
                if e == 0 and k == 0:
                    r.ready(xh)
                r.claim(ps)
                for c in range(2):
                    cols = slice((2 * k + c) * P, (2 * k + c + 1) * P)
                    last = matmul3(r.eng, ps.buf[:, c * 512:(c + 1) * 512],
                                   (n["w1"][:, 0, e, cols], n["w1"][:, 1, e, cols]),
                                   (xh.buf[:, 0, :], xh.buf[:, 1, :]))
                last.then_inc(ps.full, 1)

            def gelu(r, e=e, k=0, ps=None, hT=hT, xh=xh):
                r.ready(ps)
                if k == 0:
                    r.claim(hT)
                for c in range(2):
                    last = r.eng.activation(hT.buf[:, 2 * k + c, :], ps.buf[:, c * 512:(c + 1) * 512], ACT.Gelu,
                                            bias=n["b1"][:, e, 2 * k + c:2 * k + c + 1])
                last.then_inc(ps.free, 1)
                if k == 1:
                    r.eng.wait_ge(ps.free, r.nth(ps) + 2)
                    r.eng.sem_inc(hT.full, 1)
                    if e == EM:
                        r.eng.sem_inc(xh.free, 1)
            for k in range(2):
                part.step("tensor", at[k], partial(hidden, k=k, ps=hps[k]), [hps[k]])
                part.step("scalar", at[k] + at[3], partial(gelu, k=k, ps=hps[k]))

            ops, mx = part.ring(), part.use(n["mixed"][e % 2])

            def output(r, e=e, hT=hT, ops=ops):
                r.ready(hT)
                r.claim(ops)
                for t in range(4):
                    for k in range(HT):
                        last = r.eng.matmul(ops.buf[:, t * P:(t + 1) * P], hT.buf[:, k, t * P:(t + 1) * P],
                                            n["w2"][:, e, k, :], start=(k == 0), stop=(k == HT - 1))
                last.then_inc(ops.full, 1)
            part.step("tensor", at[2], output, [ops])

            def combine(r, e=e, blkn=blkn, hT=hT, ops=ops, mx=mx):
                r.ready(ops)
                r.eng.sem_inc(hT.free, 1)
                r.claim(mx)
                weights = w["combine"][:, bass.ds(r.i * TPB + 4 * blkn, 4), e]
                r.eng.tensor_tensor(mx.buf[:, :, :], ops.buf[:, 0:512].rearrange("p (t d) -> p t d", t=4),
                                    spread(weights, D), ALU.mult).then_inc(mx.full, 1)
                r.ready(mx)
                r.eng.sem_inc(ops.free, 1)
            part.step("vector", at[2] + at[4], combine)

            def add(r, blkn=blkn, mx=mx):
                r.ready_apart(mx, n["tally"])
                xt = x[:, bass.ds(r.i * TPB + 4 * blkn, 4), :]
                r.eng.tensor_tensor(xt, xt, mx.buf[:, :, :], ALU.add).then_inc(mx.free, 1)
                r.eng.wait_ge(mx.free, r.nth(mx) + 2)
            part.step("gpsimd", at[2] + at[4] + 0.05, add)

        at = TICKS2["bias"][blkn]
        cps, cT, bps = part.ring(), part.use(n["cT"]), part.ring()

        cm = part.use(n["cmb"])

        def turn(r, cps=cps, cm=cm):
            r.ready(cm)
            r.claim(cps)
            for t in range(4):
                last = r.eng.transpose(cps.buf[0:EM + 1, t * P:(t + 1) * P], n["cmb"].buf[:, t, :], ident[:, :])
            last.then_inc(cps.full, 1)

        def copy_combine(r, blkn=blkn, cm=cm):
            r.claim_apart(cm, n["tally"])
            r.eng.tensor_copy(n["cmb"].buf[:, :, :], w["combine"][:, bass.ds(r.i * TPB + 4 * blkn, 4), :])\
                .then_inc(cm.full, 1)
        part.step("gpsimd", at - 0.01, copy_combine)
        part.step("tensor", at, turn, [cps])

        def keep(r, cps=cps, cT=cT, cm=cm):
            r.ready(cps)
            r.eng.sem_inc(cm.free, 1)
            r.claim(cT)
            r.eng.activation(n["cT"].buf[:, :], cps.buf[0:EM + 1, 0:512], ACT.Copy).then_inc(cT.full, 1)
            r.ready(cT)
            r.eng.sem_inc(cps.free, 1)
        part.step("scalar", at + 0.01, keep)

        def biases(r, cT=cT, bps=bps):
            r.ready(cT)
            r.claim(bps)
            for t in range(4):
                last = r.eng.matmul(bps.buf[:, t * P:(t + 1) * P], n["cT"].buf[:, t * P:(t + 1) * P], n["b2"][:, :],
                                    start=True, stop=True)
            last.then_inc(bps.full, 1)
        part.step("tensor", at + 0.02, biases, [bps])
        bb = part.use(n["biased"])

        def keep_biases(r, cT=cT, bps=bps, bb=bb):
            r.ready(bps)
            r.eng.sem_inc(cT.free, 1)
            r.claim(bb)
            r.eng.activation(n["biased"].buf[:, :, :], bps.buf[:, 0:512].rearrange("p (t d) -> p t d", t=4), ACT.Copy)\
                .then_inc(bb.full, 1)
            r.ready(bb)
            r.eng.sem_inc(bps.free, 1)
        part.step("scalar", at + 0.03, keep_biases)

        def add(r, blkn=blkn, bb=bb):
            r.ready_apart(bb, n["tally"])
            xt = x[:, bass.ds(r.i * TPB + 4 * blkn, 4), :]
            r.eng.tensor_tensor(xt, xt, n["biased"].buf[:, :, :], ALU.add).then_inc(bb.free, 1)
            r.eng.wait_ge(bb.free, r.nth(bb) + 2)
        part.step("gpsimd", at + 0.04, add)


def build(nc, a):
    with ExitStack() as whole:
        def keep(name, shape, dt=F32):
            return whole.enter_context(nc.sbuf_tensor(name, shape, dt))

        x = keep("x", [P, NT, D])
        xnT = keep("xnT", [P, B * T])
        ident = keep("ident", [P, P])
        order = keep("order", [P, 8])
        with ExitStack() as l0:
            def keep0(name, shape, dt=F32):
                return l0.enter_context(nc.sbuf_tensor(name, shape, dt))
            w = {
                "gate": keep0("gate", [P, NT, 2 * HS * ES]),
                "ks": keep0("ks", [P, 2, B * T], BF16),
                "split": keep0("split", [P, 4]),
                "v32": keep0("v32", [P, NT, 32]),
                "qk": keep0("qk", [P, HS, P]),
                "o_all": keep0("o_all", [P, NT, H0, HD + 1]),
            }
            prepare0(nc, a, x, xnT, ident, order, w)
            main0(nc, a, x, xnT, ident, w)
            close0(nc, a, x, ident, w)

        with ExitStack() as l1:
            w = {k: l1.enter_context(nc.sbuf_tensor(k, shape, F32)) for k, shape in (
                ("combine", [P, NT, EM + 1]), ("w1", [D, 2, EM + 1, HID]), ("b1", [P, EM + 1, HT]),
                ("w2", [P, EM + 1, HT, D]))}
            prepare1(nc, a, x, xnT, ident, order, w)
            main1(nc, a, x, xnT, ident, w)
        with nc.semaphore("stored") as stored, nc.Block() as block:
            @block.sync
            def _(eng):
                eng.dma_start(a["out"].rearrange("(t p) d -> p t d", p=P), x[:, :, :]).then_inc(stored, 16)
                eng.wait_ge(stored, 16)


def layout(i):
    f = np.float32
    get = {k: np.asarray(v) for k, v in i.items()}
    wq, bq = get["L0_attn_Wq"], get["L0_attn_bq"]
    wkv, bkv = get["L0_attn_Wkv"], get["L0_attn_bkv"]
    rows = SPLIT * HD
    wqs, bqs = np.zeros((H0 // 2, D, P), f), np.zeros((P, H0 // 2), f)
    wks, bks = np.zeros((D, 2, P), f), np.zeros((P, 2), f)
    for g in range(SPLIT):
        for hh in range(2):
            at = slice(hh * rows + g * HD, hh * rows + (g + 1) * HD)
            wks[:, hh, at] = wkv[:HD].T
            bks[at, hh] = bkv[:HD]
            for pair in range(H0 // 2):
                h = slice((2 * pair + hh) * HD, (2 * pair + hh + 1) * HD)
                wqs[pair][:, at] = wq[h].T
                bqs[at, pair] = bq[h]
    for hh in range(2):
        bks[96 + 3 * hh:99 + 3 * hh, hh] = 1
    split = np.zeros((P, 4), f)
    for col, classes in ((0, (0, 0, 0, 1, 1, 2)), (2, (0, 1, 2, 0, 1, 0))):
        for hh in range(2):
            for g, c in enumerate(classes):
                at = slice(hh * rows + g * HD, hh * rows + (g + 1) * HD)
                split[at, col], split[at, col + 1] = -(c >= 1), -(c == 2)
    proj, half, vmask = np.zeros((P, HF * JF), f), np.zeros((P, HF), f), np.zeros((P, 18), f)
    for h in range(HF):
        proj[h * HD:(h + 1) * HD, h * JF:(h + 1) * JF] = get["L1_attn_proj"][h].T
        half[h * HD:(h + 1) * HD, h] = 0.5
    for hh in range(2):
        vmask[hh * JF:(hh + 1) * JF, hh * HD:(hh + 1) * HD] = 1
        vmask[hh * JF:(hh + 1) * JF, 16 + hh] = 1
    selv = np.concatenate([get["L0_ffn_sel_v_w"].T, get["L0_ffn_sel_o_w"].T, wkv[HD:].T,
                           np.zeros((D, 32 - HD), f)], axis=1)
    bv = np.concatenate([bkv[HD:], np.ones(1, f), np.zeros(32 - HD - 1, f)])
    return {
        "x": get["L0_attn_x"].reshape(B * T, D),
        "q_w": get["L0_ffn_q_w"], "k_w": get["L0_ffn_k_w"],
        "v_w": get["L0_ffn_v_w"], "o_w": get["L0_ffn_o_w"],
        "selv": selv, "wk": wks, "bk": bks, "bv": bv, "wq": wqs, "split": split,
        "route": get["L0_ffn_route_scale"], "order": np.arange(8, 0, -1).astype(f),
        "wo": get["L0_attn_Wo"].T, "bo": get["L0_attn_bo"],
        "bq": bqs,
        "gate_w": get["L1_ffn_gate_w"], "gate_b": get["L1_ffn_gate_b"],
        "wqT": get["L1_attn_Wq"].T, "wkT": get["L1_attn_Wk"].T, "wvT": get["L1_attn_Wv"].T,
        "woT": get["L1_attn_Wo"].T, "bqk": np.stack([get["L1_attn_bq"], get["L1_attn_bk"]], axis=1),
        "bv1": get["L1_attn_bv"], "bo1": get["L1_attn_bo"], "proj": proj, "half": half, "vmask": vmask,
        "w1": get["L1_ffn_w1"], "ws1": get["L1_ffn_ws1"],
        "w2": np.concatenate([get["L1_ffn_w2"], get["L1_ffn_ws2"][None]]),
        "b1": np.concatenate([get["L1_ffn_b1"], get["L1_ffn_bs1"][None]]),
        "b2": np.concatenate([get["L1_ffn_b2"], get["L1_ffn_bs2"][None]]),
    }


def kernel(**inputs):
    import concourse.bacc as _bacc
    from concourse.bass_utils import run_bass_kernel_spmd as _run

    nc = _bacc.Bacc("TRN2", target_bir_lowering=False, num_devices=1)
    arrays = {f"in_{k}": np.ascontiguousarray(v) for k, v in layout(inputs).items()}
    a = {k[3:]: nc.dram_tensor(k, v.shape, mybir.dt.from_np(v.dtype), kind="ExternalInput").ap()
         for k, v in arrays.items()}
    a["out"] = nc.dram_tensor("out", (B * T, D), F32, kind="ExternalOutput").ap()
    build(nc, a)
    return _run(nc, [arrays], core_ids=[0]).results[0]["out"].reshape(B, T, D)
```
